# Optimizing a Trainium2 kernel written in Bass

```python
import numpy as np
import jax
import jax.numpy as jnp

def _softmax(x, axis=-1):
    return jax.nn.softmax(x, axis=axis)

def _gelu(x):
    return jax.nn.gelu(x, approximate=True)

def _silu(x):
    return jax.nn.silu(x)

def _sigmoid(x):
    return jax.nn.sigmoid(x)

def _layernorm(x, axis=-1, eps=1e-05):
    m = jnp.mean(x, axis=axis, keepdims=True)
    v = jnp.var(x, axis=axis, keepdims=True)
    return (x - m) / jnp.sqrt(v + eps)

def _scatter_add(tgt, idx, src, axis=0):
    return tgt.at[idx].add(src)

def _segment_sum(src, seg, n):
    return jax.ops.segment_sum(src, seg, n)
kernel_name = 'mk_adaln_d1_jaxref_r4_5dfbbd'

def setup_inputs(seed: int=0):
    np.random.seed(seed)
    _w = jnp.asarray

    def _L0_attn_setup():
        import jax, jax.numpy as jnp
        import numpy as np
        D_MODEL = 512
        NUM_HEADS = 16
        D_K = D_MODEL // NUM_HEADS

        def _heads(t, B, S):
            return t.reshape(B, S, NUM_HEADS, D_K).transpose(0, 2, 1, 3)
        key = jax.random.key(seed)
        ks = jax.random.split(key, 9)
        s = 1.0 / np.sqrt(D_MODEL)
        x = jax.random.normal(ks[0], (4, 1024, D_MODEL), dtype=jnp.float32)
        wq = jax.random.uniform(ks[1], (D_MODEL, D_MODEL), jnp.float32, -s, s)
        bq = jax.random.uniform(ks[2], (D_MODEL,), jnp.float32, -s, s)
        wk = jax.random.uniform(ks[3], (D_MODEL, D_MODEL), jnp.float32, -s, s)
        bk = jax.random.uniform(ks[4], (D_MODEL,), jnp.float32, -s, s)
        wv = jax.random.uniform(ks[5], (D_MODEL, D_MODEL), jnp.float32, -s, s)
        bv = jax.random.uniform(ks[6], (D_MODEL,), jnp.float32, -s, s)
        wo = jax.random.uniform(ks[7], (D_MODEL, D_MODEL), jnp.float32, -s, s)
        bo = jax.random.uniform(ks[8], (D_MODEL,), jnp.float32, -s, s)
        return {'x': x, 'wq': wq, 'bq': bq, 'wk': wk, 'bk': bk, 'wv': wv, 'bv': bv, 'wo': wo, 'bo': bo}
    _L0_attn_in = _L0_attn_setup()

    def _L0_ffn_setup():
        import jax, jax.numpy as jnp
        import numpy as np
        _FP4_LUT = jnp.array([0.0, 0.5, 1.0, 1.5, 2.0, 3.0, 4.0, 6.0, -0.0, -0.5, -1.0, -1.5, -2.0, -3.0, -4.0, -6.0], dtype=jnp.float32)
        GROUP_SIZE = 128
        EPS = 1e-06

        def _dequant_fp4(packed_i32, scales_f16, group_size):
            out_f, in_p = packed_i32.shape
            w = packed_i32.astype(jnp.uint32)
            shifts = jnp.arange(8, dtype=jnp.uint32) * 4
            nib = w[:, :, None] >> shifts & jnp.uint32(15)
            vals = _FP4_LUT[nib.astype(jnp.int32)].reshape(out_f, in_p * 8)
            s = scales_f16.astype(jnp.float32).T
            s_full = jnp.repeat(s, group_size, axis=1)
            return vals * s_full
        key = jax.random.key(seed)
        k1, k2, k3, k4, k5 = jax.random.split(key, 5)
        B, S, H, I = (4, 512, 512, 1408)
        x = jax.random.normal(k1, (B, S, H), dtype=jnp.float32)
        gate_up_packed = jax.random.randint(k2, (2 * I, H // 8), 0, 2147483647, dtype=jnp.int32)
        gate_up_scales = jax.random.uniform(k3, (H // GROUP_SIZE, 2 * I), dtype=jnp.float32).astype(jnp.float16)
        down_packed = jax.random.randint(k4, (H, I // 8), 0, 2147483647, dtype=jnp.int32)
        down_scales = jax.random.uniform(k5, (I // GROUP_SIZE, H), dtype=jnp.float32).astype(jnp.float16)
        return {'x': x, 'gate_up_packed': gate_up_packed, 'gate_up_scales': gate_up_scales, 'down_packed': down_packed, 'down_scales': down_scales}
    _L0_ffn_in = _L0_ffn_setup()
    _L0_c = _w((lambda *s: np.random.randn(*s).astype(np.float32) * 0.05)(4, 512))
    _L0_wmod = _w((lambda *s: np.random.randn(*s).astype(np.float32) * 0.05)(512, 6 * 512) * 512 ** (-0.5))
    _d = {'L0_attn_x': _L0_attn_in['x'], 'L0_attn_wq': _L0_attn_in['wq'], 'L0_attn_bq': _L0_attn_in['bq'], 'L0_attn_wk': _L0_attn_in['wk'], 'L0_attn_bk': _L0_attn_in['bk'], 'L0_attn_wv': _L0_attn_in['wv'], 'L0_attn_bv': _L0_attn_in['bv'], 'L0_attn_wo': _L0_attn_in['wo'], 'L0_attn_bo': _L0_attn_in['bo'], 'L0_ffn_gate_up_packed': _L0_ffn_in['gate_up_packed'], 'L0_ffn_gate_up_scales': _L0_ffn_in['gate_up_scales'], 'L0_ffn_down_packed': _L0_ffn_in['down_packed'], 'L0_ffn_down_scales': _L0_ffn_in['down_scales'], 'L0_c': _L0_c, 'L0_wmod': _L0_wmod}
    _x0 = _d['L0_attn_x']
    _d['L0_attn_x'] = jax.random.normal(jax.random.fold_in(jax.random.key(seed), 1), (4, 1024, 512), dtype=_x0.dtype)
    del _x0
    return _d

def reference(L0_attn_x, L0_attn_wq, L0_attn_bq, L0_attn_wk, L0_attn_bk, L0_attn_wv, L0_attn_bv, L0_attn_wo, L0_attn_bo, L0_ffn_gate_up_packed, L0_ffn_gate_up_scales, L0_ffn_down_packed, L0_ffn_down_scales, L0_c, L0_wmod):

    def _L0_attn_ref(x, wq, bq, wk, bk, wv, bv, wo, bo):
        import jax, jax.numpy as jnp
        import numpy as np
        D_MODEL = 512
        NUM_HEADS = 16
        D_K = D_MODEL // NUM_HEADS

        def _heads(t, B, S):
            return t.reshape(B, S, NUM_HEADS, D_K).transpose(0, 2, 1, 3)
        B, S, _ = x.shape
        Q = _heads(x @ wq.T + bq, B, S)
        K = _heads(x @ wk.T + bk, B, S)
        V = _heads(x @ wv.T + bv, B, S)
        Q = jax.nn.elu(Q) + 1.0
        K = jax.nn.elu(K) + 1.0
        KV = jnp.einsum('bhsd,bhse->bhde', K, V)
        QKV = jnp.einsum('bhsd,bhde->bhse', Q, KV)
        K_sum = jnp.sum(K, axis=-2)
        QK_sum = jnp.einsum('bhsd,bhd->bhs', Q, K_sum)
        out = QKV / (QK_sum[..., None] + 1e-08)
        out = out.transpose(0, 2, 1, 3).reshape(B, S, D_MODEL)
        return out @ wo.T + bo

    def _L0_ffn_ref(x, gate_up_packed, gate_up_scales, down_packed, down_scales):
        import jax, jax.numpy as jnp
        import numpy as np
        _FP4_LUT = jnp.array([0.0, 0.5, 1.0, 1.5, 2.0, 3.0, 4.0, 6.0, -0.0, -0.5, -1.0, -1.5, -2.0, -3.0, -4.0, -6.0], dtype=jnp.float32)
        GROUP_SIZE = 128
        EPS = 1e-06

        def _dequant_fp4(packed_i32, scales_f16, group_size):
            out_f, in_p = packed_i32.shape
            w = packed_i32.astype(jnp.uint32)
            shifts = jnp.arange(8, dtype=jnp.uint32) * 4
            nib = w[:, :, None] >> shifts & jnp.uint32(15)
            vals = _FP4_LUT[nib.astype(jnp.int32)].reshape(out_f, in_p * 8)
            s = scales_f16.astype(jnp.float32).T
            s_full = jnp.repeat(s, group_size, axis=1)
            return vals * s_full
        I = gate_up_packed.shape[0] // 2
        w_gu = _dequant_fp4(gate_up_packed, gate_up_scales, GROUP_SIZE)
        w_down = _dequant_fp4(down_packed, down_scales, GROUP_SIZE)
        gate_up = jnp.einsum('bsh,oh->bso', x, w_gu)
        gate, up = (gate_up[..., :I], gate_up[..., I:])
        h = jax.nn.silu(gate) * up
        y = jnp.einsum('bsi,hi->bsh', h, w_down)
        rms = jnp.sqrt(jnp.mean(y * y, axis=-1, keepdims=True) + EPS)
        return y / rms
    x = L0_attn_x
    mod = (_silu(L0_c) @ L0_wmod).reshape(L0_c.shape[0], 6, 1, -1)
    sa, ca, ga, sb, cb, gb = (mod[:, 0], mod[:, 1], mod[:, 2], mod[:, 3], mod[:, 4], mod[:, 5])
    ga = (2 * (ga >= 0) - 1) * jnp.maximum(jnp.abs(ga), 0.25)
    gb = (2 * (gb >= 0) - 1) * jnp.maximum(jnp.abs(gb), 0.25)
    h = _layernorm(x, axis=-1) * (1 + ca) + sa
    x = x + ga * _L0_attn_ref(h, L0_attn_wq, L0_attn_bq, L0_attn_wk, L0_attn_bk, L0_attn_wv, L0_attn_bv, L0_attn_wo, L0_attn_bo)
    h = _layernorm(x, axis=-1) * (1 + cb) + sb
    x = x + gb * _L0_ffn_ref(h, L0_ffn_gate_up_packed, L0_ffn_gate_up_scales, L0_ffn_down_packed, L0_ffn_down_scales)
    return x

_drawn_inputs = setup_inputs


def setup_inputs(seed=0):
    import zlib

    import numpy as np

    out = dict(_drawn_inputs(seed))
    spreads = {}
    factors = {'L0_attn_wq': 8.0,
     'L0_attn_bq': 64.0,
     'L0_attn_wk': 8.0,
     'L0_attn_bk': 190.691,
     'L0_attn_wv': 8.0,
     'L0_attn_bv': 8.0,
     'L0_attn_wo': 8.0,
     'L0_attn_bo': 8.0}
    for name, (base, spread) in spreads.items():
        noise = np.random.default_rng([zlib.crc32(name.encode()), seed]).standard_normal(out[name].shape)
        drawn = base * np.exp(spread * noise) if base else spread * noise
        out[name] = jnp.asarray(drawn.astype(out[name].dtype))
    for name, factor in factors.items():
        out[name] = (out[name] * factor).astype(out[name].dtype)
    return out
```

```python
from contextlib import ExitStack

import concourse.bass as bass
from concourse import mybir

F32 = mybir.dt.float32
F32R = mybir.dt.float32r
F16 = mybir.dt.float16
I32 = mybir.dt.int32
ALU = mybir.AluOpType
ACT = mybir.ActivationFunctionType

P = 128
BATCH = 4
SEQ = 1024
D = 512
HEADS = 16
DK = D // HEADS
KC = D // P
TOK = 512
TT = TOK // P
JB = SEQ // TOK
INNER = 1408
FC = INNER // P
NIB = 8
WPG = P // NIB
XW = D + 2
LN_EPS = 1e-5
RMS_EPS = 1e-6
DEN_EPS = 1e-8
C_ID, C_MASK, C_HEAD, C_SEL, C_END = 0, P, 2 * P, 2 * P + KC * HEADS, 2 * P + KC * HEADS + D
LO_ROW = 32


def wait(eng, sem, value):
    if isinstance(value, int) and value <= 0:
        return
    eng.wait_ge(sem, value)


class Steps:

    def __init__(self, eng, sem, per_round):
        self.eng, self.sem, self.per_round = eng, sem, per_round

    def start(self, rnd):
        self.base, self.n = rnd * self.per_round, 0

    def mark(self, ins):
        ins.then_inc(self.sem, 1)
        self.n += 1
        return self.base + self.n

    def link(self, ins):
        self.eng.wait_ge(self.sem, self.mark(ins))

    def end(self):
        assert self.n == self.per_round, self.n


def inverse_sqrt(nc, steps, out, work, src, scale, eps):
    v, a, h = work
    steps.link(nc.vector.tensor_scalar(v, src, scale, eps, ALU.mult, ALU.add))
    steps.link(nc.vector.tensor_scalar(a.bitcast(I32), v.bitcast(I32), 1, None, ALU.arith_shift_right))
    steps.link(nc.vector.tensor_scalar(out.bitcast(I32), a.bitcast(I32), -1.0, float(0x5F3759DF), ALU.mult, ALU.add))
    steps.link(nc.vector.tensor_scalar(h, v, -0.5, None, ALU.mult))
    for _ in range(3):
        steps.link(nc.vector.tensor_tensor(a, out, out, ALU.mult))
        steps.link(nc.vector.tensor_tensor(a, a, h, ALU.mult))
        steps.link(nc.vector.scalar_tensor_tensor(out, a, 1.5, out, ALU.add, ALU.mult))


def split_matmul(nc, out, parts, start_first, stop_last):
    for i, (stationary, moving) in enumerate(parts):
        last = nc.tensor.matmul(out, stationary, moving, start=start_first and i == 0,
                                stop=stop_last and i == len(parts) - 1)
    return last


def adaln_block(nc, x, wq_t, wk_t, wv_t, wo_t, bq, bk, bv, bo, gu_down_words, gu_scales, down_scales,
                c_t, wmod, consts, shifts, out):
    mod_cols_dram = nc.dram_tensor("mod_cols", (BATCH, P, 4 * KC), F32).ap()
    gate_rows_dram = nc.dram_tensor("gate_rows", (BATCH, 2, D), F32).ap()
    x2_dram = nc.dram_tensor("x_after_attention", (BATCH * JB, P, TT * XW), F32).ap()
    x_blocks = x.rearrange("(n p t) d -> n p (t d)", p=P, t=TT)
    out_blocks = out.rearrange("(n p t) d -> n p (t d)", p=P, t=TT)

    with ExitStack() as whole:
        const_sb = whole.enter_context(nc.sbuf_tensor("const_sb", [P, C_END], F32))
        with ExitStack() as attention_memory:
            def sb(name, shape, dt=F32):
                return attention_memory.enter_context(nc.sbuf_tensor(name, shape, dt))

            weights = {
                "wq": (sb("wq_hi", [P, KC, D], F32R), sb("wq_lo", [P, KC, D], F32R)),
                "wk": (sb("wk_hi", [P, KC, D], F32R), sb("wk_lo", [P, KC, D], F32R)),
                "wv": (sb("wv_hi", [P, KC, D], F32R), sb("wv_lo", [P, KC, D], F32R)),
                "wo": sb("wo_sb", [P, KC, D]),
                "bq": sb("bq_sb", [P, KC]),
                "bq_neg": sb("bq_neg", [P, KC]),
                "bk": sb("bk_rows", [LO_ROW + 1, D], F32R),
                "ones": sb("ones_rows", [LO_ROW + 1, P], F32R),
                "bv": sb("bv_all", [P, D]),
                "bo": sb("bo_all", [P, D]),
                "sel": sb("head_rows", [LO_ROW + HEADS, D], F32R),
            }
            setup(nc, weights, const_sb, wq_t, wk_t, wv_t, wo_t, bq, bk, bv, bo, c_t, wmod, consts,
                  mod_cols_dram, gate_rows_dram)
            attention(nc, weights, const_sb, x_blocks, x2_dram, mod_cols_dram, gate_rows_dram)
        mlp(nc, const_sb, gu_down_words, gu_scales, down_scales, shifts, x2_dram, mod_cols_dram,
            gate_rows_dram, out_blocks)


def setup(nc, weights, const_sb, wq_t, wk_t, wv_t, wo_t, bq, bk, bv, bo, c_t, wmod, consts,
          mod_cols_dram, gate_rows_dram):
    with ExitStack() as ctx:
        def sb(name, shape, dt=F32):
            return ctx.enter_context(nc.sbuf_tensor(name, shape, dt))

        def sem(name):
            return ctx.enter_context(nc.semaphore(name))

        raw = [sb(f"{n}_raw", [P, KC, D]) for n in ("wq", "wk", "wv")]
        wmod_sb = sb("wmod_sb", [P, KC, 6 * D])
        c_sb = sb("c_sb", [P, KC, BATCH])
        silu_c = sb("silu_c", [P, KC, BATCH])
        mod_cols = sb("mod_cols_sb", [P, BATCH, 4 * KC])
        rows_raw = sb("rows_raw", [BATCH, 2 * D])
        rows_abs = sb("rows_abs", [BATCH, 2 * D])
        rows_sign = sb("rows_sign", [BATCH, 2 * D])
        gate_rows = sb("gate_rows_sb", [BATCH, 2 * D])
        bk_raw = sb("bk_raw", [1, D])
        cols_psum = ctx.enter_context(nc.psum_tensor("cols_psum", [P, 512], F32))
        rows_psum = [ctx.enter_context(nc.psum_tensor(f"rows_psum{i}", [P, 512], F32)) for i in range(2)]

        c_loaded, wmod_loaded, small_loaded, late_loaded = (
            sem("c_loaded"), sem("wmod_loaded"), sem("small_loaded"), sem("late_loaded"))
        raw_loaded = [sem(f"raw_loaded{i}") for i in range(3)]
        silu_done, mod_done, hi_done, mod_saved = sem("silu_done"), sem("mod_done"), sem("hi_done"), sem("mod_saved")
        cols_ready, rows_ready, zeroed, steps_sem = sem("cols_ready"), sem("rows_ready"), sem("zeroed"), sem("setup_steps")
        col_sections = [0, 1, 3, 4]
        row_sections = [2, 5]

        with nc.Block() as block:
            @block.sync
            def _(sp):
                sp.dma_start(c_sb[:], c_t).then_inc(c_loaded, 16)
                for k in range(KC):
                    sp.dma_start(wmod_sb[:, k, :], wmod[k * P:(k + 1) * P, :]).then_inc(wmod_loaded, 16)
                sp.wait_ge(cols_ready, 4)
                for b in range(BATCH):
                    sp.dma_start(mod_cols_dram[b], mod_cols[:, b, :]).then_inc(mod_saved, 16)
                sp.wait_ge(rows_ready, 1)
                sp.dma_start(gate_rows_dram.rearrange("b two d -> b (two d)"), gate_rows[:]).then_inc(mod_saved, 16)
                sp.wait_ge(mod_saved, 16 * (BATCH + 1))
                sp.wait_ge(late_loaded, 64)

            @block.scalar
            def _(act):
                act.dma_start(const_sb[:], consts).then_inc(small_loaded, 16)
                act.dma_start(bk_raw[:], bk).then_inc(small_loaded, 16)
                for i, w in enumerate((wk_t, wv_t, wq_t)):
                    act.dma_start(raw[i][:], w.rearrange("(k p) n -> p k n", p=P)).then_inc(raw_loaded[i], 16)
                act.dma_start(weights["wo"][:], wo_t.rearrange("(k p) n -> p k n", p=P)).then_inc(late_loaded, 16)
                act.dma_start(weights["bq"][:], bq).then_inc(late_loaded, 16)
                act.dma_start(weights["bv"][:], bv.partition_broadcast(P)).then_inc(late_loaded, 16)
                act.dma_start(weights["bo"][:], bo.partition_broadcast(P)).then_inc(late_loaded, 16)
                act.wait_ge(c_loaded, 16)
                nc.scalar.activation(silu_c[:], c_sb[:], ACT.Silu).then_inc(silu_done, 1)
                act.wait_ge(small_loaded, 32)
                act.wait_ge(zeroed, 1)
                nc.scalar.activation(weights["bk"][0:1, :], bk_raw[:], ACT.Copy).then_inc(hi_done, 1)
                nc.scalar.activation(weights["sel"][:], const_sb[0:LO_ROW + HEADS, C_SEL:C_END], ACT.Copy).then_inc(hi_done, 1)
                for r in (0, LO_ROW):
                    nc.scalar.activation(weights["ones"][r:r + 1, :], const_sb[r:r + 1, C_ID:C_ID + P],
                                         ACT.Identity, bias=const_sb[r:r + 1, C_MASK + r:C_MASK + r + 1],
                                         scale=0.0).then_inc(hi_done, 1)
                act.wait_ge(late_loaded, 64)
                nc.scalar.activation(weights["bq_neg"][:], weights["bq"][:], ACT.Copy, scale=-1.0)
                for i, name in enumerate(("wk", "wv", "wq")):
                    act.wait_ge(raw_loaded[i], 16)
                    nc.scalar.activation(weights[name][0][:], raw[i][:], ACT.Copy).then_inc(hi_done, 1)

            @block.tensor
            def _(pe):
                pe.wait_ge(silu_done, 1)
                pe.wait_ge(wmod_loaded, 16 * KC)
                for s, section in enumerate(col_sections):
                    for j in range(KC):
                        at = (s * KC + j) * BATCH
                        for k in range(KC):
                            f0 = section * D + j * P
                            last = nc.tensor.matmul(cols_psum[:, at:at + BATCH], wmod_sb[:, k, f0:f0 + P],
                                                    silu_c[:, k, :], start=(k == 0), stop=(k == KC - 1))
                last.then_inc(mod_done, 1)
                for i, section in enumerate(row_sections):
                    for k in range(KC):
                        last = nc.tensor.matmul(rows_psum[i][0:BATCH, :], silu_c[:, k, :],
                                                wmod_sb[:, k, section * D:(section + 1) * D],
                                                start=(k == 0), stop=(k == KC - 1))
                    last.then_inc(mod_done, 1)

            @block.vector
            def _(dve):
                steps = Steps(dve, steps_sem, 7)
                steps.start(0)
                steps.link(nc.vector.memset(weights["bk"][:].bitcast(F32), 0.0))
                nc.vector.memset(weights["ones"][:].bitcast(F32), 0.0).then_inc(zeroed, 1)
                dve.wait_ge(mod_done, 1)
                for s in range(4):
                    src = cols_psum[:, s * KC * BATCH:(s + 1) * KC * BATCH].rearrange("p (j b) -> p b j", b=BATCH)
                    nc.vector.tensor_scalar(mod_cols[:, :, s * KC:(s + 1) * KC], src, float(s % 2), None,
                                            ALU.add).then_inc(cols_ready, 1)
                dve.wait_ge(mod_done, 3)
                for i in range(2):
                    s = slice(i * D, (i + 1) * D)
                    steps.link(nc.vector.tensor_copy(rows_raw[:, s], rows_psum[i][0:BATCH, :]))
                steps.link(nc.vector.scalar_tensor_tensor(rows_abs[:], rows_raw[:], -1.0, rows_raw[:], ALU.mult, ALU.max))
                steps.link(nc.vector.tensor_scalar(rows_abs[:], rows_abs[:], 0.25, None, ALU.max))
                steps.link(nc.vector.tensor_scalar(rows_sign[:], rows_raw[:], 0.0, 2.0, ALU.is_ge, ALU.mult))
                nc.vector.scalar_tensor_tensor(gate_rows[:], rows_sign[:], -1.0, rows_abs[:], ALU.add,
                                               ALU.mult).then_inc(rows_ready, 1)
                dve.wait_ge(hi_done, 1)
                steps.link(nc.vector.tensor_tensor(weights["bk"][LO_ROW:LO_ROW + 1, :], bk_raw[:],
                                                   weights["bk"][0:1, :].bitcast(F32), ALU.subtract))
                for i, name in enumerate(("wk", "wv", "wq")):
                    dve.wait_ge(hi_done, 5 + i)
                    nc.vector.tensor_tensor(weights[name][1][:], raw[i][:], weights[name][0][:].bitcast(F32),
                                            ALU.subtract)
                steps.end()


def attention(nc, weights, const_sb, x_blocks, x2_dram, mod_cols_dram, gate_rows_dram):
    wq, wk, wv = weights["wq"], weights["wk"], weights["wv"]
    ident = const_sb[:, C_ID:C_ID + P]
    mask = const_sb[:, C_MASK:C_MASK + P]
    head_mask = const_sb[:, C_HEAD:C_SEL].rearrange("p (k h) -> p k h", h=HEADS)
    VW = P + 1

    with ExitStack() as ctx:
        def sb(name, shape, dt=F32):
            return ctx.enter_context(nc.sbuf_tensor(name, shape, dt))

        def bank(name):
            return ctx.enter_context(nc.psum_tensor(name, [P, 512], F32))

        def sem(name):
            return ctx.enter_context(nc.semaphore(name))

        x_in = [sb(f"x_in{j}", [P, TT, D]) for j in range(JB)]
        stats = sb("stats", [P, TT, 6])
        moments = sb("moments", [P, 3, TT])
        work = [sb(f"rsqrt_work{i}", [P, TT])[:] for i in range(3)]
        rstd = sb("rstd", [P, TT])
        shift = sb("shift", [P, TT])
        mod_now = sb("mod_now", [P, 4 * KC])
        h_full = [sb(f"h_full{i}", [P, TOK]) for i in range(2)]
        h_hi, h_lo = sb("h_hi", [P, KC, TOK], F32R), sb("h_lo", [P, KC, TOK], F32R)
        k_exp = [sb(f"k_exp{i}", [P, D]) for i in range(2)]
        k_sb = [sb(f"k_sb{i}", [P, D]) for i in range(2)]
        v_sb = [sb(f"v_sb{i}", [P, KC, VW]) for i in range(2)]
        q_exp = [sb(f"q_exp{i}", [P, TOK]) for i in range(2)]
        q_sb = [sb(f"q_sb{j}", [P, KC, TOK]) for j in range(JB)]
        credit = sb("credit", [P, 4])
        k_sum = sb("k_sum", [P, KC])
        k_sum_heads = sb("k_sum_heads", [P, KC, HEADS])
        kv_sb = sb("kv_sb", [P, KC, P])
        kv_t = sb("kv_t", [P, D])
        m_full = [sb(f"m_full{i}", [P, D]) for i in range(2)]
        m_hi, m_lo = sb("m_hi", [P, KC, D], F32R), sb("m_lo", [P, KC, D], F32R)
        ga_all = sb("ga_all", [P, D])
        ga_bo = sb("ga_bo", [P, D])
        recip = sb("recip", [HEADS, TOK])
        recip_rows = sb("recip_rows", [LO_ROW + HEADS, TOK], F32R)
        qn_full = [sb(f"qn_full{i}", [P, TOK]) for i in range(2)]
        qn_hi, qn_lo = sb("qn_hi", [P, KC, TOK], F32R), sb("qn_lo", [P, KC, TOK], F32R)
        x2 = [sb(f"x2_{j}", [P, TT, XW]) for j in range(JB)]

        turn = [bank(f"turn{i}") for i in range(2)]
        prod = [bank(f"prod{i}") for i in range(2)]
        kv_psum = [bank(f"kv_psum{i}") for i in range(2)]
        den = bank("den")
        spread = bank("spread")

        x_loaded = [sem(f"x_loaded{j}") for j in range(JB)]
        mod_loaded = sem("mod_loaded")
        ga_loaded = sem("ga_loaded")
        x2_loaded = [sem(f"x2_loaded{j}") for j in range(JB)]
        x2_stored = [sem(f"x2_stored{j}") for j in range(JB)]
        norm_ready, xn_ready, turned, h_full_ready, h_ready = (
            sem("norm_ready"), sem("xn_ready"), sem("turned"), sem("h_full_ready"), sem("h_ready"))
        k_product, v_product, q_product, m_product, o_product = (
            sem("k_product"), sem("v_product"), sem("q_product"), sem("m_product"), sem("o_product"))
        k_exp_ready, k_ready, v_ready, q_exp_ready, q_ready = (
            sem("k_exp_ready"), sem("k_ready"), sem("v_ready"), sem("q_exp_ready"), sem("q_ready"))
        k_relu_ready, q_relu_ready = sem("k_relu_ready"), sem("q_relu_ready")
        kv_tile, heads_ready, kv_ready, kv_turned, kv_t_ready = (
            sem("kv_tile"), sem("heads_ready"), sem("kv_ready"), sem("kv_turned"), sem("kv_t_ready"))
        m_read, m_ready = sem("m_read"), sem("m_ready")
        den_product, recip_ready, spread_ready, spread_read, qn_ready = (
            sem("den_product"), sem("recip_ready"), sem("spread_ready"), sem("spread_read"), sem("qn_ready"))
        ga_bo_ready, x2_biased, o_read, x2_ready = sem("ga_bo_ready"), sem("x2_biased"), sem("o_read"), sem("x2_ready")
        ones_set, zero_set = sem("ones_set"), sem("zero_set")
        in_steps, out_steps = sem("in_steps"), sem("out_steps")

        NT = JB * TT
        NC = JB * KC

        def rounds(eng, emit):
            emit(0, None)
            with eng.Fori(1, BATCH) as b:
                emit(b, b - 1)
            emit(None, BATCH - 1)

        with nc.Block() as block:
            @block.sync
            def _(sp):
                sp.wait_ge(zero_set, 1)

                def emit(b, e):
                    if e is not None:
                        sp.wait_ge(q_ready, (e + 1) * NC)
                        sp.wait_ge(ga_bo_ready, e + 1)
                        sp.dma_start(ga_all[:], gate_rows_dram[bass.ds(e, 1), 0, :].squeeze(0).partition_broadcast(P)
                                     ).then_inc(ga_loaded, 16)
                    if b is not None:
                        wait(sp, h_full_ready, b * NC)
                        sp.dma_start(mod_now[:], mod_cols_dram[bass.ds(b, 1)].squeeze(0)).then_inc(mod_loaded, 16)
                    for j in range(JB):
                        if b is not None:
                            wait(sp, turned, (b - 1) * NC + (j + 1) * KC)
                            sp.dma_start(x_in[j][:].rearrange("p t d -> p (t d)"),
                                         x_blocks[bass.ds(b * JB + j, 1)].squeeze(0)).then_inc(x_loaded[j], 16)
                        if e is not None:
                            sp.wait_ge(x2_stored[j], 16 * (e + 1))
                            sp.dma_start(x2[j][:, :, 0:D], x_blocks[bass.ds(e * JB + j, 1)].squeeze(0)
                                         .rearrange("p (t d) -> p t d", t=TT)).then_inc(x2_loaded[j], 16)

                rounds(sp, emit)
                for j in range(JB):
                    sp.wait_ge(x2_stored[j], 16 * (BATCH + 1))

            @block.gpsimd
            def _(pool):
                for j in range(JB):
                    nc.gpsimd.memset(credit[:, j:j + 1], 0.0).then_inc(x2_stored[j], 16)
                nc.gpsimd.memset(credit[:, 2:3], 0.0).then_inc(ga_bo_ready, 1)
                nc.gpsimd.memset(credit[:, 3:4], 0.0).then_inc(x2_biased, 1)
                nc.gpsimd.memset(recip_rows[:].bitcast(F32), 0.0).then_inc(zero_set, 1)
                for i in range(2):
                    nc.gpsimd.memset(v_sb[i][:, :, P:VW], 1.0).then_inc(ones_set, 1)

                def emit(b, e):
                    if e is None:
                        return
                    pool.wait_ge(ga_loaded, 16 * (e + 1))
                    pool.wait_ge(x2_biased, JB * e + 1)
                    nc.gpsimd.tensor_tensor(ga_bo[:], ga_all[:], weights["bo"][:], ALU.mult).then_inc(ga_bo_ready, 1)
                    pool.wait_ge(ga_bo_ready, e + 2)
                    for j in range(JB):
                        pool.wait_ge(x2_loaded[j], 16 * (e + 1))
                        for t in range(TT):
                            last = nc.gpsimd.tensor_tensor(x2[j][:, t, 0:D], x2[j][:, t, 0:D], ga_bo[:], ALU.add)
                        last.then_inc(x2_biased, 1)

                rounds(pool, emit)

            @block.scalar
            def _(act):
                def normalize(b, j):
                    act.wait_ge(norm_ready, b * JB + j + 1)
                    for t in range(TT):
                        nc.scalar.activation(x_in[j][:, t, :], x_in[j][:, t, :], ACT.Identity,
                                             bias=shift[:, t:t + 1], scale=rstd[:, t:t + 1]).then_inc(xn_ready, 1)

                def store(e, j):
                    act.wait_ge(x2_ready, e * JB + j + 1)
                    act.dma_start(x2_dram[bass.ds(e * JB + j, 1)].squeeze(0),
                                  x2[j][:].rearrange("p t d -> p (t d)")).then_inc(x2_stored[j], 16)

                act.wait_ge(ones_set, 2)

                def emit(b, e):
                    if b is not None:
                        normalize(b, 0)
                        act.wait_ge(mod_loaded, 16 * (b + 1))
                    for j in range(JB):
                        if b is not None:
                            for c in range(KC):
                                n = b * NC + j * KC + c
                                act.wait_ge(turned, n + 1)
                                wait(act, h_ready, n - 1)
                                nc.scalar.activation(h_full[c % 2][:], turn[c % 2][:], ACT.Identity,
                                                     bias=mod_now[:, c:c + 1], scale=mod_now[:, KC + c:KC + c + 1]
                                                     ).then_inc(h_full_ready, 1)
                            for t in range(TT):
                                n = b * NT + j * TT + t
                                act.wait_ge(k_product, n + 1)
                                wait(act, k_ready, n - 1)
                                nc.scalar.activation(k_exp[t % 2][:], prod[0][:], ACT.Relu, scale=-1.0
                                                     ).then_inc(k_relu_ready, 1)
                                act.wait_ge(k_relu_ready, n + 1)
                                nc.scalar.activation(k_exp[t % 2][:], k_exp[t % 2][:], ACT.Exp, scale=-1.0
                                                     ).then_inc(k_exp_ready, 1)
                                act.wait_ge(v_product, n + 1)
                                wait(act, kv_tile, n - 1)
                                nc.scalar.activation(v_sb[t % 2][:, :, 0:P],
                                                     prod[1][:].rearrange("p (g n) -> p g n", g=KC),
                                                     ACT.Copy).then_inc(v_ready, 1)
                            for k in range(KC):
                                n = b * NC + j * KC + k
                                act.wait_ge(q_product, n + 1)
                                wait(act, q_ready, n - 1)
                                nc.scalar.activation(q_exp[k % 2][:], prod[k % 2][:], ACT.Relu, scale=-1.0,
                                                     bias=weights["bq_neg"][:, k:k + 1]).then_inc(q_relu_ready, 1)
                                act.wait_ge(q_relu_ready, n + 1)
                                nc.scalar.activation(q_exp[k % 2][:], q_exp[k % 2][:], ACT.Exp, scale=-1.0
                                                     ).then_inc(q_exp_ready, 1)
                            if j + 1 < JB:
                                normalize(b, j + 1)
                        if e is not None:
                            store(e, j)

                rounds(act, emit)

            @block.vector
            def _(dve):
                ins = Steps(dve, in_steps, JB * (17 + 2 * KC))
                outs = Steps(dve, out_steps, 1 + KC + KC + JB * (2 + KC + TT + 16))

                def normalization(steps, rstd_out, shift_out):
                    both, apart, spread_sq = moments[:, 0, :], moments[:, 1, :], moments[:, 2, :]
                    nc.vector.tensor_tensor(both, stats[:, :, 1], stats[:, :, 4], ALU.add)
                    nc.vector.tensor_tensor(apart, stats[:, :, 1], stats[:, :, 4], ALU.subtract)
                    steps.link(nc.vector.tensor_tensor(spread_sq, stats[:, :, 2], stats[:, :, 5], ALU.add))
                    steps.link(nc.vector.tensor_tensor(apart, apart, apart, ALU.mult))
                    steps.link(nc.vector.scalar_tensor_tensor(spread_sq, apart, D / 4, spread_sq, ALU.mult, ALU.add))
                    inverse_sqrt(nc, steps, rstd_out, work, spread_sq, 1.0 / D, LN_EPS)
                    return nc.vector.scalar_tensor_tensor(shift_out, both, -0.5, rstd_out, ALU.mult, ALU.mult)

                def norm_in(b, j):
                    dve.wait_ge(x_loaded[j], 16 * (b + 1))
                    for t in range(TT):
                        last = nc.vector.bn_stats(stats[:, t, :], x_in[j][:, t, :])
                    ins.link(last)
                    normalization(ins, rstd[:], shift[:]).then_inc(norm_ready, 1)

                def finish_kv(e):
                    dve.wait_ge(kv_tile, NT * (e + 1))
                    for i in range(2):
                        last = nc.vector.tensor_copy(
                            k_sum[:, 2 * i:2 * i + 2], kv_psum[i][:, 0:2 * VW].rearrange("p (g n) -> p g n", g=2)[:, :, P])
                    outs.link(last)
                    for k in range(KC):
                        nc.vector.tensor_scalar(k_sum_heads[:, k, :], head_mask[:, k, :], k_sum[:, k:k + 1], None,
                                                ALU.mult).then_inc(heads_ready, 1)
                    marks = []
                    for k in range(KC):
                        at = (k % 2) * VW
                        marks.append(outs.mark(nc.vector.scalar_tensor_tensor(
                            kv_sb[:, k, :], weights["bv"][:, k * P:(k + 1) * P], k_sum[:, k:k + 1],
                            kv_psum[k // 2][:, at:at + P], ALU.mult, ALU.add)))
                    for k in range(KC):
                        dve.wait_ge(out_steps, marks[k])
                        nc.vector.tensor_tensor(kv_sb[:, k, :], kv_sb[:, k, :], mask, ALU.mult).then_inc(kv_ready, 1)

                def reciprocal(e, j):
                    n = e * JB + j
                    dve.wait_ge(den_product, n + 1)
                    outs.link(nc.vector.tensor_scalar(recip[:], den[0:HEADS, :], DEN_EPS, None, ALU.add))
                    outs.link(nc.vector.reciprocal(recip[:], recip[:]))
                    nc.vector.tensor_copy(recip_rows[0:HEADS, :], recip[:]).then_inc(recip_ready, 1)
                    dve.wait_ge(recip_ready, 2 * n + 1)
                    nc.vector.tensor_tensor(recip_rows[LO_ROW:LO_ROW + HEADS, :], recip[:],
                                            recip_rows[0:HEADS, :].bitcast(F32), ALU.subtract).then_inc(recip_ready, 1)

                def split_m(e):
                    for k in range(KC):
                        dve.wait_ge(m_product, KC * e + k + 1)
                        nc.vector.tensor_tensor(m_full[k % 2][:], prod[k % 2][:], ga_all[:], ALU.mult).then_inc(m_read, 1)
                        dve.wait_ge(m_read, KC * e + k + 1)
                        outs.link(nc.vector.tensor_copy(m_hi[:, k, :], m_full[k % 2][:]))
                        nc.vector.tensor_tensor(m_lo[:, k, :], m_full[k % 2][:], m_hi[:, k, :].bitcast(F32),
                                                ALU.subtract).then_inc(m_ready, 1)

                def emit(b, e):
                    ins.start(b) if b is not None else None
                    outs.start(e) if e is not None else None
                    if b is not None:
                        norm_in(b, 0)
                    if e is not None:
                        finish_kv(e)
                        dve.wait_ge(kv_turned, e + 1)
                        nc.vector.tensor_copy(kv_t[:], turn[0][:]).then_inc(kv_t_ready, 1)
                    for j in range(JB):
                        if b is not None:
                            wait(dve, q_product, b * NC + j * KC)
                            for c in range(KC):
                                dve.wait_ge(h_full_ready, b * NC + j * KC + c + 1)
                                ins.link(nc.vector.tensor_copy(h_hi[:, c, :], h_full[c % 2][:]))
                                nc.vector.tensor_tensor(h_lo[:, c, :], h_full[c % 2][:], h_hi[:, c, :].bitcast(F32),
                                                        ALU.subtract).then_inc(h_ready, 1)
                        for t in range(TT):
                            if b is not None:
                                n = b * NT + j * TT + t
                                dve.wait_ge(k_exp_ready, n + 1)
                                wait(dve, kv_tile, n - 1)
                                nc.vector.scalar_tensor_tensor(k_sb[t % 2][:], prod[0][:], 0.0, k_exp[t % 2][:],
                                                               ALU.max, ALU.add).then_inc(k_ready, 1)
                            if e is not None and t == 0:
                                reciprocal(e, j)
                            if e is not None and t == 1 and j == 0:
                                dve.wait_ge(ga_loaded, 16 * (e + 1))
                                split_m(e)
                        for k in range(KC):
                            if e is not None:
                                n = e * NC + j * KC + k
                                dve.wait_ge(spread_ready, n + 1)
                                nc.vector.tensor_tensor(qn_full[k % 2][:], q_sb[j][:, k, :], spread[:],
                                                        ALU.mult).then_inc(spread_read, 1)
                                dve.wait_ge(spread_read, n + 1)
                                outs.link(nc.vector.tensor_copy(qn_hi[:, k, :], qn_full[k % 2][:]))
                                nc.vector.tensor_tensor(qn_lo[:, k, :], qn_full[k % 2][:],
                                                        qn_hi[:, k, :].bitcast(F32), ALU.subtract).then_inc(qn_ready, 1)
                            if b is not None:
                                n = b * NC + j * KC + k
                                dve.wait_ge(q_relu_ready, n + 1)
                                ins.link(nc.vector.tensor_scalar(q_sb[j][:, k, :], prod[k % 2][:],
                                                                 weights["bq"][:, k:k + 1], 0.0, ALU.add, ALU.max))
                                dve.wait_ge(q_exp_ready, n + 1)
                                nc.vector.tensor_tensor(q_sb[j][:, k, :], q_exp[k % 2][:], q_sb[j][:, k, :],
                                                        ALU.add).then_inc(q_ready, 1)
                        if b is not None and j + 1 < JB:
                            norm_in(b, j + 1)
                        if e is not None:
                            dve.wait_ge(x2_biased, e * JB + j + 2)
                            for t in range(TT):
                                n = e * NT + j * TT + t
                                dve.wait_ge(o_product, n + 1)
                                nc.vector.tensor_tensor(x2[j][:, t, 0:D], prod[t % 2][:], x2[j][:, t, 0:D],
                                                        ALU.add).then_inc(o_read, 1)
                                dve.wait_ge(o_read, n + 1)
                                last = outs.mark(nc.vector.bn_stats(stats[:, t, :], x2[j][:, t, 0:D]))
                            dve.wait_ge(out_steps, last)
                            rs, sh = x2[j][:, :, D], x2[j][:, :, D + 1]
                            normalization(outs, rs, sh).then_inc(x2_ready, 1)
                    ins.end() if b is not None else None
                    outs.end() if e is not None else None

                rounds(dve, emit)

            @block.tensor
            def _(pe):
                def denominators(e, j):
                    for k in range(KC):
                        last = nc.tensor.matmul(den[0:HEADS, :], k_sum_heads[:, k, :], q_sb[j][:, k, :],
                                                start=(k == 0), stop=(k == KC - 1))
                    last.then_inc(den_product, 1)

                def key_value(n, t):
                    pe.wait_ge(k_ready, n + 1)
                    pe.wait_ge(v_ready, n + 1)
                    for g in range(KC):
                        at = (g % 2) * VW
                        last = nc.tensor.matmul(kv_psum[g // 2][:, at:at + VW], k_sb[t % 2][:, g * P:(g + 1) * P],
                                                v_sb[t % 2][:, g, :], start=(t == 0 and g % 2 == 0 and first_block[0]),
                                                stop=(t == TT - 1), skip_group_check=True)
                    last.then_inc(kv_tile, 1)

                first_block = [True]

                def emit(b, e):
                    if e is not None:
                        pe.wait_ge(heads_ready, KC * (e + 1))
                        denominators(e, 0)
                        pe.wait_ge(kv_ready, KC * (e + 1))
                        for k in range(KC):
                            last = nc.tensor.transpose(turn[0][:, k * P:(k + 1) * P], kv_sb[:, k, :], ident)
                        last.then_inc(kv_turned, 1)

                    def times_wo():
                        pe.wait_ge(kv_t_ready, e + 1)
                        for k in range(KC):
                            if k >= 2:
                                pe.wait_ge(m_read, KC * e + k - 1)
                            elif b is not None and k == 0:
                                pe.wait_ge(k_ready, b * NT + 2)
                            elif b is not None:
                                pe.wait_ge(v_ready, b * NT + 2)
                            nc.tensor.matmul(prod[k % 2][:], kv_t[:, k * P:(k + 1) * P], weights["wo"][:, k, :],
                                             start=True, stop=True).then_inc(m_product, 1)

                    for j in range(JB):
                        first_block[0] = j == 0
                        if e is not None and j > 0:
                            denominators(e, j)
                        if b is not None:
                            pe.wait_ge(xn_ready, b * NT + (j + 1) * TT)
                            if e is not None and j == 0:
                                pe.wait_ge(kv_t_ready, e + 1)
                            for c in range(KC):
                                wait(pe, h_full_ready, b * NC + j * KC + c - 1)
                                for t in range(TT):
                                    last = nc.tensor.transpose(turn[c % 2][:, t * P:(t + 1) * P],
                                                               x_in[j][:, t, c * P:(c + 1) * P], ident)
                                last.then_inc(turned, 1)
                            pe.wait_ge(h_ready, b * NC + (j + 1) * KC)
                            if e is not None and j > 0:
                                pe.wait_ge(o_read, e * NT + j * TT)
                            elif j > 0:
                                pe.wait_ge(q_ready, b * NC + j * KC)
                            for t in range(TT):
                                n = b * NT + j * TT + t
                                s = slice(t * P, (t + 1) * P)
                                if t > 0:
                                    pe.wait_ge(k_ready, n)
                                if e is not None and j == 0 and t == 2:
                                    pe.wait_ge(m_read, KC * (e + 1))
                                parts = [(weights["ones"][:], weights["bk"][:])]
                                for c in range(KC):
                                    parts += [(h_hi[:, c, s], wk[0][:, c, :]), (h_hi[:, c, s], wk[1][:, c, :]),
                                              (h_lo[:, c, s], wk[0][:, c, :])]
                                split_matmul(nc, prod[0][:], parts, True, True).then_inc(k_product, 1)
                                if t > 0:
                                    pe.wait_ge(v_ready, n)
                                parts = []
                                for c in range(KC):
                                    parts += [(h_hi[:, c, s], wv[0][:, c, :]), (h_hi[:, c, s], wv[1][:, c, :]),
                                              (h_lo[:, c, s], wv[0][:, c, :])]
                                split_matmul(nc, prod[1][:], parts, True, True).then_inc(v_product, 1)
                                if t > 0:
                                    key_value(n - 1, t - 1)
                                if e is not None and j == 0 and t == 1:
                                    times_wo()
                        elif e is not None and j == 0:
                            times_wo()
                        for k in range(KC):
                            if e is not None:
                                n = e * NC + j * KC + k
                                pe.wait_ge(recip_ready, 2 * (e * JB + j + 1))
                                if k > 0:
                                    pe.wait_ge(spread_read, n)
                                nc.tensor.matmul(spread[:], weights["sel"][:, k * P:(k + 1) * P], recip_rows[:],
                                                 start=True, stop=True).then_inc(spread_ready, 1)
                            if b is not None:
                                n = b * NC + j * KC + k
                                s = slice(k * P, (k + 1) * P)
                                if k == 0:
                                    pe.wait_ge(k_ready, b * NT + (j + 1) * TT)
                                elif k == 1:
                                    pe.wait_ge(v_ready, b * NT + (j + 1) * TT)
                                else:
                                    pe.wait_ge(q_ready, n - 1)
                                parts = []
                                for c in range(KC):
                                    parts += [(wq[0][:, c, s], h_hi[:, c, :]), (wq[1][:, c, s], h_hi[:, c, :]),
                                              (wq[0][:, c, s], h_lo[:, c, :])]
                                split_matmul(nc, prod[k % 2][:], parts, True, True).then_inc(q_product, 1)
                                if k == 0:
                                    key_value(b * NT + (j + 1) * TT - 1, TT - 1)
                        if e is not None:
                            pe.wait_ge(qn_ready, e * NC + (j + 1) * KC)
                            pe.wait_ge(m_ready, KC * (e + 1))
                            if b is not None:
                                pe.wait_ge(q_ready, b * NC + (j + 1) * KC)
                            for t in range(TT):
                                n = e * NT + j * TT + t
                                s = slice(t * P, (t + 1) * P)
                                if t >= 2 or (b is None and j > 0):
                                    pe.wait_ge(o_read, n - 1)
                                parts = []
                                for k in range(KC):
                                    parts += [(qn_hi[:, k, s], m_hi[:, k, :]), (qn_hi[:, k, s], m_lo[:, k, :]),
                                              (qn_lo[:, k, s], m_hi[:, k, :])]
                                split_matmul(nc, prod[t % 2][:], parts, True, True).then_inc(o_product, 1)

                rounds(pe, emit)


def mlp(nc, const_sb, words, gu_scales, down_scales, shifts, x2_dram, mod_cols_dram, gate_rows_dram, out_blocks):
    ident = const_sb[:, C_ID:C_ID + P]
    GU = KC * 2 * P
    NB = BATCH * JB
    HALF_BITS = -1912602624
    FP4_SCALE = 16384.0

    with ExitStack() as ctx:
        def sb(name, shape, dt=F32):
            return ctx.enter_context(nc.sbuf_tensor(name, shape, dt))

        def bank(name):
            return ctx.enter_context(nc.psum_tensor(name, [P, 512], F32))

        def sem(name):
            return ctx.enter_context(nc.semaphore(name))

        gu_w = sb("gu_w", [P, FC, KC, 2, P], F32R)
        down_hi, down_lo = sb("down_hi", [P, FC, D], F32R), sb("down_lo", [P, FC, D], F32R)
        scale16 = sb("scale16", [P, 2 * FC * KC], F16)
        scale = sb("scale", [P, 2, FC, KC])
        down_scale = [sb(f"down_scale{i}", [P, D], F16) for i in range(2)]
        shift_sb = sb("shift_sb", [P, 1], I32)
        raw = [sb(f"raw{i}", [P, GU + D], I32) for i in range(2)]
        down_full = sb("down_full", [P, D])
        x_in = sb("x2_in", [P, TT, XW])
        x_res = sb("x2_res", [P, TT, XW])
        mod_now = sb("mod_now_b", [P, 4 * KC])
        gb_all = sb("gb_all", [P, D])
        xn = sb("xn", [P, TT, KC, NIB, WPG])
        h_full = [sb(f"h2_full{i}", [P, TOK]) for i in range(2)]
        h_hi = [sb(f"h2_hi{i}", [P, KC, TOK], F32R) for i in range(2)]
        h_lo = [sb(f"h2_lo{i}", [P, KC, TOK], F32R) for i in range(2)]
        acc = [[sb(f"acc{i}{u}", [P, TOK]) for u in range(2)] for i in range(2)]
        gate = [sb(f"gate{i}", [P, TOK]) for i in range(2)]
        hid_hi = [sb(f"hid_hi{i}", [P, TOK], F32R) for i in range(2)]
        hid_lo = [sb(f"hid_lo{i}", [P, TOK], F32R) for i in range(2)]
        square = sb("square", [P, D])
        sum_sq = sb("sum_sq", [P, TT])
        work = [sb(f"rms_work{i}", [P, TT])[:] for i in range(3)]
        rms = sb("rms", [P, TT])
        o_sb = sb("o_sb", [P, TT, D])

        part = [bank(f"part{i}") for i in range(4)]
        y = [bank(f"y{t}") for t in range(TT)]

        words_loaded = [sem(f"words_loaded{i}") for i in range(2)]
        scales_loaded, scale_ready, masked = sem("scales_loaded"), sem("scale_ready"), sem("masked")
        gu_ready, down_full_ready, down_hi_ready, down_ready = (
            sem("gu_ready"), sem("down_full_ready"), sem("down_hi_ready"), sem("down_ready"))
        x_loaded, mod_loaded, res_loaded, gb_loaded, out_stored = (
            sem("x2_in_loaded"), sem("mod_b_loaded"), sem("res_loaded"), sem("gb_loaded"), sem("out_stored"))
        xn_ready, turned, h_full_ready, h_hi_ready, h_ready = (
            sem("xn2_ready"), sem("turned2"), sem("h2_full_ready"), sem("h2_hi_ready"), sem("h2_ready"))
        part_done, acc_first, acc_step, silu_ready, prod_ready, hid_hi_ready, hid_ready, hid_used = (
            sem("part_done"), sem("acc_first"), sem("acc_step"), sem("silu_ready"), sem("prod_ready"),
            sem("hid_hi_ready"), sem("hid_ready"), sem("hid_used"))
        squares_ready, y_read, o_ready = sem("squares_ready"), sem("y_read"), sem("o_ready")
        prep_steps, rms_steps = sem("prep_steps"), sem("rms_steps")

        def pairs(eng, emit, finish):
            emit(0, 0, False)
            emit(1, 1, False)
            with eng.Fori(1, BATCH - 1) as m:
                emit(m * JB, 0, False)
                emit(m * JB + 1, 1, False)
            emit(NB - 2, 0, False)
            emit(NB - 1, 1, True)
            finish()

        def slot(par, f):
            return (par * FC + f) % 2

        def batch_of(n, par):
            return (n - par) // JB if isinstance(n, int) else n_batch(n, par)

        NORM_AT = 2
        TURN_AT = 6
        OUT_AT = 1

        with nc.Block() as block:
            @block.sync
            def _(sp):
                def load_in(n, batch):
                    wait(sp, xn_ready, n * TT)
                    sp.dma_start(x_in[:].rearrange("p t d -> p (t d)"),
                                 x2_dram[bass.ds(n, 1)].squeeze(0)).then_inc(x_loaded, 16)
                    wait(sp, h_full_ready, n * KC)
                    sp.dma_start(mod_now[:], mod_cols_dram[bass.ds(batch, 1)].squeeze(0)).then_inc(mod_loaded, 16)

                def load_res(n, batch):
                    wait(sp, o_ready, n * TT)
                    sp.dma_start(x_res[:].rearrange("p t d -> p (t d)"),
                                 x2_dram[bass.ds(n, 1)].squeeze(0)).then_inc(res_loaded, 16)
                    wait(sp, y_read, n * TT)
                    sp.dma_start(gb_all[:], gate_rows_dram[bass.ds(batch, 1), 1, :].squeeze(0).partition_broadcast(P)
                                 ).then_inc(gb_loaded, 16)

                def load_words(f):
                    wait(sp, gu_ready, f - 1)
                    wait(sp, down_full_ready, f - 1)
                    for s in range(NIB):
                        sp.dma_start(raw[f % 2][s * WPG:(s + 1) * WPG, :], words[f]).then_inc(words_loaded[f % 2], 16)
                    sp.dma_start(down_scale[f % 2][:], down_scales[f:f + 1, :].squeeze(0).partition_broadcast(P)
                                 ).then_inc(words_loaded[f % 2], 16)

                load_in(0, 0)
                sp.dma_start(shift_sb[:], shifts).then_inc(scales_loaded, 16)
                sp.dma_start(scale16[:], gu_scales).then_inc(scales_loaded, 16)
                for f in range(2):
                    load_words(f)

                def emit(n, par, last):
                    if isinstance(n, int) and n == 0:
                        for f in range(2, FC):
                            load_words(f)
                            if f == 3:
                                load_in(1, 0)
                        load_res(0, 0)
                        return
                    batch = n // JB if isinstance(n, int) else sp_batch[0]
                    if not last:
                        load_in(n + 1, batch + par)
                    load_res(n, batch)

                sp_batch = [None]
                emit(0, 0, False)
                emit(1, 1, False)
                with sp.Fori(1, BATCH - 1) as m:
                    sp_batch[0] = m
                    emit(m * JB, 0, False)
                    emit(m * JB + 1, 1, False)
                emit(NB - 2, 0, False)
                emit(NB - 1, 1, True)
                sp.wait_ge(out_stored, 16 * NB)

            @block.gpsimd
            def _(pool):
                def expand(f):
                    pool.wait_ge(down_hi_ready, f + 1)
                    nc.gpsimd.tensor_tensor(down_lo[:, f, :], down_full[:], down_hi[:, f, :].bitcast(F32),
                                            ALU.subtract).then_inc(down_ready, 1)

                def finish_out(n):
                    pool.wait_ge(res_loaded, 16 * (n + 1))
                    for t in range(TT):
                        pool.wait_ge(y_read, n * TT + t + 1)
                        nc.gpsimd.tensor_tensor(o_sb[:, t, :], o_sb[:, t, :], x_res[:, t, 0:D],
                                                ALU.add).then_inc(o_ready, 1)
                    pool.wait_ge(o_ready, (n + 1) * TT)
                    pool.dma_start(out_blocks[bass.ds(n, 1)].squeeze(0),
                                   o_sb[:].rearrange("p t d -> p (t d)")).then_inc(out_stored, 16)

                def emit(n, par, last):
                    first = isinstance(n, int) and n == 0
                    if first:
                        expand(0)
                        expand(1)
                    for f in range(FC):
                        if first and f + 2 < FC:
                            expand(f + 2)
                        q = n * FC + f
                        s = slot(par, f)
                        pool.wait_ge(hid_hi_ready, q + 1)
                        nc.gpsimd.tensor_tensor(hid_lo[s][:], gate[s][:], hid_hi[s][:].bitcast(F32),
                                                ALU.subtract).then_inc(hid_ready, 1)
                        if f == OUT_AT and not first:
                            finish_out(n - 1)

                pairs(pool, emit, lambda: finish_out(NB - 1))

            @block.scalar
            def _(act):
                def expand(f):
                    act.wait_ge(masked, f + 1)
                    half = raw[f % 2][:].bitcast(F16).rearrange("p (n two) -> p n two", two=2)[:, :, 1]
                    nc.scalar.activation(gu_w[:, f, :, :, :].rearrange("p g u n -> p (g u n)"), half[:, 0:GU],
                                         ACT.Copy, scale=FP4_SCALE).then_inc(gu_ready, 1)
                    act.wait_ge(down_full_ready, f + 1)
                    nc.scalar.activation(down_hi[:, f, :], down_full[:], ACT.Copy).then_inc(down_hi_ready, 1)

                def normalize(n, t):
                    if t == 0:
                        act.wait_ge(x_loaded, 16 * (n + 1))
                        wait(act, turned, n * KC)
                    nc.scalar.activation(xn[:, t].rearrange("p g s a -> p g a s"),
                                         x_in[:, t, 0:D].rearrange("p (g a s) -> p g a s", g=KC, s=NIB), ACT.Identity,
                                         bias=x_in[:, t, D + 1:D + 2], scale=x_in[:, t, D:D + 1]).then_inc(xn_ready, 1)

                def modulate(n, c):
                    act.wait_ge(turned, n * KC + c + 1)
                    act.wait_ge(mod_loaded, 16 * (n + 1))
                    wait(act, h_ready, n * KC + c - 1)
                    nc.scalar.activation(h_full[c % 2][:], part[c if first_turn[0] else 0][:], ACT.Identity,
                                         bias=mod_now[:, 2 * KC + c:2 * KC + c + 1],
                                         scale=mod_now[:, 3 * KC + c:3 * KC + c + 1]).then_inc(h_full_ready, 1)

                def squares(n):
                    act.wait_ge(hid_used, (n + 1) * FC)
                    wait(act, y_read, n * TT)
                    for t in range(TT):
                        nc.scalar.activation(square[:], y[t][:], ACT.Square,
                                             accum_out=sum_sq[:, t:t + 1]).then_inc(squares_ready, 1)
                        act.wait_ge(squares_ready, n * TT + t + 1)

                def hidden(q, s):
                    act.wait_ge(acc_step, 6 * q + 5)
                    wait(act, hid_ready, q - 1)
                    nc.scalar.activation(gate[s][:], acc[s][0][:], ACT.Silu).then_inc(silu_ready, 1)

                def hidden_hi(q, s):
                    act.wait_ge(prod_ready, q + 1)
                    wait(act, hid_used, q - 1)
                    nc.scalar.activation(hid_hi[s][:], gate[s][:], ACT.Copy).then_inc(hid_hi_ready, 1)

                first_turn = [True]
                expand(0)
                for t in range(TT):
                    normalize(0, t)
                for c in range(KC):
                    modulate(0, c)
                expand(1)
                first_turn[0] = False

                def emit(n, par, last):
                    first = isinstance(n, int) and n == 0
                    for f in range(FC):
                        q = n * FC + f
                        s = slot(par, f)
                        if not last and TURN_AT < f <= TURN_AT + KC:
                            modulate(n + 1, f - TURN_AT - 1)
                        if f > 0 or not first:
                            hidden(q - 1, 1 - s)
                        for u in range(2):
                            act.wait_ge(part_done, 8 * q + u + 1)
                            wait(act, prod_ready, q - 1)
                            if first and f == 0:
                                act.wait_ge(scale_ready, 1)
                            nc.scalar.activation(acc[s][u][:], part[u][:], ACT.Identity,
                                                 scale=scale[:, u, f, 0:1]).then_inc(acc_first, 1)
                        if f > 0 or not first:
                            hidden_hi(q - 1, 1 - s)
                        if first and f + 2 < FC:
                            expand(f + 2)
                        if f == OUT_AT and not first:
                            squares(n - 1)
                        if not last:
                            if NORM_AT <= f < NORM_AT + TT:
                                normalize(n + 1, f - NORM_AT)

                def finish():
                    q = NB * FC
                    hidden(q - 1, slot(1, FC - 1))
                    hidden_hi(q - 1, slot(1, FC - 1))
                    squares(NB - 1)

                pairs(act, emit, finish)

            @block.vector
            def _(dve):
                prep = Steps(dve, prep_steps, 2 * FC)
                outs = Steps(dve, rms_steps, 13)

                def unpack(f):
                    dve.wait_ge(words_loaded[f % 2], 16 * (NIB + 1) * (f // 2 + 1))
                    r = raw[f % 2][:]
                    nc.vector.tensor_scalar(r, r, shift_sb[:, 0:1], 3, ALU.logical_shift_left,
                                            ALU.arith_shift_right).then_inc(prep_steps, 1)
                    dve.wait_ge(prep_steps, f + 1)
                    nc.vector.tensor_scalar(r, r, HALF_BITS, None, ALU.bitwise_and).then_inc(masked, 1)
                    dve.wait_ge(masked, f + 1)
                    wait(dve, down_ready, f)
                    half = r.bitcast(F16).rearrange("p (n two) -> p n two", two=2)[:, :, 1]
                    nc.vector.scalar_tensor_tensor(down_full[:], half[:, GU:GU + D], FP4_SCALE, down_scale[f % 2][:],
                                                   ALU.mult, ALU.mult).then_inc(down_full_ready, 1)

                def split(n, c, par):
                    dve.wait_ge(h_full_ready, n * KC + c + 1)
                    nc.vector.tensor_copy(h_hi[par][:, c, :], h_full[c % 2][:]).then_inc(h_hi_ready, 1)
                    dve.wait_ge(h_hi_ready, n * KC + c + 1)
                    nc.vector.tensor_tensor(h_lo[par][:, c, :], h_full[c % 2][:], h_hi[par][:, c, :].bitcast(F32),
                                            ALU.subtract).then_inc(h_ready, 1)

                def finish_out(n):
                    outs.start(n)
                    dve.wait_ge(squares_ready, (n + 1) * TT)
                    inverse_sqrt(nc, outs, rms[:], work, sum_sq[:], 1.0 / D, RMS_EPS)
                    dve.wait_ge(gb_loaded, 16 * (n + 1))
                    wait(dve, out_stored, 16 * n)
                    for t in range(TT):
                        nc.vector.scalar_tensor_tensor(o_sb[:, t, :], y[t][:], rms[:, t:t + 1], gb_all[:],
                                                       ALU.mult, ALU.mult).then_inc(y_read, 1)
                    outs.end()

                dve.wait_ge(scales_loaded, 32)
                unpack(0)
                nc.vector.tensor_copy(scale[:].rearrange("p u f g -> p (u f g)"), scale16[:]).then_inc(scale_ready, 1)
                for c in range(KC):
                    split(0, c, 0)
                unpack(1)

                def product(q, s):
                    dve.wait_ge(silu_ready, q + 1)
                    dve.wait_ge(acc_step, 6 * q + 6)
                    nc.vector.tensor_tensor(gate[s][:], gate[s][:], acc[s][1][:], ALU.mult).then_inc(prod_ready, 1)

                def emit(n, par, last):
                    first = isinstance(n, int) and n == 0
                    for f in range(FC):
                        q = n * FC + f
                        s = slot(par, f)
                        if f == 0 and first:
                            dve.wait_ge(scale_ready, 1)
                        for g in range(1, KC):
                            for u in range(2):
                                dve.wait_ge(part_done, 8 * q + 2 * g + u + 1)
                                if g == 1:
                                    dve.wait_ge(acc_first, 2 * q + u + 1)
                                else:
                                    dve.wait_ge(acc_step, 6 * q + 2 * (g - 2) + u + 1)
                                nc.vector.scalar_tensor_tensor(acc[s][u][:], part[(2 * g + u) % 4][:],
                                                               scale[:, u, f, g:g + 1], acc[s][u][:],
                                                               ALU.mult, ALU.add).then_inc(acc_step, 1)
                            if g == 1 and not (first and f == 0):
                                product(q - 1, 1 - s)
                        if first and f + 2 < FC:
                            unpack(f + 2)
                        if f == OUT_AT + 1 and not first:
                            finish_out(n - 1)
                        if not last and TURN_AT < f <= TURN_AT + KC:
                            split(n + 1, f - TURN_AT - 1, 1 - par)

                def finish():
                    product(NB * FC - 1, slot(1, FC - 1))
                    finish_out(NB - 1)

                pairs(dve, emit, finish)

            @block.tensor
            def _(pe):
                owner = {}

                def claim(i):
                    if i in owner:
                        wait(pe, *owner[i])

                def transposes(n, c, i):
                    claim(i)
                    if c == 0:
                        pe.wait_ge(xn_ready, (n + 1) * TT)
                    for t in range(TT):
                        last = nc.tensor.transpose(part[i][:, t * P:(t + 1) * P],
                                                   xn[:, t, c].rearrange("p s a -> p (s a)"), ident)
                    last.then_inc(turned, 1)
                    owner[i] = (h_full_ready, n * KC + c + 1)

                def gate_up(q, f, par):
                    for g in range(KC):
                        for u in range(2):
                            i = (2 * g + u) % 4
                            claim(i)
                            w = gu_w[:, f, g, u, :]
                            split_matmul(nc, part[i][:], [(w, h_hi[par][:, g, :]), (w, h_lo[par][:, g, :])],
                                         True, True).then_inc(part_done, 1)
                            owner[i] = (acc_first, 2 * q + u + 1) if g == 0 else (acc_step, 6 * q + 2 * (g - 1) + u + 1)

                def down(q, f, s):
                    pe.wait_ge(hid_ready, q + 1)
                    for t in range(TT):
                        ts = slice(t * P, (t + 1) * P)
                        last = split_matmul(nc, y[t][:], [(hid_hi[s][:, ts], down_hi[:, f, :]),
                                                          (hid_hi[s][:, ts], down_lo[:, f, :]),
                                                          (hid_lo[s][:, ts], down_hi[:, f, :])], f == 0, f == FC - 1)
                    last.then_inc(hid_used, 1)

                for c in range(KC):
                    transposes(0, c, c)

                def emit(n, par, last):
                    first = isinstance(n, int) and n == 0
                    if not first:
                        for i in range(4):
                            owner[i] = (acc_step, 6 * n * FC)
                        owner[0] = (acc_step, 6 * n * FC)
                    pe.wait_ge(h_ready, (n + 1) * KC)
                    for f in range(FC):
                        q = n * FC + f
                        if first:
                            pe.wait_ge(gu_ready, f + 1)
                        gate_up(q, f, par)
                        if f == 0 and not first:
                            down(q - 1, FC - 1, slot(1 - par, FC - 1))
                        if f >= 2:
                            if f == 2:
                                wait(pe, y_read, n * TT)
                            if first:
                                pe.wait_ge(down_ready, f - 1)
                            down(q - 2, f - 2, slot(par, f - 2))
                        if not last and TURN_AT <= f < TURN_AT + KC:
                            transposes(n + 1, f - TURN_AT, 0)
                    down(n * FC + FC - 2, FC - 2, slot(par, FC - 2)) if not first else (
                        pe.wait_ge(down_ready, FC), down(FC - 2, FC - 2, slot(par, FC - 2)))

                pairs(pe, emit, lambda: down(NB * FC - 1, FC - 1, slot(1, FC - 1)))


def kernel(**inputs):
    import numpy as np
    import concourse.bacc as bacc
    from concourse.bass_utils import run_bass_kernel_spmd

    a = {name: np.asarray(value) for name, value in inputs.items()}
    order = np.arange(P).reshape(WPG, NIB).T.reshape(-1)

    consts = np.zeros((P, C_END), np.float32)
    consts[:, C_ID:C_ID + P] = np.eye(P)
    head = np.arange(P) // DK
    consts[:, C_MASK:C_MASK + P] = head[:, None] == head[None, :]
    for k in range(KC):
        one = (k * (P // DK) + head)[:, None] == np.arange(HEADS)[None, :]
        consts[:, C_HEAD + k * HEADS:C_HEAD + (k + 1) * HEADS] = one
        for row in (0, LO_ROW):
            consts[row:row + HEADS, C_SEL + k * P:C_SEL + (k + 1) * P] = one.T
    shifts = (28 - 4 * (np.arange(P) // WPG)).astype(np.int32).reshape(P, 1)

    wmod = a["L0_wmod"].reshape(D, 6, KC, P).copy()
    for section in (3, 4):
        wmod[:, section] = wmod[:, section][:, :, order]
    gu = a["L0_ffn_gate_up_packed"].reshape(2, FC, P, KC, WPG)[:, :, order]
    gu = gu.transpose(1, 4, 3, 0, 2).reshape(FC, WPG, KC * 2 * P)
    down = a["L0_ffn_down_packed"].reshape(D, FC, WPG).transpose(1, 2, 0)
    gu_scales = a["L0_ffn_gate_up_scales"].reshape(KC, 2, FC, P)[:, :, :, order].transpose(3, 1, 2, 0)

    arrays = {
        "x": a["L0_attn_x"].reshape(BATCH * SEQ, D),
        "wq_t": a["L0_attn_wq"].T, "wk_t": a["L0_attn_wk"].T, "wv_t": a["L0_attn_wv"].T, "wo_t": a["L0_attn_wo"].T,
        "bq": a["L0_attn_bq"].reshape(KC, P).T, "bk": a["L0_attn_bk"].reshape(1, D),
        "bv": a["L0_attn_bv"], "bo": a["L0_attn_bo"],
        "gu_down_words": np.concatenate([gu, down], axis=2),
        "gu_scales": gu_scales.reshape(P, 2 * FC * KC),
        "down_scales": a["L0_ffn_down_scales"],
        "c_t": a["L0_c"].T.reshape(KC, P, BATCH).transpose(1, 0, 2),
        "wmod": wmod.reshape(D, 6 * D),
        "consts": consts, "shifts": shifts,
    }
    nc = bacc.Bacc("TRN2", target_bir_lowering=False, num_devices=1)
    feed, aps = {}, {}
    for name, value in arrays.items():
        feed[f"in_{name}"] = np.ascontiguousarray(value)
        aps[name] = nc.dram_tensor(f"in_{name}", value.shape, mybir.dt.from_np(value.dtype), kind="ExternalInput").ap()
    out = nc.dram_tensor("out", (BATCH * SEQ, D), F32, kind="ExternalOutput").ap()
    adaln_block(nc, **aps, out=out)
    result = run_bass_kernel_spmd(nc, [feed], core_ids=[0])
    return result.results[0]["out"].reshape(BATCH, SEQ, D)
```

```python
from contextlib import ExitStack

import concourse.bass as bass
from concourse import mybir

F32 = mybir.dt.float32
F32R = mybir.dt.float32r
F16 = mybir.dt.float16
I32 = mybir.dt.int32
ALU = mybir.AluOpType
ACT = mybir.ActivationFunctionType

P = 128
BATCH = 4
SEQ = 1024
D = 512
HEADS = 16
DK = D // HEADS
KC = D // P
TOK = 512
TT = TOK // P
JB = SEQ // TOK
INNER = 1408
FC = INNER // P
NIB = 8
WPG = P // NIB
XW = D + 2
LN_EPS = 1e-5
RMS_EPS = 1e-6
DEN_EPS = 1e-8
C_ID, C_MASK, C_HEAD, C_SEL, C_END = 0, P, 2 * P, 2 * P + KC * HEADS, 2 * P + KC * HEADS + D
LO_ROW = 32


def wait(eng, sem, value):
    if isinstance(value, int) and value <= 0:
        return
    eng.wait_ge(sem, value)


class Steps:

    def __init__(self, eng, sem, per_round):
        self.eng, self.sem, self.per_round = eng, sem, per_round

    def start(self, rnd):
        self.base, self.n = rnd * self.per_round, 0

    def mark(self, ins):
        ins.then_inc(self.sem, 1)
        self.n += 1
        return self.base + self.n

    def link(self, ins):
        self.eng.wait_ge(self.sem, self.mark(ins))

    def end(self):
        assert self.n == self.per_round, self.n


def inverse_sqrt_guess(nc, steps, out, work, src, scale, eps):
    v, a, h = work
    steps.link(nc.vector.tensor_scalar(v, src, scale, eps, ALU.mult, ALU.add))
    nc.vector.tensor_scalar(h, v, -0.5, None, ALU.mult)
    steps.link(nc.vector.tensor_scalar(a.bitcast(I32), v.bitcast(I32), 1, None, ALU.arith_shift_right))
    steps.link(nc.vector.tensor_scalar(out.bitcast(I32), a.bitcast(I32), -1.0, float(0x5F3759DF), ALU.mult, ALU.add))


def inverse_sqrt_newton(nc, steps, out, work):
    _, a, h = work
    steps.link(nc.vector.tensor_tensor(a, out, out, ALU.mult))
    steps.link(nc.vector.tensor_tensor(a, a, h, ALU.mult))
    steps.link(nc.vector.scalar_tensor_tensor(out, a, 1.5, out, ALU.add, ALU.mult))


def inverse_sqrt(nc, steps, out, work, src, scale, eps):
    inverse_sqrt_guess(nc, steps, out, work, src, scale, eps)
    for _ in range(3):
        inverse_sqrt_newton(nc, steps, out, work)


def split_matmul(nc, out, parts, start_first, stop_last):
    for i, (stationary, moving) in enumerate(parts):
        last = nc.tensor.matmul(out, stationary, moving, start=start_first and i == 0,
                                stop=stop_last and i == len(parts) - 1)
    return last


def adaln_block(nc, x, wq_t, wk_t, wv_t, wo_t, bq, bk, bv, bo, gu_down_words, gu_scales, down_scales,
                c_t, wmod, consts, shifts, out):
    mod_cols_dram = nc.dram_tensor("mod_cols", (BATCH, P, 4 * KC), F32).ap()
    gate_rows_dram = nc.dram_tensor("gate_rows", (BATCH, 2, D), F32).ap()
    x2_dram = nc.dram_tensor("x_after_attention", (BATCH * JB, P, TT * XW), F32).ap()
    x_blocks = x.rearrange("(n p t) d -> n p (t d)", p=P, t=TT)
    out_blocks = out.rearrange("(n p t) d -> n p (t d)", p=P, t=TT)

    with ExitStack() as whole:
        const_sb = whole.enter_context(nc.sbuf_tensor("const_sb", [P, C_END], F32))
        with ExitStack() as attention_memory:
            def sb(name, shape, dt=F32):
                return attention_memory.enter_context(nc.sbuf_tensor(name, shape, dt))

            weights = {
                "wq": (sb("wq_hi", [P, KC, D], F32R), sb("wq_lo", [P, KC, D], F32R)),
                "wk": (sb("wk_hi", [P, KC, D], F32R), sb("wk_lo", [P, KC, D], F32R)),
                "wv": (sb("wv_hi", [P, KC, D], F32R), sb("wv_lo", [P, KC, D], F32R)),
                "wo": sb("wo_sb", [P, KC, D]),
                "bq": sb("bq_sb", [P, KC]),
                "bq_neg": sb("bq_neg", [P, KC]),
                "bk": sb("bk_rows", [LO_ROW + 1, D], F32R),
                "ones": sb("ones_rows", [LO_ROW + 1, P], F32R),
                "bv": sb("bv_all", [P, D]),
                "bo": sb("bo_all", [P, D]),
                "sel": sb("head_rows", [LO_ROW + HEADS, D], F32R),
            }
            setup(nc, weights, const_sb, wq_t, wk_t, wv_t, wo_t, bq, bk, bv, bo, c_t, wmod, consts,
                  mod_cols_dram, gate_rows_dram)
            attention(nc, weights, const_sb, x_blocks, x2_dram, mod_cols_dram, gate_rows_dram)
        mlp(nc, const_sb, gu_down_words, gu_scales, down_scales, shifts, x2_dram, mod_cols_dram,
            gate_rows_dram, out_blocks)


def setup(nc, weights, const_sb, wq_t, wk_t, wv_t, wo_t, bq, bk, bv, bo, c_t, wmod, consts,
          mod_cols_dram, gate_rows_dram):
    with ExitStack() as ctx:
        def sb(name, shape, dt=F32):
            return ctx.enter_context(nc.sbuf_tensor(name, shape, dt))

        def sem(name):
            return ctx.enter_context(nc.semaphore(name))

        raw = [sb(f"{n}_raw", [P, KC, D]) for n in ("wq", "wk", "wv")]
        wmod_sb = sb("wmod_sb", [P, KC, 6 * D])
        c_sb = sb("c_sb", [P, KC, BATCH])
        silu_c = sb("silu_c", [P, KC, BATCH])
        mod_cols = sb("mod_cols_sb", [P, BATCH, 4 * KC])
        rows_raw = sb("rows_raw", [BATCH, 2 * D])
        rows_abs = sb("rows_abs", [BATCH, 2 * D])
        rows_sign = sb("rows_sign", [BATCH, 2 * D])
        gate_rows = sb("gate_rows_sb", [BATCH, 2 * D])
        bk_raw = sb("bk_raw", [1, D])
        cols_psum = ctx.enter_context(nc.psum_tensor("cols_psum", [P, 512], F32))
        rows_psum = [ctx.enter_context(nc.psum_tensor(f"rows_psum{i}", [P, 512], F32)) for i in range(2)]

        c_loaded, wmod_loaded, small_loaded, late_loaded = (
            sem("c_loaded"), sem("wmod_loaded"), sem("small_loaded"), sem("late_loaded"))
        raw_loaded = [sem(f"raw_loaded{i}") for i in range(3)]
        silu_done, mod_done, hi_done, mod_saved = sem("silu_done"), sem("mod_done"), sem("hi_done"), sem("mod_saved")
        cols_ready, rows_ready, zeroed, steps_sem = sem("cols_ready"), sem("rows_ready"), sem("zeroed"), sem("setup_steps")
        col_sections = [0, 1, 3, 4]
        row_sections = [2, 5]

        with nc.Block() as block:
            @block.sync
            def _(sp):
                sp.dma_start(c_sb[:], c_t).then_inc(c_loaded, 16)
                for k in range(KC):
                    sp.dma_start(wmod_sb[:, k, :], wmod[k * P:(k + 1) * P, :]).then_inc(wmod_loaded, 16)
                sp.wait_ge(cols_ready, 4)
                for b in range(BATCH):
                    sp.dma_start(mod_cols_dram[b], mod_cols[:, b, :]).then_inc(mod_saved, 16)
                sp.wait_ge(rows_ready, 1)
                sp.dma_start(gate_rows_dram.rearrange("b two d -> b (two d)"), gate_rows[:]).then_inc(mod_saved, 16)
                sp.wait_ge(mod_saved, 16 * (BATCH + 1))
                sp.wait_ge(late_loaded, 64)

            @block.scalar
            def _(act):
                act.dma_start(const_sb[:], consts).then_inc(small_loaded, 16)
                act.dma_start(bk_raw[:], bk).then_inc(small_loaded, 16)
                for i, w in enumerate((wk_t, wv_t, wq_t)):
                    act.dma_start(raw[i][:], w.rearrange("(k p) n -> p k n", p=P)).then_inc(raw_loaded[i], 16)
                act.dma_start(weights["wo"][:], wo_t.rearrange("(k p) n -> p k n", p=P)).then_inc(late_loaded, 16)
                act.dma_start(weights["bq"][:], bq).then_inc(late_loaded, 16)
                act.dma_start(weights["bv"][:], bv.partition_broadcast(P)).then_inc(late_loaded, 16)
                act.dma_start(weights["bo"][:], bo.partition_broadcast(P)).then_inc(late_loaded, 16)
                act.wait_ge(c_loaded, 16)
                nc.scalar.activation(silu_c[:], c_sb[:], ACT.Silu).then_inc(silu_done, 1)
                act.wait_ge(small_loaded, 32)
                act.wait_ge(zeroed, 1)
                nc.scalar.activation(weights["bk"][0:1, :], bk_raw[:], ACT.Copy).then_inc(hi_done, 1)
                nc.scalar.activation(weights["sel"][:], const_sb[0:LO_ROW + HEADS, C_SEL:C_END], ACT.Copy).then_inc(hi_done, 1)
                for r in (0, LO_ROW):
                    nc.scalar.activation(weights["ones"][r:r + 1, :], const_sb[r:r + 1, C_ID:C_ID + P],
                                         ACT.Identity, bias=const_sb[r:r + 1, C_MASK + r:C_MASK + r + 1],
                                         scale=0.0).then_inc(hi_done, 1)
                act.wait_ge(late_loaded, 64)
                nc.scalar.activation(weights["bq_neg"][:], weights["bq"][:], ACT.Copy, scale=-1.0)
                for i, name in enumerate(("wk", "wv", "wq")):
                    act.wait_ge(raw_loaded[i], 16)
                    nc.scalar.activation(weights[name][0][:], raw[i][:], ACT.Copy).then_inc(hi_done, 1)

            @block.tensor
            def _(pe):
                pe.wait_ge(silu_done, 1)
                pe.wait_ge(wmod_loaded, 16 * KC)
                for s, section in enumerate(col_sections):
                    for j in range(KC):
                        at = (s * KC + j) * BATCH
                        for k in range(KC):
                            f0 = section * D + j * P
                            last = nc.tensor.matmul(cols_psum[:, at:at + BATCH], wmod_sb[:, k, f0:f0 + P],
                                                    silu_c[:, k, :], start=(k == 0), stop=(k == KC - 1))
                last.then_inc(mod_done, 1)
                for i, section in enumerate(row_sections):
                    for k in range(KC):
                        last = nc.tensor.matmul(rows_psum[i][0:BATCH, :], silu_c[:, k, :],
                                                wmod_sb[:, k, section * D:(section + 1) * D],
                                                start=(k == 0), stop=(k == KC - 1))
                    last.then_inc(mod_done, 1)

            @block.vector
            def _(dve):
                steps = Steps(dve, steps_sem, 7)
                steps.start(0)
                steps.link(nc.vector.memset(weights["bk"][:].bitcast(F32), 0.0))
                nc.vector.memset(weights["ones"][:].bitcast(F32), 0.0).then_inc(zeroed, 1)
                dve.wait_ge(mod_done, 1)
                for s in range(4):
                    src = cols_psum[:, s * KC * BATCH:(s + 1) * KC * BATCH].rearrange("p (j b) -> p b j", b=BATCH)
                    nc.vector.tensor_scalar(mod_cols[:, :, s * KC:(s + 1) * KC], src, float(s % 2), None,
                                            ALU.add).then_inc(cols_ready, 1)
                dve.wait_ge(mod_done, 3)
                for i in range(2):
                    s = slice(i * D, (i + 1) * D)
                    steps.link(nc.vector.tensor_copy(rows_raw[:, s], rows_psum[i][0:BATCH, :]))
                steps.link(nc.vector.scalar_tensor_tensor(rows_abs[:], rows_raw[:], -1.0, rows_raw[:], ALU.mult, ALU.max))
                steps.link(nc.vector.tensor_scalar(rows_abs[:], rows_abs[:], 0.25, None, ALU.max))
                steps.link(nc.vector.tensor_scalar(rows_sign[:], rows_raw[:], 0.0, 2.0, ALU.is_ge, ALU.mult))
                nc.vector.scalar_tensor_tensor(gate_rows[:], rows_sign[:], -1.0, rows_abs[:], ALU.add,
                                               ALU.mult).then_inc(rows_ready, 1)
                dve.wait_ge(hi_done, 1)
                steps.link(nc.vector.tensor_tensor(weights["bk"][LO_ROW:LO_ROW + 1, :], bk_raw[:],
                                                   weights["bk"][0:1, :].bitcast(F32), ALU.subtract))
                for i, name in enumerate(("wk", "wv", "wq")):
                    dve.wait_ge(hi_done, 5 + i)
                    nc.vector.tensor_tensor(weights[name][1][:], raw[i][:], weights[name][0][:].bitcast(F32),
                                            ALU.subtract)
                steps.end()


def attention(nc, weights, const_sb, x_blocks, x2_dram, mod_cols_dram, gate_rows_dram):
    wq, wk, wv = weights["wq"], weights["wk"], weights["wv"]
    ident = const_sb[:, C_ID:C_ID + P]
    mask = const_sb[:, C_MASK:C_MASK + P]
    head_mask = const_sb[:, C_HEAD:C_SEL].rearrange("p (k h) -> p k h", h=HEADS)
    VW = P + 1

    with ExitStack() as ctx:
        def sb(name, shape, dt=F32):
            return ctx.enter_context(nc.sbuf_tensor(name, shape, dt))

        def bank(name):
            return ctx.enter_context(nc.psum_tensor(name, [P, 512], F32))

        def sem(name):
            return ctx.enter_context(nc.semaphore(name))

        x_in = [sb(f"x_in{j}", [P, TT, D]) for j in range(JB)]
        stats = sb("stats", [P, TT, 6])
        moments = sb("moments", [P, 3, TT])
        work = [sb(f"rsqrt_work{i}", [P, TT])[:] for i in range(3)]
        rstd = sb("rstd", [P, TT])
        shift = sb("shift", [P, TT])
        mod_now = sb("mod_now", [P, 4 * KC])
        h_full = [sb(f"h_full{i}", [P, TOK]) for i in range(2)]
        h_hi, h_lo = sb("h_hi", [P, KC, TOK], F32R), sb("h_lo", [P, KC, TOK], F32R)
        k_exp = [sb(f"k_exp{i}", [P, D]) for i in range(2)]
        k_sb = [sb(f"k_sb{i}", [P, D]) for i in range(2)]
        v_sb = [sb(f"v_sb{i}", [P, KC, VW]) for i in range(2)]
        q_exp = [sb(f"q_exp{i}", [P, TOK]) for i in range(2)]
        q_sb = [sb(f"q_sb{j}", [P, KC, TOK]) for j in range(JB)]
        credit = sb("credit", [P, 5])
        k_sum = sb("k_sum", [P, KC])
        k_sum_heads = sb("k_sum_heads", [P, KC, HEADS])
        kv_sb = sb("kv_sb", [P, KC, P])
        kv_t = sb("kv_t", [P, D])
        m_full = [sb(f"m_full{i}", [P, D]) for i in range(2)]
        m_hi, m_lo = sb("m_hi", [P, KC, D], F32R), sb("m_lo", [P, KC, D], F32R)
        ga_all = sb("ga_all", [P, D])
        ga_bo = sb("ga_bo", [P, D])
        recip = sb("recip", [HEADS, TOK])
        recip_rows = sb("recip_rows", [LO_ROW + HEADS, TOK], F32R)
        qn_full = [sb(f"qn_full{i}", [P, TOK]) for i in range(2)]
        qn_hi, qn_lo = sb("qn_hi", [P, KC, TOK], F32R), sb("qn_lo", [P, KC, TOK], F32R)
        x2 = [sb(f"x2_{j}", [P, TT, XW]) for j in range(JB)]

        turn = [bank(f"turn{i}") for i in range(2)]
        prod = [bank(f"prod{i}") for i in range(2)]
        kv_psum = [bank(f"kv_psum{i}") for i in range(2)]
        den = bank("den")
        spread = bank("spread")

        x_loaded = [sem(f"x_loaded{j}") for j in range(JB)]
        mod_loaded = sem("mod_loaded")
        ga_loaded = sem("ga_loaded")
        x2_loaded = [sem(f"x2_loaded{j}") for j in range(JB)]
        x2_stored = [sem(f"x2_stored{j}") for j in range(JB)]
        norm_ready, xn_ready, turned, h_full_ready, h_ready = (
            sem("norm_ready"), sem("xn_ready"), sem("turned"), sem("h_full_ready"), sem("h_ready"))
        k_product, v_product, q_product, m_product, o_product = (
            sem("k_product"), sem("v_product"), sem("q_product"), sem("m_product"), sem("o_product"))
        k_exp_ready, k_ready, v_ready, q_exp_ready, q_ready = (
            sem("k_exp_ready"), sem("k_ready"), sem("v_ready"), sem("q_exp_ready"), sem("q_ready"))
        k_relu_ready, q_relu_ready = sem("k_relu_ready"), sem("q_relu_ready")
        kv_tile, heads_ready, kv_ready, kv_turned, kv_t_ready = (
            sem("kv_tile"), sem("heads_ready"), sem("kv_ready"), sem("kv_turned"), sem("kv_t_ready"))
        m_read, m_ready = sem("m_read"), sem("m_ready")
        den_product, recip_ready, spread_ready, spread_read, qn_ready = (
            sem("den_product"), sem("recip_ready"), sem("spread_ready"), sem("spread_read"), sem("qn_ready"))
        ga_bo_ready, x2_biased, o_read, x2_ready = sem("ga_bo_ready"), sem("x2_biased"), sem("o_read"), sem("x2_ready")
        ones_set, zero_set = sem("ones_set"), sem("zero_set")
        norm_steps, kv_steps, q_steps, split_steps, out_steps = (
            sem("norm_steps"), sem("kv_steps"), sem("q_steps"), sem("split_steps"), sem("out_steps"))

        NT = JB * TT
        NC = JB * KC

        def rounds(eng, emit):
            emit(0, None, True)
            with eng.Fori(1, BATCH - 1) as b:
                emit(b, b - 1, True)
            emit(BATCH - 1, BATCH - 2, False)
            emit(None, BATCH - 1, False)

        def following(b, j):
            return (b, j + 1) if j + 1 < JB else (b + 1, 0)

        with nc.Block() as block:
            @block.sync
            def _(sp):
                def load_x(b, j):
                    wait(sp, turned, (b - 1) * NC + (j + 1) * KC)
                    sp.dma_start(x_in[j][:].rearrange("p t d -> p (t d)"),
                                 x_blocks[bass.ds(b * JB + j, 1)].squeeze(0)).then_inc(x_loaded[j], 16)

                def load_x2(e, j):
                    sp.wait_ge(x2_stored[j], 16 * (e + 1))
                    sp.dma_start(x2[j][:, :, 0:D], x_blocks[bass.ds(e * JB + j, 1)].squeeze(0)
                                 .rearrange("p (t d) -> p t d", t=TT)).then_inc(x2_loaded[j], 16)

                def load_batch(b):
                    load_x(b, 0)
                    wait(sp, h_full_ready, b * NC)
                    sp.dma_start(mod_now[:], mod_cols_dram[bass.ds(b, 1)].squeeze(0)).then_inc(mod_loaded, 16)
                    load_x(b, 1)

                def load_leaving(e):
                    load_x2(e, 0)
                    sp.wait_ge(q_ready, (e + 1) * NC)
                    sp.wait_ge(ga_bo_ready, e + 1)
                    sp.dma_start(ga_all[:], gate_rows_dram[bass.ds(e, 1), 0, :].squeeze(0).partition_broadcast(P)
                                 ).then_inc(ga_loaded, 16)
                    load_x2(e, 1)

                sp.wait_ge(zero_set, 1)
                load_batch(0)
                with sp.Fori(1, BATCH) as b:
                    load_batch(b)
                    load_leaving(b - 1)
                load_leaving(BATCH - 1)
                for j in range(JB):
                    sp.wait_ge(x2_stored[j], 16 * (BATCH + 1))

            @block.gpsimd
            def _(pool):
                for j in range(JB):
                    nc.gpsimd.memset(credit[:, j:j + 1], 0.0).then_inc(x2_stored[j], 16)
                nc.gpsimd.memset(credit[:, 2:3], 0.0).then_inc(ga_bo_ready, 1)
                nc.gpsimd.memset(credit[:, 3:4], 0.0).then_inc(x2_biased, 1)
                nc.gpsimd.memset(credit[:, 4:5], 0.0).then_inc(o_read, 2)
                nc.gpsimd.memset(recip_rows[:].bitcast(F32), 0.0).then_inc(zero_set, 1)
                for i in range(2):
                    nc.gpsimd.memset(v_sb[i][:, :, P:VW], 1.0).then_inc(ones_set, 1)

                def emit(b, e, more):
                    if e is None:
                        return
                    pool.wait_ge(ga_loaded, 16 * (e + 1))
                    pool.wait_ge(x2_biased, JB * e + 1)
                    nc.gpsimd.tensor_tensor(ga_bo[:], ga_all[:], weights["bo"][:], ALU.mult).then_inc(ga_bo_ready, 1)
                    pool.wait_ge(ga_bo_ready, e + 2)
                    for j in range(JB):
                        pool.wait_ge(x2_loaded[j], 16 * (e + 1))
                        for t in range(TT):
                            last = nc.gpsimd.tensor_tensor(x2[j][:, t, 0:D], x2[j][:, t, 0:D], ga_bo[:], ALU.add)
                        last.then_inc(x2_biased, 1)

                rounds(pool, emit)

            @block.scalar
            def _(act):
                def normalize(b, j):
                    act.wait_ge(norm_ready, b * JB + j + 1)
                    for t in range(TT):
                        nc.scalar.activation(x_in[j][:, t, :], x_in[j][:, t, :], ACT.Identity,
                                             bias=shift[:, t:t + 1], scale=rstd[:, t:t + 1]).then_inc(xn_ready, 1)

                def modulate(b, j, c):
                    n = b * NC + j * KC + c
                    if j == 0 and c == 0:
                        act.wait_ge(mod_loaded, 16 * (b + 1))
                    act.wait_ge(turned, n + 1)
                    wait(act, h_ready, n - 1)
                    nc.scalar.activation(h_full[c % 2][:], turn[c % 2][:], ACT.Identity,
                                         bias=mod_now[:, c:c + 1], scale=mod_now[:, KC + c:KC + c + 1]
                                         ).then_inc(h_full_ready, 1)

                def store(e, j):
                    act.wait_ge(x2_ready, e * JB + j + 1)
                    act.dma_start(x2_dram[bass.ds(e * JB + j, 1)].squeeze(0),
                                  x2[j][:].rearrange("p t d -> p (t d)")).then_inc(x2_stored[j], 16)

                def take_kv(b, j, t):
                    n = b * NT + j * TT + t
                    act.wait_ge(k_product, n + 1)
                    wait(act, k_ready, n - 1)
                    nc.scalar.activation(k_exp[t % 2][:], prod[0][:], ACT.Relu, scale=-1.0).then_inc(k_relu_ready, 1)
                    act.wait_ge(k_relu_ready, n + 1)
                    nc.scalar.activation(k_exp[t % 2][:], k_exp[t % 2][:], ACT.Exp, scale=-1.0
                                         ).then_inc(k_exp_ready, 1)
                    act.wait_ge(v_product, n + 1)
                    wait(act, kv_tile, n - 1)
                    nc.scalar.activation(v_sb[t % 2][:, :, 0:P], prod[1][:].rearrange("p (g n) -> p g n", g=KC),
                                         ACT.Copy).then_inc(v_ready, 1)

                def take_q(b, j, k):
                    n = b * NC + j * KC + k
                    act.wait_ge(q_product, n + 1)
                    wait(act, q_ready, n - 1)
                    nc.scalar.activation(q_exp[k % 2][:], prod[k % 2][:], ACT.Relu, scale=-1.0,
                                         bias=weights["bq_neg"][:, k:k + 1]).then_inc(q_relu_ready, 1)
                    act.wait_ge(q_relu_ready, n + 1)
                    nc.scalar.activation(q_exp[k % 2][:], q_exp[k % 2][:], ACT.Exp, scale=-1.0
                                         ).then_inc(q_exp_ready, 1)

                act.wait_ge(ones_set, 2)
                normalize(0, 0)
                for c in range(KC):
                    modulate(0, 0, c)

                def emit(b, e, more):
                    for j in range(JB):
                        next_in = b is not None and (j + 1 < JB or more)
                        if b is not None:
                            for t in range(TT):
                                take_kv(b, j, t)
                            for k in range(KC):
                                take_q(b, j, k)
                                if next_in and k == 1:
                                    normalize(*following(b, j))
                        if next_in:
                            for c in range(KC):
                                modulate(*following(b, j), c)
                        if e is not None:
                            store(e, j)

                rounds(act, emit)

            @block.vector
            def _(dve):
                norms = Steps(dve, norm_steps, 16)
                kvs = Steps(dve, kv_steps, 1 + KC)
                qs = Steps(dve, q_steps, JB * KC)
                splits = Steps(dve, split_steps, KC)
                outs = Steps(dve, out_steps, KC + JB * (2 + KC + TT + 15))

                def normalization(steps, rstd_out, shift_out):
                    both, apart, spread_sq = moments[:, 0, :], moments[:, 1, :], moments[:, 2, :]
                    nc.vector.tensor_tensor(both, stats[:, :, 1], stats[:, :, 4], ALU.add)
                    nc.vector.tensor_tensor(apart, stats[:, :, 1], stats[:, :, 4], ALU.subtract)
                    steps.link(nc.vector.tensor_tensor(spread_sq, stats[:, :, 2], stats[:, :, 5], ALU.add))
                    steps.link(nc.vector.tensor_tensor(apart, apart, apart, ALU.mult))
                    steps.link(nc.vector.scalar_tensor_tensor(spread_sq, apart, D / 4, spread_sq, ALU.mult, ALU.add))
                    inverse_sqrt(nc, steps, rstd_out, work, spread_sq, 1.0 / D, LN_EPS)
                    return nc.vector.scalar_tensor_tensor(shift_out, both, -0.5, rstd_out, ALU.mult, ALU.mult)

                def statistics(b, j, t):
                    if t == 0:
                        dve.wait_ge(x_loaded[j], 16 * (b + 1))
                        norms.start(b * JB + j)
                    ins = nc.vector.bn_stats(stats[:, t, :], x_in[j][:, t, :])
                    if t == TT - 1:
                        norms.mark(ins)

                def norm_in(b, j):
                    dve.wait_ge(norm_steps, norms.base + 1)
                    normalization(norms, rstd[:], shift[:]).then_inc(norm_ready, 1)
                    norms.end()

                def split_h(b, j, c):
                    if c == 0:
                        splits.start(b * JB + j)
                    dve.wait_ge(h_full_ready, b * NC + j * KC + c + 1)
                    splits.link(nc.vector.tensor_copy(h_hi[:, c, :], h_full[c % 2][:]))
                    nc.vector.tensor_tensor(h_lo[:, c, :], h_full[c % 2][:], h_hi[:, c, :].bitcast(F32),
                                            ALU.subtract).then_inc(h_ready, 1)

                def finish_kv(b):
                    dve.wait_ge(kv_tile, NT * (b + 1))
                    kvs.start(b)
                    for i in range(2):
                        last = nc.vector.tensor_copy(
                            k_sum[:, 2 * i:2 * i + 2], kv_psum[i][:, 0:2 * VW].rearrange("p (g n) -> p g n", g=2)[:, :, P])
                    kvs.link(last)
                    for k in range(KC):
                        nc.vector.tensor_scalar(k_sum_heads[:, k, :], head_mask[:, k, :], k_sum[:, k:k + 1], None,
                                                ALU.mult).then_inc(heads_ready, 1)
                    marks = []
                    for k in range(KC):
                        at = (k % 2) * VW
                        marks.append(kvs.mark(nc.vector.scalar_tensor_tensor(
                            kv_sb[:, k, :], weights["bv"][:, k * P:(k + 1) * P], k_sum[:, k:k + 1],
                            kv_psum[k // 2][:, at:at + P], ALU.mult, ALU.add)))
                    for k in range(KC):
                        dve.wait_ge(kv_steps, marks[k])
                        nc.vector.tensor_tensor(kv_sb[:, k, :], kv_sb[:, k, :], mask, ALU.mult).then_inc(kv_ready, 1)
                    kvs.end()

                def take_k(b, j, t):
                    n = b * NT + j * TT + t
                    dve.wait_ge(k_exp_ready, n + 1)
                    wait(dve, kv_tile, n - 1)
                    nc.vector.scalar_tensor_tensor(k_sb[t % 2][:], prod[0][:], 0.0, k_exp[t % 2][:],
                                                   ALU.max, ALU.add).then_inc(k_ready, 1)

                def take_q(b, j, k):
                    n = b * NC + j * KC + k
                    dve.wait_ge(q_relu_ready, n + 1)
                    qs.link(nc.vector.tensor_scalar(q_sb[j][:, k, :], prod[k % 2][:],
                                                    weights["bq"][:, k:k + 1], 0.0, ALU.add, ALU.max))
                    dve.wait_ge(q_exp_ready, n + 1)
                    nc.vector.tensor_tensor(q_sb[j][:, k, :], q_exp[k % 2][:], q_sb[j][:, k, :],
                                            ALU.add).then_inc(q_ready, 1)

                def reciprocal(e, j):
                    n = e * JB + j
                    dve.wait_ge(den_product, n + 1)
                    outs.link(nc.vector.tensor_scalar(recip[:], den[0:HEADS, :], DEN_EPS, None, ALU.add))
                    outs.link(nc.vector.reciprocal(recip[:], recip[:]))
                    nc.vector.tensor_copy(recip_rows[0:HEADS, :], recip[:]).then_inc(recip_ready, 1)
                    dve.wait_ge(recip_ready, 2 * n + 1)
                    nc.vector.tensor_tensor(recip_rows[LO_ROW:LO_ROW + HEADS, :], recip[:],
                                            recip_rows[0:HEADS, :].bitcast(F32), ALU.subtract).then_inc(recip_ready, 1)

                def split_m(e, k):
                    if k == 0:
                        dve.wait_ge(ga_loaded, 16 * (e + 1))
                    dve.wait_ge(m_product, KC * e + k + 1)
                    if k >= 2:
                        dve.wait_ge(m_ready, KC * e + k - 1)
                    nc.vector.tensor_tensor(m_full[k % 2][:], spread[:], ga_all[:], ALU.mult).then_inc(m_read, 1)
                    dve.wait_ge(m_read, KC * e + k + 1)
                    outs.link(nc.vector.tensor_copy(m_hi[:, k, :], m_full[k % 2][:]))
                    nc.vector.tensor_tensor(m_lo[:, k, :], m_full[k % 2][:], m_hi[:, k, :].bitcast(F32),
                                            ALU.subtract).then_inc(m_ready, 1)

                def scale_q(e, j, k):
                    n = e * NC + j * KC + k
                    dve.wait_ge(spread_ready, n + 1)
                    if k >= 2:
                        dve.wait_ge(qn_ready, n - 1)
                    nc.vector.tensor_tensor(qn_full[k % 2][:], q_sb[j][:, k, :], spread[:], ALU.mult).then_inc(spread_read, 1)
                    dve.wait_ge(spread_read, n + 1)
                    outs.link(nc.vector.tensor_copy(qn_hi[:, k, :], qn_full[k % 2][:]))
                    nc.vector.tensor_tensor(qn_lo[:, k, :], qn_full[k % 2][:], qn_hi[:, k, :].bitcast(F32),
                                            ALU.subtract).then_inc(qn_ready, 1)

                def take_o(e, j, t):
                    n = e * NT + j * TT + t
                    if t == 0:
                        dve.wait_ge(x2_biased, e * JB + j + 2)
                    dve.wait_ge(o_product, n + 1)
                    nc.vector.tensor_tensor(x2[j][:, t, 0:D], prod[t % 2][:], x2[j][:, t, 0:D],
                                            ALU.add).then_inc(o_read, 1)
                    dve.wait_ge(o_read, n + 3)
                    return outs.mark(nc.vector.bn_stats(stats[:, t, :], x2[j][:, t, 0:D]))

                for t in range(TT):
                    statistics(0, 0, t)
                norm_in(0, 0)
                for c in range(KC):
                    split_h(0, 0, c)

                def emit(b, e, more):
                    if b is not None:
                        qs.start(b)
                    if e is not None:
                        outs.start(e)
                        dve.wait_ge(kv_turned, e + 1)
                        nc.vector.tensor_copy(kv_t[:], turn[0][:]).then_inc(kv_t_ready, 1)
                    for j in range(JB):
                        next_in = b is not None and (j + 1 < JB or more)
                        for t in range(TT):
                            if b is not None:
                                take_k(b, j, t)
                            if e is not None and t == 0:
                                reciprocal(e, j)
                            if e is not None and j == 0:
                                split_m(e, t)
                            if next_in:
                                statistics(*following(b, j), t)
                        if next_in:
                            norm_in(*following(b, j))
                        for k in range(KC):
                            if e is not None:
                                scale_q(e, j, k)
                            if b is not None:
                                take_q(b, j, k)
                        if b is not None and j == JB - 1:
                            finish_kv(b)
                        for t in range(TT):
                            if next_in:
                                split_h(*following(b, j), t)
                            if e is not None:
                                last = take_o(e, j, t)
                        if next_in:
                            splits.end()
                        if e is not None:
                            dve.wait_ge(out_steps, last)
                            normalization(outs, x2[j][:, :, D], x2[j][:, :, D + 1]).then_inc(x2_ready, 1)
                    if b is not None:
                        qs.end()
                    if e is not None:
                        outs.end()

                rounds(dve, emit)

            @block.tensor
            def _(pe):
                def denominators(e, j):
                    for k in range(KC):
                        last = nc.tensor.matmul(den[0:HEADS, :], k_sum_heads[:, k, :], q_sb[j][:, k, :],
                                                start=(k == 0), stop=(k == KC - 1))
                    last.then_inc(den_product, 1)

                def key_value(b, j, t):
                    n = b * NT + j * TT + t
                    pe.wait_ge(k_ready, n + 1)
                    pe.wait_ge(v_ready, n + 1)
                    for g in range(KC):
                        at = (g % 2) * VW
                        last = nc.tensor.matmul(kv_psum[g // 2][:, at:at + VW], k_sb[t % 2][:, g * P:(g + 1) * P],
                                                v_sb[t % 2][:, g, :], start=(j == 0 and t == 0 and g % 2 == 0),
                                                stop=(j == JB - 1 and t == TT - 1), skip_group_check=True)
                    last.then_inc(kv_tile, 1)

                def turn_x(b, j, c):
                    if c == 0:
                        pe.wait_ge(xn_ready, b * NT + (j + 1) * TT)
                    wait(pe, h_full_ready, b * NC + j * KC + c - 1)
                    for t in range(TT):
                        last = nc.tensor.transpose(turn[c % 2][:, t * P:(t + 1) * P],
                                                   x_in[j][:, t, c * P:(c + 1) * P], ident)
                    last.then_inc(turned, 1)

                def times_wo(e, k):
                    if k == 0:
                        pe.wait_ge(kv_t_ready, e + 1)
                    else:
                        pe.wait_ge(m_read, KC * e + k)
                    nc.tensor.matmul(spread[:], kv_t[:, k * P:(k + 1) * P], weights["wo"][:, k, :],
                                     start=True, stop=True).then_inc(m_product, 1)

                def project_kv(b, e, j, t):
                    n = b * NT + j * TT + t
                    s = slice(t * P, (t + 1) * P)
                    if t > 0:
                        pe.wait_ge(k_ready, n)
                    elif e is not None:
                        pe.wait_ge(o_read, e * NT + j * TT + 1)
                    elif j > 0:
                        pe.wait_ge(q_ready, b * NC + j * KC - 1)
                    parts = [(weights["ones"][:], weights["bk"][:])]
                    for c in range(KC):
                        parts += [(h_hi[:, c, s], wk[0][:, c, :]), (h_hi[:, c, s], wk[1][:, c, :]),
                                  (h_lo[:, c, s], wk[0][:, c, :])]
                    split_matmul(nc, prod[0][:], parts, True, True).then_inc(k_product, 1)
                    if t > 0:
                        pe.wait_ge(v_ready, n)
                    elif e is not None:
                        pe.wait_ge(o_read, e * NT + j * TT + 2)
                    elif j > 0:
                        pe.wait_ge(q_ready, b * NC + j * KC)
                    parts = []
                    for c in range(KC):
                        parts += [(h_hi[:, c, s], wv[0][:, c, :]), (h_hi[:, c, s], wv[1][:, c, :]),
                                  (h_lo[:, c, s], wv[0][:, c, :])]
                    split_matmul(nc, prod[1][:], parts, True, True).then_inc(v_product, 1)

                def project_q(b, j, k):
                    n = b * NC + j * KC + k
                    s = slice(k * P, (k + 1) * P)
                    if k == 0:
                        pe.wait_ge(k_ready, b * NT + (j + 1) * TT)
                    elif k == 1:
                        pe.wait_ge(v_ready, b * NT + (j + 1) * TT)
                    else:
                        pe.wait_ge(q_ready, n - 1)
                    parts = []
                    for c in range(KC):
                        parts += [(wq[0][:, c, s], h_hi[:, c, :]), (wq[1][:, c, s], h_hi[:, c, :]),
                                  (wq[0][:, c, s], h_lo[:, c, :])]
                    split_matmul(nc, prod[k % 2][:], parts, True, True).then_inc(q_product, 1)

                def spread_recip(e, j, k):
                    n = e * NC + j * KC + k
                    if k == 0:
                        pe.wait_ge(recip_ready, 2 * (e * JB + j + 1))
                        pe.wait_ge(m_read, KC * (e + 1))
                    else:
                        pe.wait_ge(spread_read, n)
                    nc.tensor.matmul(spread[:], weights["sel"][:, k * P:(k + 1) * P], recip_rows[:],
                                     start=True, stop=True).then_inc(spread_ready, 1)

                def times_m(b, e, j, t):
                    n = e * NT + j * TT + t
                    s = slice(t * P, (t + 1) * P)
                    if t == 0:
                        pe.wait_ge(qn_ready, e * NC + (j + 1) * KC)
                        pe.wait_ge(m_ready, KC * (e + 1))
                    if t >= 2 or b is None:
                        pe.wait_ge(o_read, n + 1)
                    else:
                        pe.wait_ge(q_ready, b * NC + (j + 1) * KC - 1 + t)
                    parts = []
                    for k in range(KC):
                        parts += [(qn_hi[:, k, s], m_hi[:, k, :]), (qn_hi[:, k, s], m_lo[:, k, :]),
                                  (qn_lo[:, k, s], m_hi[:, k, :])]
                    split_matmul(nc, prod[t % 2][:], parts, True, True).then_inc(o_product, 1)

                for c in range(KC):
                    turn_x(0, 0, c)

                def emit(b, e, more):
                    if e is not None:
                        pe.wait_ge(kv_ready, KC * (e + 1))
                        if b is not None:
                            pe.wait_ge(h_full_ready, b * NC + KC)
                        for k in range(KC):
                            last = nc.tensor.transpose(turn[0][:, k * P:(k + 1) * P], kv_sb[:, k, :], ident)
                        last.then_inc(kv_turned, 1)
                    for j in range(JB):
                        next_in = b is not None and (j + 1 < JB or more)
                        if e is not None:
                            pe.wait_ge(heads_ready, KC * (e + 1))
                            denominators(e, j)
                        if b is not None:
                            pe.wait_ge(h_ready, b * NC + (j + 1) * KC)
                        for t in range(TT):
                            if b is not None:
                                project_kv(b, e, j, t)
                            if e is not None and j == 0:
                                times_wo(e, t)
                            if b is not None and t > 0:
                                key_value(b, j, t - 1)
                        for k in range(KC):
                            if e is not None:
                                spread_recip(e, j, k)
                            if b is not None:
                                project_q(b, j, k)
                                if k == 0:
                                    key_value(b, j, TT - 1)
                        for t in range(TT):
                            if next_in:
                                turn_x(*following(b, j), t)
                            if e is not None:
                                times_m(b, e, j, t)

                rounds(pe, emit)


def mlp(nc, const_sb, words, gu_scales, down_scales, shifts, x2_dram, mod_cols_dram, gate_rows_dram, out_blocks):
    ident = const_sb[:, C_ID:C_ID + P]
    GU = KC * 2 * P
    NB = BATCH * JB
    HALF_BITS = -1912602624
    FP4_SCALE = 16384.0

    with ExitStack() as ctx:
        def sb(name, shape, dt=F32):
            return ctx.enter_context(nc.sbuf_tensor(name, shape, dt))

        def bank(name):
            return ctx.enter_context(nc.psum_tensor(name, [P, 512], F32))

        def sem(name):
            return ctx.enter_context(nc.semaphore(name))

        gu_w = sb("gu_w", [P, FC, KC, 2, P], F32R)
        down_hi, down_lo = sb("down_hi", [P, FC, D], F32R), sb("down_lo", [P, FC, D], F32R)
        scale16 = sb("scale16", [P, 2 * FC * KC], F16)
        scale = sb("scale", [P, 2, FC, KC])
        down_scale = [sb(f"down_scale{i}", [P, D], F16) for i in range(2)]
        shift_sb = sb("shift_sb", [P, 1], I32)
        raw = [sb(f"raw{i}", [P, GU + D], I32) for i in range(2)]
        down_full = sb("down_full", [P, D])
        x_in = sb("x2_in", [P, TT, XW])
        x_res = sb("x2_res", [P, TT, XW])
        mod_now = sb("mod_now_b", [P, 4 * KC])
        gb_all = sb("gb_all", [P, D])
        xn = sb("xn", [P, TT, KC, NIB, WPG])
        h_full = [sb(f"h2_full{i}", [P, TOK]) for i in range(2)]
        h_hi = [sb(f"h2_hi{i}", [P, KC, TOK], F32R) for i in range(2)]
        h_lo = [sb(f"h2_lo{i}", [P, KC, TOK], F32R) for i in range(2)]
        acc = [[sb(f"acc{i}{u}", [P, TOK]) for u in range(2)] for i in range(2)]
        gate = [sb(f"gate{i}", [P, TOK]) for i in range(2)]
        hid_hi = [sb(f"hid_hi{i}", [P, TOK], F32R) for i in range(2)]
        hid_lo = [sb(f"hid_lo{i}", [P, TOK], F32R) for i in range(2)]
        y_sb = sb("y_sb", [P, TT, D])
        sum_sq = sb("sum_sq", [P, TT])
        work = [sb(f"rms_work{i}", [P, TT])[:] for i in range(3)]
        rms = sb("rms", [P, TT])
        o_sb = sb("o_sb", [P, TT, D])

        part = [bank(f"part{i}") for i in range(4)]
        y = [bank(f"y{t}") for t in range(TT)]

        words_loaded = [sem(f"words_loaded{i}") for i in range(2)]
        scales_loaded, scale_ready, masked = sem("scales_loaded"), sem("scale_ready"), sem("masked")
        gu_ready, down_full_ready, down_hi_ready, down_ready = (
            sem("gu_ready"), sem("down_full_ready"), sem("down_hi_ready"), sem("down_ready"))
        x_loaded, mod_loaded, res_loaded, gb_loaded, out_stored = (
            sem("x2_in_loaded"), sem("mod_b_loaded"), sem("res_loaded"), sem("gb_loaded"), sem("out_stored"))
        xn_ready, turned, h_full_ready, h_hi_ready, h_ready = (
            sem("xn2_ready"), sem("turned2"), sem("h2_full_ready"), sem("h2_hi_ready"), sem("h2_ready"))
        part_done, acc_first, acc_step, silu_ready, prod_ready, hid_hi_ready, hid_ready, hid_used = (
            sem("part_done"), sem("acc_first"), sem("acc_step"), sem("silu_ready"), sem("prod_ready"),
            sem("hid_hi_ready"), sem("hid_ready"), sem("hid_used"))
        squares_ready, y_read, y_scaled, y_gated, o_ready = (
            sem("squares_ready"), sem("y_read"), sem("y_scaled"), sem("y_gated"), sem("o_ready"))
        prep_steps, rms_steps = sem("prep_steps"), sem("rms_steps")

        def pairs(eng, emit, finish):
            emit(0, 0, False)
            emit(1, 1, False)
            with eng.Fori(1, BATCH - 1) as m:
                emit(m * JB, 0, False)
                emit(m * JB + 1, 1, False)
            emit(NB - 2, 0, False)
            emit(NB - 1, 1, True)
            finish()

        def slot(par, f):
            return (par * FC + f) % 2

        def batch_of(n, par):
            return (n - par) // JB if isinstance(n, int) else n_batch(n, par)

        LAG = 2
        NORM_AT = 0
        TURN_AT = 4
        SQUARE_AT, ROOT_AT, SCALE_AT, GATE_AT = LAG, LAG + 2, LAG + 4, LAG + 5

        with nc.Block() as block:
            @block.sync
            def _(sp):
                def load_in(n, batch):
                    wait(sp, xn_ready, n * TT)
                    sp.dma_start(x_in[:].rearrange("p t d -> p (t d)"),
                                 x2_dram[bass.ds(n, 1)].squeeze(0)).then_inc(x_loaded, 16)
                    wait(sp, h_full_ready, n * KC)
                    sp.dma_start(mod_now[:], mod_cols_dram[bass.ds(batch, 1)].squeeze(0)).then_inc(mod_loaded, 16)

                def load_res(n, batch):
                    wait(sp, o_ready, n * TT)
                    sp.dma_start(x_res[:].rearrange("p t d -> p (t d)"),
                                 x2_dram[bass.ds(n, 1)].squeeze(0)).then_inc(res_loaded, 16)
                    sp.dma_start(gb_all[:], gate_rows_dram[bass.ds(batch, 1), 1, :].squeeze(0).partition_broadcast(P)
                                 ).then_inc(gb_loaded, 16)

                def load_words(f):
                    wait(sp, gu_ready, f - 1)
                    wait(sp, down_full_ready, f - 1)
                    for s in range(NIB):
                        sp.dma_start(raw[f % 2][s * WPG:(s + 1) * WPG, :], words[f]).then_inc(words_loaded[f % 2], 16)
                    sp.dma_start(down_scale[f % 2][:], down_scales[f:f + 1, :].squeeze(0).partition_broadcast(P)
                                 ).then_inc(words_loaded[f % 2], 16)

                load_in(0, 0)
                sp.dma_start(shift_sb[:], shifts).then_inc(scales_loaded, 16)
                sp.dma_start(scale16[:], gu_scales).then_inc(scales_loaded, 16)
                for f in range(2):
                    load_words(f)

                for f in range(2, FC):
                    load_words(f)
                    if f == 3:
                        load_in(1, 0)

                def pair(m, last):
                    for par in range(JB):
                        if not last:
                            load_in((m + 1) * JB + par, m + 1)
                        load_res(m * JB + par, m)

                pair(0, False)
                with sp.Fori(1, BATCH - 1) as m:
                    pair(m, False)
                pair(BATCH - 1, True)
                sp.wait_ge(out_stored, 16 * NB)

            @block.gpsimd
            def _(pool):
                def expand(f):
                    pool.wait_ge(down_hi_ready, f + 1)
                    nc.gpsimd.tensor_tensor(down_lo[:, f, :], down_full[:], down_hi[:, f, :].bitcast(F32),
                                            ALU.subtract).then_inc(down_ready, 1)

                def finish_out(n, t):
                    if t == 0:
                        pool.wait_ge(gb_loaded, 16 * (n + 1))
                        pool.wait_ge(res_loaded, 16 * (n + 1))
                    pool.wait_ge(y_scaled, n * TT + t + 1)
                    nc.gpsimd.tensor_tensor(o_sb[:, t, :], o_sb[:, t, :], gb_all[:], ALU.mult).then_inc(y_gated, 1)
                    pool.wait_ge(y_gated, n * TT + t + 1)
                    nc.gpsimd.tensor_tensor(o_sb[:, t, :], o_sb[:, t, :], x_res[:, t, 0:D],
                                            ALU.add).then_inc(o_ready, 1)

                def store(n):
                    pool.wait_ge(o_ready, (n + 1) * TT)
                    pool.dma_start(out_blocks[bass.ds(n, 1)].squeeze(0),
                                   o_sb[:].rearrange("p t d -> p (t d)")).then_inc(out_stored, 16)

                def emit(n, par, last):
                    first = isinstance(n, int) and n == 0
                    if first:
                        expand(0)
                        expand(1)
                    for f in range(FC):
                        if first and f + 2 < FC:
                            expand(f + 2)
                        q = n * FC + f
                        s = slot(par, f)
                        pool.wait_ge(hid_hi_ready, q + 1)
                        nc.gpsimd.tensor_tensor(hid_lo[s][:], gate[s][:], hid_hi[s][:].bitcast(F32),
                                                ALU.subtract).then_inc(hid_ready, 1)
                        if GATE_AT <= f < GATE_AT + TT and not first:
                            finish_out(n - 1, f - GATE_AT)
                            if f == GATE_AT + TT - 1:
                                store(n - 1)

                def finish():
                    for t in range(TT):
                        finish_out(NB - 1, t)
                    store(NB - 1)

                pairs(pool, emit, finish)

            @block.scalar
            def _(act):
                def expand(f):
                    act.wait_ge(masked, f + 1)
                    half = raw[f % 2][:].bitcast(F16).rearrange("p (n two) -> p n two", two=2)[:, :, 1]
                    nc.scalar.activation(gu_w[:, f, :, :, :].rearrange("p g u n -> p (g u n)"), half[:, 0:GU],
                                         ACT.Copy, scale=FP4_SCALE).then_inc(gu_ready, 1)
                    act.wait_ge(down_full_ready, f + 1)
                    nc.scalar.activation(down_hi[:, f, :], down_full[:], ACT.Copy).then_inc(down_hi_ready, 1)

                def normalize(n, t):
                    if t == 0:
                        act.wait_ge(x_loaded, 16 * (n + 1))
                        wait(act, turned, n * KC)
                    nc.scalar.activation(xn[:, t].rearrange("p g s a -> p g a s"),
                                         x_in[:, t, 0:D].rearrange("p (g a s) -> p g a s", g=KC, s=NIB), ACT.Identity,
                                         bias=x_in[:, t, D + 1:D + 2], scale=x_in[:, t, D:D + 1]).then_inc(xn_ready, 1)

                def modulate(n, c):
                    act.wait_ge(turned, n * KC + c + 1)
                    act.wait_ge(mod_loaded, 16 * (n + 1))
                    wait(act, h_ready, n * KC + c - 1)
                    nc.scalar.activation(h_full[c % 2][:], part[c if first_turn[0] else 0][:], ACT.Identity,
                                         bias=mod_now[:, 2 * KC + c:2 * KC + c + 1],
                                         scale=mod_now[:, 3 * KC + c:3 * KC + c + 1]).then_inc(h_full_ready, 1)

                def take_y(n, t):
                    act.wait_ge(hid_used, (n * FC + FC - 1) * TT + t + 1)
                    nc.scalar.activation(y_sb[:, t, :], y[t][:], ACT.Copy).then_inc(y_read, 1)

                def squares(n, t):
                    act.wait_ge(y_read, n * TT + t + 1)
                    wait(act, squares_ready, n * TT + t)
                    act.wait_ge(down_ready, FC)
                    nc.scalar.activation(down_full[:], y_sb[:, t, :], ACT.Square,
                                         accum_out=sum_sq[:, t:t + 1]).then_inc(squares_ready, 1)

                def scale_y(n, t):
                    act.wait_ge(rms_steps, 12 * (n + 1))
                    wait(act, out_stored, 16 * n)
                    nc.scalar.activation(o_sb[:, t, :], y_sb[:, t, :], ACT.Copy,
                                         scale=rms[:, t:t + 1]).then_inc(y_scaled, 1)

                def hidden(q, s):
                    act.wait_ge(acc_step, 6 * q + 5)
                    wait(act, hid_ready, q - 1)
                    nc.scalar.activation(gate[s][:], acc[s][0][:], ACT.Silu).then_inc(silu_ready, 1)

                def hidden_hi(q, s):
                    act.wait_ge(prod_ready, q + 1)
                    wait(act, hid_used, (q - 1) * TT)
                    nc.scalar.activation(hid_hi[s][:], gate[s][:], ACT.Copy).then_inc(hid_hi_ready, 1)

                first_turn = [True]
                expand(0)
                for t in range(TT):
                    normalize(0, t)
                for c in range(KC):
                    modulate(0, c)
                first_turn[0] = False

                def emit(n, par, last):
                    first = isinstance(n, int) and n == 0
                    for f in range(FC):
                        q = n * FC + f
                        s = slot(par, f)
                        if f == LAG and not first:
                            take_y(n - 1, TT - 1)
                        if f > 0 or not first:
                            hidden(q - 1, 1 - s)
                        for u in range(2):
                            act.wait_ge(part_done, 8 * q + u + 1)
                            wait(act, prod_ready, q - 1)
                            if first and f == 0:
                                act.wait_ge(scale_ready, 1)
                            nc.scalar.activation(acc[s][u][:], part[u][:], ACT.Identity,
                                                 scale=scale[:, u, f, 0:1]).then_inc(acc_first, 1)
                        if first and f + 1 < FC:
                            expand(f + 1)
                        if not last and TURN_AT <= f < TURN_AT + KC:
                            modulate(n + 1, f - TURN_AT)
                        if f > 0 or not first:
                            hidden_hi(q - 1, 1 - s)
                        if not first:
                            if f == LAG - 1:
                                for t in range(TT - 1):
                                    take_y(n - 1, t)
                            if SQUARE_AT <= f < SQUARE_AT + 2:
                                for t in (2 * (f - SQUARE_AT), 2 * (f - SQUARE_AT) + 1):
                                    squares(n - 1, t)
                            if SCALE_AT <= f < SCALE_AT + 2:
                                for t in (2 * (f - SCALE_AT), 2 * (f - SCALE_AT) + 1):
                                    scale_y(n - 1, t)
                        if not last:
                            if NORM_AT <= f < NORM_AT + TT:
                                normalize(n + 1, f - NORM_AT)

                def finish():
                    q = NB * FC
                    hidden(q - 1, slot(1, FC - 1))
                    hidden_hi(q - 1, slot(1, FC - 1))
                    for t in range(TT):
                        take_y(NB - 1, t)
                        squares(NB - 1, t)
                    for t in range(TT):
                        scale_y(NB - 1, t)

                pairs(act, emit, finish)

            @block.vector
            def _(dve):
                prep = Steps(dve, prep_steps, 2 * FC)
                outs = Steps(dve, rms_steps, 12)

                def unpack(f):
                    dve.wait_ge(words_loaded[f % 2], 16 * (NIB + 1) * (f // 2 + 1))
                    r = raw[f % 2][:]
                    nc.vector.tensor_scalar(r, r, shift_sb[:, 0:1], 3, ALU.logical_shift_left,
                                            ALU.arith_shift_right).then_inc(prep_steps, 1)
                    dve.wait_ge(prep_steps, f + 1)
                    nc.vector.tensor_scalar(r, r, HALF_BITS, None, ALU.bitwise_and).then_inc(masked, 1)
                    dve.wait_ge(masked, f + 1)
                    wait(dve, down_ready, f)
                    half = r.bitcast(F16).rearrange("p (n two) -> p n two", two=2)[:, :, 1]
                    nc.vector.scalar_tensor_tensor(down_full[:], half[:, GU:GU + D], FP4_SCALE, down_scale[f % 2][:],
                                                   ALU.mult, ALU.mult).then_inc(down_full_ready, 1)

                def split(n, c, par):
                    dve.wait_ge(h_full_ready, n * KC + c + 1)
                    nc.vector.tensor_copy(h_hi[par][:, c, :], h_full[c % 2][:]).then_inc(h_hi_ready, 1)
                    dve.wait_ge(h_hi_ready, n * KC + c + 1)
                    nc.vector.tensor_tensor(h_lo[par][:, c, :], h_full[c % 2][:], h_hi[par][:, c, :].bitcast(F32),
                                            ALU.subtract).then_inc(h_ready, 1)

                def root(n, part):
                    if part == 0:
                        outs.start(n)
                        dve.wait_ge(squares_ready, (n + 1) * TT)
                        wait(dve, y_scaled, n * TT)
                        inverse_sqrt_guess(nc, outs, rms[:], work, sum_sq[:], 1.0 / D, RMS_EPS)
                    else:
                        inverse_sqrt_newton(nc, outs, rms[:], work)
                    if part == 3:
                        outs.end()

                dve.wait_ge(scales_loaded, 32)
                unpack(0)
                nc.vector.tensor_copy(scale[:].rearrange("p u f g -> p (u f g)"), scale16[:]).then_inc(scale_ready, 1)
                for c in range(KC):
                    split(0, c, 0)
                unpack(1)

                def product(q, s):
                    dve.wait_ge(silu_ready, q + 1)
                    dve.wait_ge(acc_step, 6 * q + 6)
                    nc.vector.tensor_tensor(gate[s][:], gate[s][:], acc[s][1][:], ALU.mult).then_inc(prod_ready, 1)

                def emit(n, par, last):
                    first = isinstance(n, int) and n == 0
                    for f in range(FC):
                        q = n * FC + f
                        s = slot(par, f)
                        if f == 0 and first:
                            dve.wait_ge(scale_ready, 1)
                        for g in range(1, KC):
                            for u in range(2):
                                dve.wait_ge(part_done, 8 * q + 2 * g + u + 1)
                                if g == 1:
                                    dve.wait_ge(acc_first, 2 * q + u + 1)
                                else:
                                    dve.wait_ge(acc_step, 6 * q + 2 * (g - 2) + u + 1)
                                nc.vector.scalar_tensor_tensor(acc[s][u][:], part[(2 * g + u) % 4][:],
                                                               scale[:, u, f, g:g + 1], acc[s][u][:],
                                                               ALU.mult, ALU.add).then_inc(acc_step, 1)
                            if g == 1 and not (first and f == 0):
                                product(q - 1, 1 - s)
                            if not first and ROOT_AT <= f < ROOT_AT + 2 and g >= 2:
                                root(n - 1, 2 * (f - ROOT_AT) + g - 2)
                        if first and f + 2 < FC:
                            unpack(f + 2)
                        if not last and TURN_AT <= f < TURN_AT + KC:
                            split(n + 1, f - TURN_AT, 1 - par)

                def finish():
                    product(NB * FC - 1, slot(1, FC - 1))
                    for part in range(4):
                        root(NB - 1, part)

                pairs(dve, emit, finish)

            @block.tensor
            def _(pe):
                owner = {}

                def claim(i):
                    if i in owner:
                        wait(pe, *owner[i])

                def transposes(n, c, i):
                    claim(i)
                    if c == 0:
                        pe.wait_ge(xn_ready, (n + 1) * TT)
                    for t in range(TT):
                        last = nc.tensor.transpose(part[i][:, t * P:(t + 1) * P],
                                                   xn[:, t, c].rearrange("p s a -> p (s a)"), ident)
                    last.then_inc(turned, 1)
                    owner[i] = (h_full_ready, n * KC + c + 1)

                def gate_up(q, f, par, g):
                    for u in range(2):
                        i = (2 * g + u) % 4
                        claim(i)
                        w = gu_w[:, f, g, u, :]
                        split_matmul(nc, part[i][:], [(w, h_hi[par][:, g, :]), (w, h_lo[par][:, g, :])],
                                     True, True).then_inc(part_done, 1)
                        owner[i] = (acc_first, 2 * q + u + 1) if g == 0 else (acc_step, 6 * q + 2 * (g - 1) + u + 1)

                def down(q, f, s, t):
                    if t == 0:
                        pe.wait_ge(hid_ready, q + 1)
                    ts = slice(t * P, (t + 1) * P)
                    split_matmul(nc, y[t][:], [(hid_hi[s][:, ts], down_hi[:, f, :]),
                                               (hid_hi[s][:, ts], down_lo[:, f, :]),
                                               (hid_lo[s][:, ts], down_hi[:, f, :])],
                                 f == 0, f == FC - 1).then_inc(hid_used, 1)

                for c in range(KC):
                    transposes(0, c, c)

                def emit(n, par, last):
                    first = isinstance(n, int) and n == 0
                    if not first:
                        for i in range(4):
                            owner[i] = (acc_step, 6 * n * FC)
                        owner[0] = (acc_step, 6 * n * FC)
                    pe.wait_ge(h_ready, (n + 1) * KC)
                    for f in range(FC):
                        q = n * FC + f
                        if first:
                            pe.wait_ge(gu_ready, f + 1)
                        for i in range(KC):
                            gate_up(q, f, par, i)
                            if f >= LAG:
                                if f == LAG:
                                    wait(pe, y_read, (n - 1) * TT + i + 1)
                                if first:
                                    pe.wait_ge(down_ready, f - LAG + 1)
                                down(q - LAG, f - LAG, slot(par, f - LAG), i)
                            elif not first:
                                down(q - LAG, f - LAG + FC, slot(1 - par, f - LAG + FC), i)
                            if i == 0 and not last and TURN_AT <= f < TURN_AT + KC:
                                transposes(n + 1, f - TURN_AT, 0)

                def finish():
                    for f in range(FC - LAG, FC):
                        for t in range(TT):
                            down((NB - 1) * FC + f, f, slot(1, f), t)

                pairs(pe, emit, finish)


def kernel(**inputs):
    import numpy as np
    import concourse.bacc as bacc
    from concourse.bass_utils import run_bass_kernel_spmd

    a = {name: np.asarray(value) for name, value in inputs.items()}
    order = np.arange(P).reshape(WPG, NIB).T.reshape(-1)

    consts = np.zeros((P, C_END), np.float32)
    consts[:, C_ID:C_ID + P] = np.eye(P)
    head = np.arange(P) // DK
    consts[:, C_MASK:C_MASK + P] = head[:, None] == head[None, :]
    for k in range(KC):
        one = (k * (P // DK) + head)[:, None] == np.arange(HEADS)[None, :]
        consts[:, C_HEAD + k * HEADS:C_HEAD + (k + 1) * HEADS] = one
        for row in (0, LO_ROW):
            consts[row:row + HEADS, C_SEL + k * P:C_SEL + (k + 1) * P] = one.T
    shifts = (28 - 4 * (np.arange(P) // WPG)).astype(np.int32).reshape(P, 1)

    wmod = a["L0_wmod"].reshape(D, 6, KC, P).copy()
    for section in (3, 4):
        wmod[:, section] = wmod[:, section][:, :, order]
    gu = a["L0_ffn_gate_up_packed"].reshape(2, FC, P, KC, WPG)[:, :, order]
    gu = gu.transpose(1, 4, 3, 0, 2).reshape(FC, WPG, KC * 2 * P)
    down = a["L0_ffn_down_packed"].reshape(D, FC, WPG).transpose(1, 2, 0)
    gu_scales = a["L0_ffn_gate_up_scales"].reshape(KC, 2, FC, P)[:, :, :, order].transpose(3, 1, 2, 0)

    arrays = {
        "x": a["L0_attn_x"].reshape(BATCH * SEQ, D),
        "wq_t": a["L0_attn_wq"].T, "wk_t": a["L0_attn_wk"].T, "wv_t": a["L0_attn_wv"].T, "wo_t": a["L0_attn_wo"].T,
        "bq": a["L0_attn_bq"].reshape(KC, P).T, "bk": a["L0_attn_bk"].reshape(1, D),
        "bv": a["L0_attn_bv"], "bo": a["L0_attn_bo"],
        "gu_down_words": np.concatenate([gu, down], axis=2),
        "gu_scales": gu_scales.reshape(P, 2 * FC * KC),
        "down_scales": a["L0_ffn_down_scales"],
        "c_t": a["L0_c"].T.reshape(KC, P, BATCH).transpose(1, 0, 2),
        "wmod": wmod.reshape(D, 6 * D),
        "consts": consts, "shifts": shifts,
    }
    nc = bacc.Bacc("TRN2", target_bir_lowering=False, num_devices=1)
    feed, aps = {}, {}
    for name, value in arrays.items():
        feed[f"in_{name}"] = np.ascontiguousarray(value)
        aps[name] = nc.dram_tensor(f"in_{name}", value.shape, mybir.dt.from_np(value.dtype), kind="ExternalInput").ap()
    out = nc.dram_tensor("out", (BATCH * SEQ, D), F32, kind="ExternalOutput").ap()
    adaln_block(nc, **aps, out=out)
    result = run_bass_kernel_spmd(nc, [feed], core_ids=[0])
    return result.results[0]["out"].reshape(BATCH, SEQ, D)
```

```python
from contextlib import ExitStack

import concourse.bass as bass
from concourse import mybir

F32 = mybir.dt.float32
F32R = mybir.dt.float32r
F16 = mybir.dt.float16
I32 = mybir.dt.int32
ALU = mybir.AluOpType
ACT = mybir.ActivationFunctionType

P = 128
BATCH = 4
SEQ = 1024
D = 512
HEADS = 16
DK = D // HEADS
KC = D // P
TOK = 512
TT = TOK // P
JB = SEQ // TOK
INNER = 1408
FC = INNER // P
NIB = 8
WPG = P // NIB
XW = D + 2
LN_EPS = 1e-5
RMS_EPS = 1e-6
DEN_EPS = 1e-8
QUAD = P // 4
C_ID, C_MASK, C_HEAD, C_SEL = 0, P, 2 * P, 2 * P + KC * QUAD
C_PART = C_SEL + D
C_QUAD = C_PART + 2
C_ROW = C_QUAD + TT
C_END = C_ROW + BATCH
LO_ROW = 32


def wait(eng, sem, value):
    if isinstance(value, int) and value <= 0:
        return
    eng.wait_ge(sem, value)


class Steps:

    def __init__(self, eng, sem, per_round):
        self.eng, self.sem, self.per_round = eng, sem, per_round

    def start(self, rnd):
        self.base, self.n = rnd * self.per_round, 0

    def mark(self, ins):
        ins.then_inc(self.sem, 1)
        self.n += 1
        return self.base + self.n

    def link(self, ins):
        self.eng.wait_ge(self.sem, self.mark(ins))

    def end(self):
        assert self.n == self.per_round, self.n


def inverse_sqrt_guess(nc, steps, out, work, src, scale, eps):
    v, a, h = work
    steps.link(nc.vector.tensor_scalar(v, src, scale, eps, ALU.mult, ALU.add))
    nc.vector.tensor_scalar(h, v, -0.5, None, ALU.mult)
    steps.link(nc.vector.tensor_scalar(a.bitcast(I32), v.bitcast(I32), 1, None, ALU.arith_shift_right))
    steps.link(nc.vector.tensor_scalar(out.bitcast(I32), a.bitcast(I32), -1.0, float(0x5F3759DF), ALU.mult, ALU.add))


def inverse_sqrt_newton(nc, steps, out, work):
    _, a, h = work
    steps.link(nc.vector.tensor_tensor(a, out, out, ALU.mult))
    steps.link(nc.vector.tensor_tensor(a, a, h, ALU.mult))
    steps.link(nc.vector.scalar_tensor_tensor(out, a, 1.5, out, ALU.add, ALU.mult))


def inverse_sqrt(nc, steps, out, work, src, scale, eps):
    inverse_sqrt_guess(nc, steps, out, work, src, scale, eps)
    for _ in range(3):
        inverse_sqrt_newton(nc, steps, out, work)


def split_matmul(nc, out, parts, start_first, stop_last):
    for i, (stationary, moving) in enumerate(parts):
        last = nc.tensor.matmul(out, stationary, moving, start=start_first and i == 0,
                                stop=stop_last and i == len(parts) - 1)
    return last


def adaln_block(nc, x, wq_t, wk_t, wv_t, wo_t, bq, bk, bv, bo, gu_down_words, gu_scales, down_scales,
                c_t, wmod, consts, shifts, out):
    mod_cols_dram = nc.dram_tensor("mod_cols", (BATCH, P, 4 * KC), F32).ap()
    gate_rows_dram = nc.dram_tensor("gate_rows", (BATCH, 2, D), F32).ap()
    x2_dram = nc.dram_tensor("x_after_attention", (BATCH * JB, P, TT * XW), F32).ap()
    x_blocks = x.rearrange("(n p t) d -> n p (t d)", p=P, t=TT)
    out_blocks = out.rearrange("(n p t) d -> n p (t d)", p=P, t=TT)

    with ExitStack() as ctx:
        const_sb = ctx.enter_context(nc.sbuf_tensor("const_sb", [P, C_END], F32))
        banks = [ctx.enter_context(nc.psum_tensor(f"bank{i}", [P, 512], F32)) for i in range(8)]
        with ExitStack() as attention_memory:
            att = attention(nc, ctx, attention_memory, banks, const_sb, x_blocks, x2_dram, mod_cols_dram,
                            gate_rows_dram, wq_t, wk_t, wv_t, wo_t, bq, bk, bv, bo, c_t, wmod, consts)
        ff = mlp(nc, ctx, att, banks, const_sb, gu_down_words, gu_scales, down_scales, shifts, x2_dram,
                 mod_cols_dram, gate_rows_dram, out_blocks)

        with nc.Block() as block:
            @block.sync
            def _(sp):
                then = ff["sync"](sp)
                att["sync"](sp, then)
                then["blocks"]()

            @block.gpsimd
            def _(pool):
                then = ff["gpsimd"](pool)
                att["gpsimd"](pool, then)
                then["blocks"]()

            @block.scalar
            def _(act):
                then = ff["scalar"](act)
                att["scalar"](act, then)
                then["blocks"]()

            @block.vector
            def _(dve):
                then = ff["vector"](dve)
                att["vector"](dve, then)
                then["blocks"]()

            @block.tensor
            def _(pe):
                then = ff["tensor"](pe)
                att["tensor"](pe, then)
                then["blocks"]()


def attention(nc, ctx, memory, banks, const_sb, x_blocks, x2_dram, mod_cols_dram, gate_rows_dram,
              wq_t, wk_t, wv_t, wo_t, bq, bk, bv, bo, c_t, wmod, consts):
    ident = const_sb[:, C_ID:C_ID + P]
    mask = const_sb[:, C_MASK:C_MASK + P]
    head_mask = const_sb[:, C_HEAD:C_SEL].rearrange("p (k h) -> p k h", h=QUAD)
    VW = DK + 1
    HPG = P // DK

    def sb(name, shape, dt=F32):
        return memory.enter_context(nc.sbuf_tensor(name, shape, dt))

    def sem(name):
        return ctx.enter_context(nc.semaphore(name))

    weights = {n: (sb(f"{n}_hi", [P, KC, D], F32R), sb(f"{n}_lo", [P, KC, D], F32R)) for n in ("wq", "wk", "wv")}
    wq, wk, wv = weights["wq"], weights["wk"], weights["wv"]
    bq_sb = sb("bq_sb", [P, KC])
    bq_neg = sb("bq_neg", [P, KC])
    bk_rows = sb("bk_rows", [LO_ROW + 1, D], F32R)
    ones_rows = sb("ones_rows", [LO_ROW + 1, P], F32R)
    x_in = [sb(f"x_in{j}", [P, TT, D]) for j in range(JB)]
    rstd = sb("rstd", [P, TT])
    shift = sb("shift", [P, TT])
    mod_now = sb("mod_now", [P, 4 * KC])
    h_full = [sb(f"h_full{i}", [P, TOK]) for i in range(2)]
    h_hi, h_lo = sb("h_hi", [P, KC, TOK], F32R), sb("h_lo", [P, KC, TOK], F32R)
    k_exp = [sb(f"k_exp{i}", [P, D]) for i in range(2)]
    k_sb = [sb(f"k_sb{i}", [P, D]) for i in range(2)]
    v_sb = [sb(f"v_sb{i}", [P, HEADS, VW]) for i in range(2)]
    q_exp = [sb(f"q_exp{i}", [P, TOK]) for i in range(2)]

    c_sb = sb("c_sb", [P, KC, BATCH])
    silu_c = sb("silu_c", [P, KC, QUAD])
    mod_cols = sb("mod_cols_sb", [P, BATCH, 4 * KC])
    bk_raw = sb("bk_raw", [1, D])

    stats = sb("stats", [P, TT, 6])
    moments = sb("moments", [P, 3, TT])
    work = [sb(f"rsqrt_work{i}", [P, TT])[:] for i in range(3)]
    credit = sb("credit", [P, 5])
    k_sum = sb("k_sum", [P, KC])
    k_sum_heads = sb("k_sum_heads", [P, KC, QUAD])
    recip_hi = sb("recip_hi", [P, P], F32R)
    recip_rows = sb("recip_rows", [P, P], F32R)
    wo_sb = sb("wo_sb", [P, KC, D])
    bv_all = sb("bv_all", [P, D])
    bo_all = sb("bo_all", [P, D])
    head_rows = sb("head_rows", [P, TT, D], F32R)
    with ExitStack() as start_memory:
        def start_sb(name, shape):
            return start_memory.enter_context(nc.sbuf_tensor(name, shape, F32))

        raw = [start_sb(f"{n}_raw", [P, KC, D]) for n in ("wk", "wv", "wq")]
        wmod_sb = start_sb("wmod_sb", [P, KC, 6 * D])
        def rows_on(tensor):
            return tensor[:, 0:2, :].rearrange("p two d -> p (two d)")

        mod_rows = [start_sb("mod_rows0", [P, 2 * D])[:], rows_on(raw[1])]
        gate_rows, gate_raw, rows_sign = (rows[0:BATCH, :] for rows in (rows_on(raw[2]), mod_rows[1], mod_rows[0]))
    q_sb = [sb(f"q_sb{j}", [P, KC, TOK]) for j in range(JB)]
    m_hi, m_lo = sb("m_hi", [P, KC, D], F32R), sb("m_lo", [P, KC, D], F32R)
    qn_hi, qn_lo = sb("qn_hi", [P, KC, TOK], F32R), sb("qn_lo", [P, KC, TOK], F32R)
    full = [sb(f"full{i}", [P, D]) for i in range(2)]
    ga_all = sb("ga_all", [P, D])
    ga_bo = sb("ga_bo", [P, D])
    kv_sb = sb("kv_sb", [P, KC, P])
    kv_t = sb("kv_t", [P, D])
    recip = sb("recip", [P, P])
    x2 = [sb(f"x2_{j}", [P, TT, XW]) for j in range(JB)]

    turn = banks[0:2]
    prod = banks[2:4]
    kv_heads = banks[4][:, 0:KC * VW].rearrange("p (g n) -> p g n", g=KC)
    den = banks[6]
    spread = (banks[7], banks[5])
    row_banks = (den, banks[7])

    c_loaded, consts_loaded, bk_loaded, bq_loaded, late_loaded = (
        sem("c_loaded"), sem("consts_loaded"), sem("bk_loaded"), sem("bq_loaded"), sem("late_loaded"))
    raw_loaded = [sem(f"raw_loaded{i}") for i in range(3)]
    wmod_loaded = [sem(f"wmod_loaded{i}") for i in range(2)]
    silu_done, rows_done, rows_ready, cols_done, cols_ready, gates_ready, mod_saved = (
        sem("silu_done"), sem("rows_done"), sem("rows_ready"), sem("cols_done"), sem("cols_ready"),
        sem("gates_ready"), sem("mod_saved"))
    gates_summed, last_hi_ready = sem("gates_summed"), sem("last_hi_ready")
    zeroed, small_ready, hi_ready, lo_ready, gate_steps = (
        sem("zeroed"), sem("small_ready"), sem("hi_ready"), sem("lo_ready"), sem("gate_steps"))
    x_loaded = [sem(f"x_loaded{j}") for j in range(JB)]
    mod_loaded = sem("mod_loaded")
    ga_loaded = sem("ga_loaded")
    x2_loaded = [sem(f"x2_loaded{j}") for j in range(JB)]
    x2_stored = [sem(f"x2_stored{j}") for j in range(JB)]
    norm_ready, xn_ready, turned, h_full_ready, h_ready = (
        sem("norm_ready"), sem("xn_ready"), sem("turned"), sem("h_full_ready"), sem("h_ready"))
    k_product, v_product, q_product, m_product, o_product = (
        sem("k_product"), sem("v_product"), sem("q_product"), sem("m_product"), sem("o_product"))
    k_exp_ready, k_ready, v_ready, q_exp_ready, q_ready = (
        sem("k_exp_ready"), sem("k_ready"), sem("v_ready"), sem("q_exp_ready"), sem("q_ready"))
    k_relu_ready, q_relu_ready = sem("k_relu_ready"), sem("q_relu_ready")
    kv_tile, heads_ready, kv_ready, kv_turned, kv_t_ready = (
        sem("kv_tile"), sem("heads_ready"), sem("kv_ready"), sem("kv_turned"), sem("kv_t_ready"))
    m_read, m_ready = sem("m_read"), sem("m_ready")
    den_product, recip_ready, spread_ready, spread_read, qn_ready = (
        sem("den_product"), sem("recip_ready"), sem("spread_ready"), sem("spread_read"), sem("qn_ready"))
    ga_bo_ready, x2_biased, o_read, x2_ready = sem("ga_bo_ready"), sem("x2_biased"), sem("o_read"), sem("x2_ready")
    ones_set, head_rows_set = sem("ones_set"), sem("head_rows_set")
    norm_steps, kv_steps, split_steps, out_steps = (
        sem("norm_steps"), sem("kv_steps"), sem("split_steps"), sem("out_steps"))

    PAIRS = ((0, 1), (3, 4), (2, 5))
    NT = JB * TT
    NC = JB * KC
    NORM_TILES = ((0,), (1, 2), (3,), ())

    def rounds(eng, emit):
        emit(0, None, True)
        with eng.Fori(1, BATCH - 1) as b:
            emit(b, b - 1, True)
        emit(BATCH - 1, BATCH - 2, False)
        emit(None, BATCH - 1, False)

    def following(b, j):
        return (b, j + 1) if j + 1 < JB else (b + 1, 0)

    def store(eng, e, j):
        eng.wait_ge(x2_ready, e * JB + j + 1)
        eng.dma_start(x2_dram[bass.ds(e * JB + j, 1)].squeeze(0),
                      x2[j][:].rearrange("p t d -> p (t d)")).then_inc(x2_stored[j], 16)

    def sync(sp, then):
        def load_x(b, j):
            wait(sp, turned, (b - 1) * NC + (j + 1) * KC)
            sp.dma_start(x_in[j][:].rearrange("p t d -> p (t d)"),
                         x_blocks[bass.ds(b * JB + j, 1)].squeeze(0)).then_inc(x_loaded[j], 16)

        def load_x2(e, j):
            sp.wait_ge(x2_stored[j], 16 * (e + 1))
            sp.dma_start(x2[j][:, :, 0:D], x_blocks[bass.ds(e * JB + j, 1)].squeeze(0)
                         .rearrange("p (t d) -> p t d", t=TT)).then_inc(x2_loaded[j], 16)

        def load_batch(b):
            load_x(b, 0)
            wait(sp, h_full_ready, b * NC)
            sp.dma_start(mod_now[:], mod_cols_dram[bass.ds(b, 1)].squeeze(0)).then_inc(mod_loaded, 16)
            load_x(b, 1)

        def load_leaving(e, last=False):
            load_x2(e, 0)
            sp.wait_ge(q_ready, (e + 1) * NC)
            sp.wait_ge(ga_bo_ready, e + 1)
            sp.dma_start(ga_all[:], gate_rows_dram[bass.ds(e, 1), 0, :].squeeze(0).partition_broadcast(P)
                         ).then_inc(ga_loaded, 16)
            if last:
                then["start"]()
            load_x2(e, 1)
            if last:
                then["load_second"]()

        def load_wmod(part, sections):
            for k in range(KC):
                s = slice(sections[0] * D, (sections[1] + 1) * D)
                sp.dma_start(wmod_sb[:, k, s], wmod[k * P:(k + 1) * P, s]).then_inc(wmod_loaded[part], 16)

        sp.dma_start(c_sb[:], c_t).then_inc(c_loaded, 16)
        load_x(0, 0)
        load_wmod(0, (0, 1))
        for i, w in enumerate((wk_t, wv_t, wq_t)):
            sp.dma_start(raw[i][:], w.rearrange("(k p) n -> p k n", p=P)).then_inc(raw_loaded[i], 16)
        load_x(0, 1)
        load_wmod(1, (2, 5))
        sp.wait_ge(cols_ready, 8)
        for b in range(BATCH):
            sp.dma_start(mod_cols_dram[b], mod_cols[:, b, :]).then_inc(mod_saved, 16)
        sp.wait_ge(gates_ready, 1)
        sp.dma_start(gate_rows_dram.rearrange("b two d -> b (two d)"), gate_rows).then_inc(mod_saved, 16)
        sp.wait_ge(mod_saved, 16 * (BATCH + 1))
        with sp.Fori(1, BATCH) as b:
            load_batch(b)
            load_leaving(b - 1)
        load_leaving(BATCH - 1, last=True)
        for j in range(JB):
            store(sp, BATCH - 1, j)

    def gpsimd(pool, then):
        for j in range(JB):
            nc.gpsimd.memset(credit[:, j:j + 1], 0.0).then_inc(x2_stored[j], 16)
        nc.gpsimd.memset(credit[:, 2:3], 0.0).then_inc(ga_bo_ready, 1)
        nc.gpsimd.memset(credit[:, 3:4], 0.0).then_inc(x2_biased, 1)
        nc.gpsimd.memset(credit[:, 4:5], 0.0).then_inc(o_read, 2)
        for i in range(2):
            nc.gpsimd.memset(v_sb[i][:, :, DK:VW], 1.0).then_inc(ones_set, 1)

        pool.wait_ge(late_loaded, 48)

        def emit(b, e, more):
            if e is None:
                return
            pool.wait_ge(ga_loaded, 16 * (e + 1))
            pool.wait_ge(x2_biased, JB * e + 1)
            nc.gpsimd.tensor_tensor(ga_bo[:], ga_all[:], bo_all[:], ALU.mult).then_inc(ga_bo_ready, 1)
            pool.wait_ge(ga_bo_ready, e + 2)
            for j in range(JB):
                pool.wait_ge(x2_loaded[j], 16 * (e + 1))
                for t in range(TT):
                    last = nc.gpsimd.tensor_tensor(x2[j][:, t, 0:D], x2[j][:, t, 0:D], ga_bo[:], ALU.add)
                last.then_inc(x2_biased, 1)

        rounds(pool, emit)

    def scalar(act, then):
        def normalize(b, j, t):
            act.wait_ge(norm_ready, b * JB + j + 1)
            nc.scalar.activation(x_in[j][:, t, :], x_in[j][:, t, :], ACT.Identity,
                                 bias=shift[:, t:t + 1], scale=rstd[:, t:t + 1]).then_inc(xn_ready, 1)

        def modulate(b, j, c):
            n = b * NC + j * KC + c
            if j == 0 and c == 0:
                if isinstance(b, int) and b == 0:
                    act.wait_ge(cols_ready, 4)
                else:
                    act.wait_ge(mod_loaded, 16 * b)
            act.wait_ge(turned, n + 1)
            wait(act, h_ready, n - 1)
            nc.scalar.activation(h_full[c % 2][:], turn[c % 2][:], ACT.Identity,
                                 bias=mod_now[:, c:c + 1], scale=mod_now[:, KC + c:KC + c + 1]
                                 ).then_inc(h_full_ready, 1)

        def take_kv(b, j, t):
            n = b * NT + j * TT + t
            act.wait_ge(k_product, n + 1)
            wait(act, k_ready, n - 1)
            nc.scalar.activation(k_exp[t % 2][:], prod[0][:], ACT.Relu, scale=-1.0).then_inc(k_relu_ready, 1)
            act.wait_ge(k_relu_ready, n + 1)
            nc.scalar.activation(k_exp[t % 2][:], k_exp[t % 2][:], ACT.Exp, scale=-1.0
                                 ).then_inc(k_exp_ready, 1)
            act.wait_ge(v_product, n + 1)
            wait(act, kv_tile, n - 1)
            nc.scalar.activation(v_sb[t % 2][:, :, 0:DK], prod[1][:].rearrange("p (h n) -> p h n", h=HEADS),
                                 ACT.Copy).then_inc(v_ready, 1)

        def take_q(b, e, j, k):
            n = b * NC + j * KC + k
            act.wait_ge(q_product, n + 1)
            wait(act, q_ready, n - 1)
            nc.scalar.activation(q_exp[k % 2][:], prod[k % 2][:], ACT.Relu, scale=-1.0,
                                 bias=bq_neg[:, k:k + 1]).then_inc(q_relu_ready, 1)
            act.wait_ge(q_relu_ready, 2 * n + 1)
            nc.scalar.activation(q_exp[k % 2][:], q_exp[k % 2][:], ACT.Exp, scale=-1.0
                                 ).then_inc(q_exp_ready, 1)
            if e is not None:
                act.wait_ge(spread_read, e * NC + j * KC + k + 1)
            elif j == 1 and k == 0:
                act.wait_ge(gates_ready, 1)
            nc.scalar.activation(q_sb[j][:, k, :], prod[k % 2][:], ACT.Relu,
                                 bias=bq_sb[:, k:k + 1]).then_inc(q_relu_ready, 1)

        def split_weights(i, name):
            act.wait_ge(raw_loaded[i], 16)
            nc.scalar.activation(weights[name][0][:], raw[i][:], ACT.Copy).then_inc(hi_ready, 1)

        act.dma_start(const_sb[:], consts).then_inc(consts_loaded, 16)
        act.dma_start(bk_raw[:], bk).then_inc(bk_loaded, 16)
        act.dma_start(bq_sb[:], bq).then_inc(bq_loaded, 16)
        act.wait_ge(c_loaded, 16)
        act.wait_ge(zeroed, 1)
        nc.scalar.activation(silu_c[:, :, 0:BATCH], c_sb[:], ACT.Silu).then_inc(silu_done, 1)
        act.wait_ge(bk_loaded, 16)
        act.wait_ge(zeroed, 1)
        nc.scalar.activation(bk_rows[0:1, :], bk_raw[:], ACT.Copy).then_inc(small_ready, 1)
        act.wait_ge(consts_loaded, 16)
        for r in (0, LO_ROW):
            nc.scalar.activation(ones_rows[r:r + 1, :], const_sb[r:r + 1, C_ID:C_ID + P],
                                 ACT.Identity, bias=const_sb[r:r + 1, C_MASK + r:C_MASK + r + 1],
                                 scale=0.0).then_inc(small_ready, 1)
        act.wait_ge(bq_loaded, 16)
        nc.scalar.activation(bq_neg[:], bq_sb[:], ACT.Copy, scale=-1.0
                             ).then_inc(small_ready, 1)
        for t in range(TT):
            normalize(0, 0, t)
        act.dma_start(bv_all[:], bv.partition_broadcast(P)).then_inc(late_loaded, 16)
        act.dma_start(wo_sb[:], wo_t.rearrange("(k p) n -> p k n", p=P)).then_inc(late_loaded, 16)
        act.dma_start(bo_all[:], bo.partition_broadcast(P)).then_inc(late_loaded, 16)
        split_weights(0, "wk")
        for c in range(KC):
            modulate(0, 0, c)
        split_weights(1, "wv")
        act.wait_ge(small_ready, 4)
        act.wait_ge(ones_set, 2)

        def emit(b, e, more):
            for j in range(JB):
                next_in = b is not None and (j + 1 < JB or more)
                if b is not None:
                    for t in range(TT):
                        take_kv(b, j, t)
                        if e is None and j == 0 and t == 1:
                            split_weights(2, "wq")
                        if e is None and j == 1:
                            nc.scalar.activation(head_rows[:, t, :], const_sb[:, C_SEL:C_SEL + D], ACT.Copy,
                                                 scale=const_sb[:, C_QUAD + t:C_QUAD + t + 1]).then_inc(head_rows_set, 1)
                    for k in range(KC):
                        take_q(b, e, j, k)
                        if next_in:
                            for t in NORM_TILES[k]:
                                normalize(*following(b, j), t)
                if next_in:
                    for c in range(KC):
                        modulate(*following(b, j), c)
                if b is None:
                    if j == 0:
                        for k in range(KC):
                            act.wait_ge(m_read, KC * e + k + 1)
                            nc.scalar.activation(m_hi[:, k, :], full[k % 2][:], ACT.Copy).then_inc(last_hi_ready, 1)
                    for k in range(KC):
                        act.wait_ge(spread_read, e * NC + j * KC + k + 1)
                        nc.scalar.activation(qn_hi[:, k, :], full[k % 2][:], ACT.Copy).then_inc(last_hi_ready, 1)
                    if j == 0:
                        then["start"]()
                elif e is not None:
                    store(act, e, j)

        rounds(act, emit)

    def vector(dve, then):
        norms = Steps(dve, norm_steps, 16)
        kvs = Steps(dve, kv_steps, 1 + KC)
        splits = Steps(dve, split_steps, KC)
        outs = Steps(dve, out_steps, KC + JB * (4 + KC + TT + 15))

        def normalization(steps, rstd_out, shift_out):
            both, apart, spread_sq = moments[:, 0, :], moments[:, 1, :], moments[:, 2, :]
            nc.vector.tensor_tensor(both, stats[:, :, 1], stats[:, :, 4], ALU.add)
            nc.vector.tensor_tensor(apart, stats[:, :, 1], stats[:, :, 4], ALU.subtract)
            steps.link(nc.vector.tensor_tensor(spread_sq, stats[:, :, 2], stats[:, :, 5], ALU.add))
            steps.link(nc.vector.tensor_tensor(apart, apart, apart, ALU.mult))
            steps.link(nc.vector.scalar_tensor_tensor(spread_sq, apart, D / 4, spread_sq, ALU.mult, ALU.add))
            inverse_sqrt(nc, steps, rstd_out, work, spread_sq, 1.0 / D, LN_EPS)
            return nc.vector.scalar_tensor_tensor(shift_out, both, -0.5, rstd_out, ALU.mult, ALU.mult)

        def statistics(b, j, t):
            if t == 0:
                dve.wait_ge(x_loaded[j], 16 * (b + 1))
                norms.start(b * JB + j)
            ins = nc.vector.bn_stats(stats[:, t, :], x_in[j][:, t, :])
            if t == TT - 1:
                norms.mark(ins)

        def norm_in(b, j):
            dve.wait_ge(norm_steps, norms.base + 1)
            normalization(norms, rstd[:], shift[:]).then_inc(norm_ready, 1)
            norms.end()

        def split_h(b, j, c):
            if c == 0:
                splits.start(b * JB + j)
            dve.wait_ge(h_full_ready, b * NC + j * KC + c + 1)
            splits.link(nc.vector.tensor_copy(h_hi[:, c, :], h_full[c % 2][:]))
            nc.vector.tensor_tensor(h_lo[:, c, :], h_full[c % 2][:], h_hi[:, c, :].bitcast(F32),
                                    ALU.subtract).then_inc(h_ready, 1)

        def finish_kv(b):
            dve.wait_ge(kv_tile, NT * (b + 1))
            kvs.start(b)
            kvs.link(nc.vector.tensor_copy(k_sum[:], kv_heads[:, :, DK]))
            for k in range(KC):
                nc.vector.tensor_scalar(k_sum_heads[:, k, :], head_mask[:, k, :], k_sum[:, k:k + 1], None,
                                        ALU.mult).then_inc(heads_ready, 1)
            marks = []
            for k in range(KC):
                marks.append(kvs.mark(nc.vector.scalar_tensor_tensor(
                    kv_sb[:, k, :].rearrange("p (h n) -> p h n", h=HPG),
                    bv_all[:, k * P:(k + 1) * P].rearrange("p (h n) -> p h n", h=HPG), k_sum[:, k:k + 1],
                    kv_heads[:, k:k + 1, 0:DK].to_broadcast([P, HPG, DK]), ALU.mult, ALU.add)))
            for k in range(KC):
                dve.wait_ge(kv_steps, marks[k])
                nc.vector.tensor_tensor(kv_sb[:, k, :], kv_sb[:, k, :], mask, ALU.mult).then_inc(kv_ready, 1)
            kvs.end()

        def take_k(b, j, t):
            n = b * NT + j * TT + t
            dve.wait_ge(k_exp_ready, n + 1)
            wait(dve, kv_tile, n - 1)
            nc.vector.scalar_tensor_tensor(k_sb[t % 2][:], prod[0][:], 0.0, k_exp[t % 2][:],
                                           ALU.max, ALU.add).then_inc(k_ready, 1)

        def take_q(b, j, k):
            n = b * NC + j * KC + k
            dve.wait_ge(q_exp_ready, n + 1)
            dve.wait_ge(q_relu_ready, 2 * n + 2)
            nc.vector.tensor_tensor(q_sb[j][:, k, :], q_exp[k % 2][:], q_sb[j][:, k, :],
                                    ALU.add).then_inc(q_ready, 1)

        def reciprocal(e, j):
            n = e * JB + j
            dve.wait_ge(den_product, n + 1)
            outs.link(nc.vector.tensor_scalar(recip[:], den[:, 0:P], DEN_EPS, None, ALU.add))
            outs.link(nc.vector.reciprocal(recip[:], recip[:]))
            outs.link(nc.vector.tensor_copy(recip_hi[:], recip[:]))
            outs.link(nc.vector.tensor_scalar(recip[:], recip[:], const_sb[:, C_PART + 1:C_PART + 2], None, ALU.mult))
            nc.vector.scalar_tensor_tensor(recip_rows[:], recip_hi[:].bitcast(F32), const_sb[:, C_PART:C_PART + 1],
                                           recip[:], ALU.mult, ALU.add).then_inc(recip_ready, 1)

        def make_m(e, k):
            if k == 0:
                dve.wait_ge(ga_loaded, 16 * (e + 1))
            dve.wait_ge(m_product, KC * e + k + 1)
            if k >= 2:
                dve.wait_ge(m_ready, KC * e + k - 1)
            nc.vector.tensor_tensor(full[k % 2][:], spread[k % 2][:], ga_all[:], ALU.mult).then_inc(m_read, 1)

        def scale_q(e, j, k):
            n = e * NC + j * KC + k
            dve.wait_ge(spread_ready, n + 1)
            if k == 0 and j == 0:
                dve.wait_ge(m_ready, KC * (e + 1))
            if k >= 2:
                dve.wait_ge(qn_ready, n - 1)
            nc.vector.tensor_tensor(full[k % 2][:], q_sb[j][:, k, :], spread[k % 2][:],
                                    ALU.mult).then_inc(spread_read, 1)

        def split(e, j, k, by_act):
            if j is None:
                made, count, hi, lo, ready = m_read, KC * e + k + 1, m_hi, m_lo, m_ready
            else:
                made, count, hi, lo, ready = spread_read, e * NC + j * KC + k + 1, qn_hi, qn_lo, qn_ready
            if by_act:
                dve.wait_ge(last_hi_ready, (0 if j is None else (j + 1) * KC) + k + 1)
            else:
                dve.wait_ge(made, count)
                outs.link(nc.vector.tensor_copy(hi[:, k, :], full[k % 2][:]))
            nc.vector.tensor_tensor(lo[:, k, :], full[k % 2][:], hi[:, k, :].bitcast(F32),
                                    ALU.subtract).then_inc(ready, 1)

        def take_o(e, j, t):
            n = e * NT + j * TT + t
            if t == 0:
                dve.wait_ge(x2_biased, e * JB + j + 2)
            dve.wait_ge(o_product, n + 1)
            nc.vector.tensor_tensor(x2[j][:, t, 0:D], prod[t % 2][:], x2[j][:, t, 0:D],
                                    ALU.add).then_inc(o_read, 1)
            dve.wait_ge(o_read, n + 3)
            return outs.mark(nc.vector.bn_stats(stats[:, t, :], x2[j][:, t, 0:D]))

        def take_kv_t(b):
            dve.wait_ge(kv_turned, b + 1)
            nc.vector.tensor_copy(kv_t[:], turn[0][:]).then_inc(kv_t_ready, 1)

        def finish_leaving(e, j, last):
            dve.wait_ge(out_steps, last)
            normalization(outs, x2[j][:, :, D], x2[j][:, :, D + 1]).then_inc(x2_ready, 1)

        gates = Steps(dve, gate_steps, 5)

        def take_rows(i):
            dve.wait_ge(rows_done, 2 * (i + 1))
            wait(dve, cols_done, i - 1)
            if i == 1:
                dve.wait_ge(lo_ready, 2)
            nc.vector.tensor_copy(mod_rows[i % 2][:, 0:D], row_banks[0][:]).then_inc(rows_ready, 1)
            nc.vector.tensor_copy(mod_rows[i % 2][:, D:2 * D], row_banks[1][:]).then_inc(rows_ready, 1)

        def take_cols(i):
            dve.wait_ge(cols_done, i + 1)
            src = prod[1][:, 0:2 * KC * BATCH].rearrange("p (c b) -> p b c", b=BATCH)
            for half in range(2):
                at = (2 * i + half) * KC
                part = src[:, :, half * KC:(half + 1) * KC]
                nc.vector.tensor_scalar(mod_cols[:, :, at:at + KC], part, float(half), None,
                                        ALU.add).then_inc(cols_ready, 1)
                nc.vector.tensor_scalar(mod_now[:, at:at + KC], part[:, 0, :], float(half), None,
                                        ALU.add).then_inc(cols_ready, 1)

        def make_gates():
            gates.start(0)
            g = gate_raw
            dve.wait_ge(gates_summed, 1)
            dve.wait_ge(lo_ready, 3)
            for half, src in enumerate(row_banks):
                gates.link(nc.vector.tensor_copy(g[:, half * D:(half + 1) * D], src[0:BATCH, :]))
            gates.link(nc.vector.scalar_tensor_tensor(gate_rows, g, -1.0, g, ALU.mult, ALU.max))
            gates.link(nc.vector.tensor_scalar(gate_rows, gate_rows, 0.25, None, ALU.max))
            gates.link(nc.vector.tensor_scalar(rows_sign, g, 0.0, 2.0, ALU.is_ge, ALU.mult))
            nc.vector.scalar_tensor_tensor(gate_rows, rows_sign, -1.0, gate_rows, ALU.add,
                                           ALU.mult).then_inc(gates_ready, 1)

        def split_weights(i, name):
            dve.wait_ge(hi_ready, i + 1)
            nc.vector.tensor_tensor(weights[name][1][:], raw[i][:], weights[name][0][:].bitcast(F32),
                                    ALU.subtract).then_inc(lo_ready, 1)

        nc.vector.memset(ones_rows[:].bitcast(F32), 0.0)
        nc.vector.memset(silu_c[:], 0.0)
        nc.vector.memset(bk_rows[:].bitcast(F32), 0.0).then_inc(zeroed, 1)
        for t in range(TT):
            statistics(0, 0, t)
        norm_in(0, 0)
        dve.wait_ge(small_ready, 1)
        nc.vector.tensor_tensor(bk_rows[LO_ROW:LO_ROW + 1, :], bk_raw[:],
                                bk_rows[0:1, :].bitcast(F32), ALU.subtract)
        take_rows(0)
        split_weights(0, "wk")
        take_cols(0)
        for c in range(KC):
            split_h(0, 0, c)
        split_weights(1, "wv")

        def emit(b, e, more):
            if e is not None:
                outs.start(e)
                if b is not None:
                    take_kv_t(e)
            for j in range(JB):
                next_in = b is not None and (j + 1 < JB or more)
                for t in range(TT):
                    if b is not None:
                        take_k(b, j, t)
                    if e is None and j == 0 and t == 1:
                        split_weights(2, "wq")
                        dve.wait_ge(late_loaded, 48)
                    if e is not None and t == 0 and b is not None:
                        reciprocal(e, j)
                    if e is not None and j == 0:
                        make_m(e, t)
                        if b is not None:
                            split(e, None, t, False)
                        elif t > 0:
                            split(e, None, t - 1, True)
                        else:
                            reciprocal(e, 0)
                    if next_in:
                        statistics(*following(b, j), t)
                if next_in:
                    norm_in(*following(b, j))
                if b is None and j == 0:
                    split(e, None, KC - 1, True)
                for k in range(KC):
                    if e is not None:
                        scale_q(e, j, k)
                        if b is not None:
                            split(e, j, k, False)
                        elif k > 0:
                            split(e, j, k - 1, True)
                    if b is not None:
                        take_q(b, j, k)
                if b is None:
                    split(e, j, KC - 1, True)
                if b is not None and j == JB - 1:
                    finish_kv(b)
                if b is None and j > 0:
                    finish_leaving(e, j - 1, last)
                if b is None:
                    then["unpack"](j)
                    if j == 0:
                        then["take_scales"]()
                        reciprocal(e, 1)
                if e is None and j == 0:
                    take_rows(1)
                for t in range(TT):
                    if next_in:
                        split_h(*following(b, j), t)
                    if e is not None:
                        last = take_o(e, j, t)
                    if b is None and j == 0:
                        then["split"](0, t, 0)
                if e is None and j == 0:
                    take_cols(1)
                    take_rows(2)
                    make_gates()
                if next_in:
                    splits.end()
                if b is not None and not more and j == JB - 1:
                    take_kv_t(b)
                if e is not None and (b is not None or j == JB - 1):
                    finish_leaving(e, j, last)
            if e is not None and b is not None:
                outs.end()

        rounds(dve, emit)

    def tensor(pe, then):
        def denominators(e, j):
            for k in range(KC):
                for t in range(TT):
                    last = nc.tensor.matmul(den[t * QUAD:(t + 1) * QUAD, 0:P], k_sum_heads[:, k, :],
                                            q_sb[j][:, k, t * P:(t + 1) * P], start=(k == 0), stop=(k == KC - 1))
            last.then_inc(den_product, 1)

        def key_value(b, j, t):
            n = b * NT + j * TT + t
            pe.wait_ge(k_ready, n + 1)
            pe.wait_ge(v_ready, n + 1)
            for h in range(HEADS):
                g, q = h // HPG, h % HPG
                last = nc.tensor.matmul(kv_heads[q * DK:(q + 1) * DK, g, :], k_sb[t % 2][:, h * DK:(h + 1) * DK],
                                        v_sb[t % 2][:, h, :], start=(j == 0 and t == 0 and g == 0),
                                        stop=(j == JB - 1 and t == TT - 1), skip_group_check=True)
            last.then_inc(kv_tile, 1)

        def turn_x(b, j, c):
            if c == 0:
                pe.wait_ge(xn_ready, b * NT + (j + 1) * TT)
            wait(pe, h_full_ready, b * NC + j * KC + c - 1)
            for t in range(TT):
                last = nc.tensor.transpose(turn[c % 2][:, t * P:(t + 1) * P],
                                           x_in[j][:, t, c * P:(c + 1) * P], ident)
            last.then_inc(turned, 1)

        def times_wo(e, k):
            if k == 0:
                pe.wait_ge(kv_t_ready, e + 1)
            elif k >= 2:
                pe.wait_ge(m_read, KC * e + k - 1)
            nc.tensor.matmul(spread[k % 2][:], kv_t[:, k * P:(k + 1) * P], wo_sb[:, k, :],
                             start=True, stop=True).then_inc(m_product, 1)

        def project_kv(b, e, j, t):
            n = b * NT + j * TT + t
            s = slice(t * P, (t + 1) * P)
            if t > 0:
                pe.wait_ge(k_ready, n)
            elif e is not None:
                pe.wait_ge(o_read, e * NT + j * TT + 1)
            elif j > 0:
                pe.wait_ge(q_ready, b * NC + j * KC - 1)
            first = e is None and j == 0 and t == 0
            if first:
                pe.wait_ge(lo_ready, 1)
            parts = [(ones_rows[:], bk_rows[:])]
            for c in range(KC):
                parts += [(h_hi[:, c, s], wk[0][:, c, :]), (h_hi[:, c, s], wk[1][:, c, :]),
                          (h_lo[:, c, s], wk[0][:, c, :])]
            split_matmul(nc, prod[0][:], parts, True, True).then_inc(k_product, 1)
            if t > 0:
                pe.wait_ge(v_ready, n)
            elif e is not None:
                pe.wait_ge(o_read, e * NT + j * TT + 2)
            elif j > 0:
                pe.wait_ge(q_ready, b * NC + j * KC)
                pe.wait_ge(cols_ready, 8)
            if first:
                pe.wait_ge(cols_ready, 4)
                pe.wait_ge(lo_ready, 2)
            parts = []
            for c in range(KC):
                parts += [(h_hi[:, c, s], wv[0][:, c, :]), (h_hi[:, c, s], wv[1][:, c, :]),
                          (h_lo[:, c, s], wv[0][:, c, :])]
            split_matmul(nc, prod[1][:], parts, True, True).then_inc(v_product, 1)

        def project_q(b, j, k):
            n = b * NC + j * KC + k
            s = slice(k * P, (k + 1) * P)
            if k == 0:
                pe.wait_ge(k_ready, b * NT + (j + 1) * TT)
            elif k == 1:
                pe.wait_ge(v_ready, b * NT + (j + 1) * TT)
            else:
                pe.wait_ge(q_ready, n - 1)
            parts = []
            for c in range(KC):
                parts += [(wq[0][:, c, s], h_hi[:, c, :]), (wq[1][:, c, s], h_hi[:, c, :]),
                          (wq[0][:, c, s], h_lo[:, c, :])]
            split_matmul(nc, prod[k % 2][:], parts, True, True).then_inc(q_product, 1)

        def spread_recip(e, j, k):
            n = e * NC + j * KC + k
            if k == 0:
                pe.wait_ge(recip_ready, e * JB + j + 1)
                pe.wait_ge(m_read, KC * (e + 1))
            elif k >= 2:
                pe.wait_ge(spread_read, n - 1)
            for t in range(TT):
                last = nc.tensor.matmul(spread[k % 2][:, t * P:(t + 1) * P], head_rows[:, t, k * P:(k + 1) * P],
                                        recip_rows[:], start=True, stop=True)
            last.then_inc(spread_ready, 1)

        def times_m(b, e, j, t):
            n = e * NT + j * TT + t
            s = slice(t * P, (t + 1) * P)
            if t == 0:
                pe.wait_ge(qn_ready, e * NC + (j + 1) * KC)
                pe.wait_ge(m_ready, KC * (e + 1))
            if t >= 2 or b is None:
                pe.wait_ge(o_read, n + 1)
            else:
                pe.wait_ge(q_ready, b * NC + (j + 1) * KC - 1 + t)
            parts = []
            for k in range(KC):
                parts += [(qn_hi[:, k, s], m_hi[:, k, :]), (qn_hi[:, k, s], m_lo[:, k, :]),
                          (qn_lo[:, k, s], m_hi[:, k, :])]
            split_matmul(nc, prod[t % 2][:], parts, True, True).then_inc(o_product, 1)

        def mod_rows_product(i):
            if i > 0:
                pe.wait_ge(rows_ready, 2 * i)
            pe.wait_ge(wmod_loaded[min(i, 1)], 16 * KC)
            for into, section in zip(row_banks, PAIRS[i]):
                for k in range(KC):
                    last = nc.tensor.matmul(into[k * QUAD:(k + 1) * QUAD, :], silu_c[:, k, :],
                                            wmod_sb[:, k, section * D:(section + 1) * D], start=True, stop=True)
                last.then_inc(rows_done, 1)

        quadrants_of = const_sb[:, C_ROW:C_END]

        def turn_mod(i):
            pe.wait_ge(rows_ready, 2 * (i + 1))
            for c in range(2 * KC):
                last = nc.tensor.matmul(prod[1][:, c * BATCH:(c + 1) * BATCH], mod_rows[i % 2][:, c * P:(c + 1) * P],
                                        quadrants_of, start=True, stop=True)
            last.then_inc(cols_done, 1)

        def sum_gates():
            pe.wait_ge(rows_ready, 6)
            for half, into in enumerate(row_banks):
                last = nc.tensor.matmul(into[0:BATCH, :], quadrants_of, mod_rows[0][:, half * D:(half + 1) * D],
                                        start=True, stop=True)
            last.then_inc(gates_summed, 1)

        pe.wait_ge(silu_done, 1)
        mod_rows_product(0)
        pe.wait_ge(consts_loaded, 16)
        turn_mod(0)
        for c in range(KC):
            turn_x(0, 0, c)
        pe.wait_ge(small_ready, 3)

        def emit(b, e, more):
            if e is not None:
                pe.wait_ge(kv_ready, KC * (e + 1))
                if b is not None:
                    pe.wait_ge(h_full_ready, b * NC + KC)
                for k in range(KC):
                    last = nc.tensor.transpose(turn[0][:, k * P:(k + 1) * P], kv_sb[:, k, :], ident)
                last.then_inc(kv_turned, 1)
            for j in range(JB):
                next_in = b is not None and (j + 1 < JB or more)
                if e is not None and (b is not None or j == 0):
                    pe.wait_ge(heads_ready, KC * (e + 1))
                    denominators(e, j)
                if b is not None:
                    pe.wait_ge(h_ready, b * NC + (j + 1) * KC)
                for t in range(TT):
                    if b is not None:
                        project_kv(b, e, j, t)
                    if e is not None and j == 0:
                        times_wo(e, t)
                    if b is not None and t > 0:
                        key_value(b, j, t - 1)
                for k in range(KC):
                    if e is not None:
                        spread_recip(e, j, k)
                    if b is not None:
                        if e is None and j == 0 and k == 0:
                            pe.wait_ge(lo_ready, 3)
                        project_q(b, j, k)
                        if k == 0:
                            key_value(b, j, TT - 1)
                if e is None and j == 0:
                    mod_rows_product(1)
                if b is None and j == 0:
                    denominators(e, 1)
                if next_in:
                    turn_x(*following(b, j), 0)
                for t in range(TT):
                    if next_in and t + 1 < TT:
                        turn_x(*following(b, j), t + 1)
                    if e is not None:
                        times_m(b, e, j, t)
                    if b is None and j == 0 and t == 1:
                        then["start"]()
                if e is None and j == 1:
                    pe.wait_ge(head_rows_set, TT)
                if e is None and j == 0:
                    pe.wait_ge(q_ready, KC)
                    turn_mod(1)
                    mod_rows_product(2)
                    sum_gates()

        rounds(pe, emit)

    return dict(sync=sync, gpsimd=gpsimd, scalar=scalar, vector=vector, tensor=tensor,
                h_full_ready=h_full_ready, kv_tile=kv_tile, q_ready=q_ready, spread_read=spread_read,
                o_read=o_read, x2_stored=x2_stored)


def mlp(nc, ctx, att, banks, const_sb, words, gu_scales, down_scales, shifts, x2_dram, mod_cols_dram,
        gate_rows_dram, out_blocks):
    ident = const_sb[:, C_ID:C_ID + P]
    GU = KC * 2 * P
    NB = BATCH * JB
    HALF_BITS = -1912602624
    FP4_SCALE = 16384.0

    def sb(name, shape, dt=F32):
        return ctx.enter_context(nc.sbuf_tensor(name, shape, dt))

    def sem(name):
        return ctx.enter_context(nc.semaphore(name))

    scale16 = sb("scale16", [P, 2 * FC * KC], F16)
    scale = sb("scale", [P, 2, FC, KC])
    down_scale = [sb(f"down_scale{i}", [P, D], F16) for i in range(2)]
    shift_sb = sb("shift_sb", [P, 1], I32)
    raw = [sb(f"raw{i}", [P, GU + D], I32) for i in range(2)]
    down_full = sb("down_full", [P, D])
    x_in = sb("x2_in", [P, TT, XW])
    mod_now = sb("mod_now_b", [P, 4 * KC])
    xn = sb("xn", [P, TT, KC, NIB, WPG])
    h_full = [sb(f"h2_full{i}", [P, TOK]) for i in range(2)]
    h0 = (sb("h2_hi0", [P, KC, TOK], F32R), sb("h2_lo0", [P, KC, TOK], F32R))
    gu_w = sb("gu_w", [P, FC, KC, 2, P], F32R)
    down_w = sb("down_w", [P, FC, 2, D], F32R)
    acc = [[sb(f"acc{i}{u}", [P, TOK]) for u in range(2)] for i in range(2)]
    gate = [sb(f"gate{i}", [P, TOK]) for i in range(2)]
    hid_hi = [sb(f"hid_hi{i}", [P, TOK], F32R) for i in range(2)]
    hid_lo = [sb(f"hid_lo{i}", [P, TOK], F32R) for i in range(2)]
    sum_sq = sb("sum_sq", [P, TT])
    work = [sb(f"rms_work{i}", [P, TT])[:] for i in range(3)]
    rms = sb("rms", [P, TT])
    h1 = (sb("h2_hi1", [P, KC, TOK], F32R), sb("h2_lo1", [P, KC, TOK], F32R))
    o_last = xn[:].rearrange("p t g s a -> p t (g s a)")
    h_hi, h_lo = (h0[0], h1[0]), (h0[1], h1[1])
    gb_all = sb("gb_all", [P, D])
    x_res = sb("x2_res", [P, TT, XW])
    y_sb = sb("y_sb", [P, TT, D])
    o_sb = sb("o_sb", [P, TT, D])

    part = [banks[i] for i in (1, 4, 0, 5)]
    FIRST_TURNS = (0, 1, 2, 0)
    y = [banks[i] for i in (2, 3, 6, 7)]

    words_loaded = [sem(f"words_loaded{i}") for i in range(2)]
    scales_loaded, scale_ready, masked = sem("scales_loaded"), sem("scale_ready"), sem("masked")
    gu_ready, down_full_ready, down_hi_ready, down_ready = (
        sem("gu_ready"), sem("down_full_ready"), sem("down_hi_ready"), sem("down_ready"))
    x_loaded, mod_loaded, res_loaded, gb_loaded, out_stored = (
        sem("x2_in_loaded"), sem("mod_b_loaded"), sem("res_loaded"), sem("gb_loaded"), sem("out_stored"))
    xn_ready, turned, h_full_ready, h_hi_ready, h_ready = (
        sem("xn2_ready"), sem("turned2"), sem("h2_full_ready"), sem("h2_hi_ready"), sem("h2_ready"))
    part_done, acc_first, acc_step, silu_ready, prod_ready, hid_hi_ready, hid_ready, hid_used = (
        sem("part_done"), sem("acc_first"), sem("acc_step"), sem("silu_ready"), sem("prod_ready"),
        sem("hid_hi_ready"), sem("hid_ready"), sem("hid_used"))
    squares_ready, y_read, y_scaled, y_gated, o_ready = (
        sem("squares_ready"), sem("y_read"), sem("y_scaled"), sem("y_gated"), sem("o_ready"))
    shifted, rms_steps = sem("shifted"), sem("rms_steps")
    last_gated, last_ready, last_stored = sem("last_gated"), sem("last_ready"), sem("last_stored")

    def pairs(eng, emit, finish):
        emit(0, 0, False)
        emit(1, 1, False)
        with eng.Fori(1, BATCH - 1) as m:
            emit(m * JB, 0, False)
            emit(m * JB + 1, 1, False)
        emit(NB - 2, 0, False)
        emit(NB - 1, 1, True)
        if finish is not None:
            finish()

    def slot(par, f):
        return (par * FC + f) % 2

    LAG = 2
    NORM_AT = 0
    TURN_AT = 6
    SQUARE_AT, ROOT_AT, SCALE_AT, GATE_AT = LAG, LAG + 2, LAG + 4, LAG + 5

    def sync(sp):
        def load_in(n, batch):
            wait(sp, xn_ready, n * TT)
            sp.dma_start(x_in[:].rearrange("p t d -> p (t d)"),
                         x2_dram[bass.ds(n, 1)].squeeze(0)).then_inc(x_loaded, 16)
            wait(sp, h_full_ready, n * KC)
            sp.dma_start(mod_now[:], mod_cols_dram[bass.ds(batch, 1)].squeeze(0)).then_inc(mod_loaded, 16)

        def load_res(n, batch):
            wait(sp, o_ready, n * TT)
            sp.dma_start(x_res[:].rearrange("p t d -> p (t d)"),
                         x2_dram[bass.ds(n, 1)].squeeze(0)).then_inc(res_loaded, 16)
            sp.dma_start(gb_all[:], gate_rows_dram[bass.ds(batch, 1), 1, :].squeeze(0).partition_broadcast(P)
                         ).then_inc(gb_loaded, 16)

        def load_words(f):
            wait(sp, gu_ready, f - 1)
            wait(sp, down_full_ready, f - 1)
            for s in range(NIB):
                sp.dma_start(raw[f % 2][s * WPG:(s + 1) * WPG, :], words[f]).then_inc(words_loaded[f % 2], 16)
            sp.dma_start(down_scale[f % 2][:], down_scales[f:f + 1, :].squeeze(0).partition_broadcast(P)
                         ).then_inc(words_loaded[f % 2], 16)

        def start():
            sp.wait_ge(att["q_ready"], BATCH * JB * KC)
            sp.wait_ge(att["kv_tile"], BATCH * JB * TT)
            sp.wait_ge(att["x2_stored"][0], 32)
            load_in(0, 0)
            sp.dma_start(shift_sb[:], shifts).then_inc(scales_loaded, 16)
            sp.dma_start(scale16[:], gu_scales).then_inc(scales_loaded, 16)
            for f in range(2):
                load_words(f)

        def pair(m, last):
            for par in range(JB):
                if not last:
                    load_in((m + 1) * JB + par, m + 1)
                load_res(m * JB + par, m)

        def load_second():
            sp.wait_ge(att["x2_stored"][1], 32)
            load_in(1, 0)
            load_words(2)

        def blocks():
            for f in range(3, FC):
                load_words(f)
            for j in range(JB):
                sp.wait_ge(att["x2_stored"][j], 16 * (BATCH + 1))
            pair(0, False)
            with sp.Fori(1, BATCH - 1) as m:
                pair(m, False)
            pair(BATCH - 1, True)
            for t in range(TT):
                sp.wait_ge(last_ready, t + 1)
                sp.dma_start(out_blocks[NB - 1, :, t * D:(t + 1) * D], o_last[:, t, :]).then_inc(last_stored, 16)
            sp.wait_ge(last_stored, 16 * TT)
            sp.wait_ge(out_stored, 16 * (NB - 1))

        return dict(start=start, load_second=load_second, blocks=blocks)

    def gpsimd(pool):
        def expand(f):
            pool.wait_ge(masked, f + 1)
            wait(pool, down_ready, f)
            half = raw[f % 2][:].bitcast(F16).rearrange("p (n two) -> p n two", two=2)[:, :, 1]
            nc.gpsimd.tensor_tensor(down_full[:], half[:, GU:GU + D], down_scale[f % 2][:],
                                    ALU.mult).then_inc(down_full_ready, 1)
            pool.wait_ge(down_hi_ready, f + 1)
            nc.gpsimd.tensor_tensor(down_w[:, f, 1, :], down_full[:], down_w[:, f, 0, :].bitcast(F32),
                                    ALU.subtract).then_inc(down_ready, 1)

        def finish_out(n, t):
            if t == 0:
                pool.wait_ge(gb_loaded, 16 * (n + 1))
                pool.wait_ge(res_loaded, 16 * (n + 1))
            pool.wait_ge(y_scaled, n * TT + t + 1)
            nc.gpsimd.tensor_tensor(o_sb[:, t, :], o_sb[:, t, :], gb_all[:], ALU.mult).then_inc(y_gated, 1)
            pool.wait_ge(y_gated, n * TT + t + 1)
            nc.gpsimd.tensor_tensor(o_sb[:, t, :], o_sb[:, t, :], x_res[:, t, 0:D],
                                    ALU.add).then_inc(o_ready, 1)

        def store(n):
            pool.wait_ge(o_ready, (n + 1) * TT)
            pool.dma_start(out_blocks[bass.ds(n, 1)].squeeze(0),
                           o_sb[:].rearrange("p t d -> p (t d)")).then_inc(out_stored, 16)

        def emit(n, par, last):
            first = isinstance(n, int) and n == 0
            if first:
                expand(0)
                expand(1)
            for f in range(FC):
                if first and f + 2 < FC:
                    expand(f + 2)
                q = n * FC + f
                s = slot(par, f)
                pool.wait_ge(hid_hi_ready, q + 1)
                nc.gpsimd.tensor_tensor(hid_lo[s][:], gate[s][:], hid_hi[s][:].bitcast(F32),
                                        ALU.subtract).then_inc(hid_ready, 1)
                if GATE_AT <= f < GATE_AT + TT and not first:
                    finish_out(n - 1, f - GATE_AT)
                    if f == GATE_AT + TT - 1:
                        store(n - 1)

        return dict(blocks=lambda: pairs(pool, emit, None))

    def scalar(act):
        def expand(f):
            act.wait_ge(masked, f + 1)
            half = raw[f % 2][:].bitcast(F16).rearrange("p (n two) -> p n two", two=2)[:, :, 1]
            nc.scalar.activation(gu_w[:, f, :, :, :].rearrange("p g u n -> p (g u n)"), half[:, 0:GU],
                                 ACT.Copy, scale=FP4_SCALE).then_inc(gu_ready, 1)
            act.wait_ge(down_full_ready, f + 1)
            nc.scalar.activation(down_w[:, f, 0, :], down_full[:], ACT.Copy).then_inc(down_hi_ready, 1)

        def normalize(n, t):
            if t == 0:
                act.wait_ge(x_loaded, 16 * (n + 1))
                wait(act, turned, n * KC)
            nc.scalar.activation(xn[:, t].rearrange("p g s a -> p g a s"),
                                 x_in[:, t, 0:D].rearrange("p (g a s) -> p g a s", g=KC, s=NIB), ACT.Identity,
                                 bias=x_in[:, t, D + 1:D + 2], scale=x_in[:, t, D:D + 1]).then_inc(xn_ready, 1)

        def modulate(n, c, i):
            act.wait_ge(turned, n * KC + c + 1)
            act.wait_ge(mod_loaded, 16 * (n + 1))
            wait(act, h_ready, n * KC + c - 1)
            nc.scalar.activation(h_full[c % 2][:], part[i][:], ACT.Identity,
                                 bias=mod_now[:, 2 * KC + c:2 * KC + c + 1],
                                 scale=mod_now[:, 3 * KC + c:3 * KC + c + 1]).then_inc(h_full_ready, 1)

        def take_y(n, t):
            act.wait_ge(hid_used, (n * FC + FC - 1) * TT + t + 1)
            nc.scalar.activation(y_sb[:, t, :], y[t][:], ACT.Copy, scale=FP4_SCALE).then_inc(y_read, 1)

        def squares(n, t):
            act.wait_ge(y_read, n * TT + t + 1)
            wait(act, squares_ready, n * TT + t)
            act.wait_ge(down_ready, FC)
            nc.scalar.activation(down_full[:], y_sb[:, t, :], ACT.Square,
                                 accum_out=sum_sq[:, t:t + 1]).then_inc(squares_ready, 1)

        def scale_y(n, t):
            act.wait_ge(rms_steps, 12 * (n + 1))
            wait(act, out_stored, 16 * n)
            nc.scalar.activation(o_sb[:, t, :], y_sb[:, t, :], ACT.Copy,
                                 scale=rms[:, t:t + 1]).then_inc(y_scaled, 1)

        def hidden(q, s):
            act.wait_ge(acc_step, 6 * q + 5)
            wait(act, hid_ready, q - 1)
            nc.scalar.activation(gate[s][:], acc[s][0][:], ACT.Silu).then_inc(silu_ready, 1)

        def hidden_hi(q, s):
            act.wait_ge(prod_ready, q + 1)
            wait(act, hid_used, (q - 1) * TT)
            nc.scalar.activation(hid_hi[s][:], gate[s][:], ACT.Copy).then_inc(hid_hi_ready, 1)

        def start():
            act.wait_ge(att["kv_tile"], BATCH * JB * TT)
            for t in range(TT):
                normalize(0, t)
            expand(0)
            for c in range(KC):
                modulate(0, c, FIRST_TURNS[c])

        def emit(n, par, last):
            first = isinstance(n, int) and n == 0
            for f in range(FC):
                q = n * FC + f
                s = slot(par, f)
                if f == LAG and not first:
                    take_y(n - 1, TT - 1)
                if f > 0 or not first:
                    hidden(q - 1, 1 - s)
                for u in range(2):
                    act.wait_ge(part_done, 8 * q + u + 1)
                    wait(act, prod_ready, q - 1)
                    if first and f == 0:
                        act.wait_ge(scale_ready, 1)
                        act.wait_ge(att["o_read"], BATCH * JB * TT + 2)
                    nc.scalar.activation(acc[s][u][:], part[u][:], ACT.Identity,
                                         scale=scale[:, u, f, 0:1]).then_inc(acc_first, 1)
                if first and f + 1 < FC:
                    expand(f + 1)
                if not last and TURN_AT <= f < TURN_AT + KC:
                    modulate(n + 1, f - TURN_AT, 0)
                if f > 0 or not first:
                    hidden_hi(q - 1, 1 - s)
                if not first:
                    if f == LAG - 1:
                        for t in range(TT - 1):
                            take_y(n - 1, t)
                    if SQUARE_AT <= f < SQUARE_AT + 2:
                        for t in (2 * (f - SQUARE_AT), 2 * (f - SQUARE_AT) + 1):
                            squares(n - 1, t)
                    if SCALE_AT <= f < SCALE_AT + 2:
                        for t in (2 * (f - SCALE_AT), 2 * (f - SCALE_AT) + 1):
                            scale_y(n - 1, t)
                if not last:
                    if NORM_AT <= f < NORM_AT + TT:
                        normalize(n + 1, f - NORM_AT)

        def finish():
            q = NB * FC
            hidden(q - 1, slot(1, FC - 1))
            hidden_hi(q - 1, slot(1, FC - 1))
            for t in range(TT):
                act.wait_ge(hid_used, (q - 1) * TT + t + 1)
                wait(act, squares_ready, (NB - 1) * TT + t)
                nc.scalar.activation(down_full[:], y[t][:], ACT.Square, scale=FP4_SCALE,
                                     accum_out=sum_sq[:, t:t + 1]).then_inc(squares_ready, 1)
            for t in range(TT):
                take_y(NB - 1, t)

        return dict(start=start, blocks=lambda: pairs(act, emit, finish))

    def vector(dve):
        outs = Steps(dve, rms_steps, 12)

        def unpack(f):
            dve.wait_ge(words_loaded[f % 2], 16 * (NIB + 1) * (f // 2 + 1))
            r = raw[f % 2][:]
            nc.vector.tensor_scalar(r, r, shift_sb[:, 0:1], 3, ALU.logical_shift_left,
                                    ALU.arith_shift_right).then_inc(shifted, 1)
            dve.wait_ge(shifted, f + 1)
            nc.vector.tensor_scalar(r, r, HALF_BITS, None, ALU.bitwise_and).then_inc(masked, 1)

        def split(n, c, par):
            dve.wait_ge(h_full_ready, n * KC + c + 1)
            nc.vector.tensor_copy(h_hi[par][:, c, :], h_full[c % 2][:]).then_inc(h_hi_ready, 1)
            dve.wait_ge(h_hi_ready, n * KC + c + 1)
            nc.vector.tensor_tensor(h_lo[par][:, c, :], h_full[c % 2][:], h_hi[par][:, c, :].bitcast(F32),
                                    ALU.subtract).then_inc(h_ready, 1)

        def root(n, part):
            if part == 0:
                outs.start(n)
                dve.wait_ge(squares_ready, (n + 1) * TT)
                wait(dve, y_scaled, n * TT)
                inverse_sqrt_guess(nc, outs, rms[:], work, sum_sq[:], 1.0 / D, RMS_EPS)
            else:
                inverse_sqrt_newton(nc, outs, rms[:], work)
            if part == 3:
                outs.end()

        def take_scales():
            dve.wait_ge(scales_loaded, 32)
            nc.vector.tensor_copy(scale[:].rearrange("p u f g -> p (u f g)"), scale16[:]).then_inc(scale_ready, 1)

        def product(q, s):
            dve.wait_ge(silu_ready, q + 1)
            dve.wait_ge(acc_step, 6 * q + 6)
            nc.vector.tensor_tensor(gate[s][:], gate[s][:], acc[s][1][:], ALU.mult).then_inc(prod_ready, 1)

        def emit(n, par, last):
            first = isinstance(n, int) and n == 0
            for f in range(FC):
                q = n * FC + f
                s = slot(par, f)
                if f == 0 and first:
                    dve.wait_ge(scale_ready, 1)
                for g in range(1, KC):
                    for u in range(2):
                        dve.wait_ge(part_done, 8 * q + 2 * g + u + 1)
                        if g == 1:
                            dve.wait_ge(acc_first, 2 * q + u + 1)
                        else:
                            dve.wait_ge(acc_step, 6 * q + 2 * (g - 2) + u + 1)
                        nc.vector.scalar_tensor_tensor(acc[s][u][:], part[(2 * g + u) % 4][:],
                                                       scale[:, u, f, g:g + 1], acc[s][u][:],
                                                       ALU.mult, ALU.add).then_inc(acc_step, 1)
                    if g == 1 and not (first and f == 0):
                        product(q - 1, 1 - s)
                    if not first and ROOT_AT <= f < ROOT_AT + 2 and g >= 2:
                        root(n - 1, 2 * (f - ROOT_AT) + g - 2)
                if first and f + 2 < FC:
                    unpack(f + 2)
                if not last and TURN_AT <= f < TURN_AT + KC:
                    split(n + 1, f - TURN_AT, 1 - par)

        def finish():
            product(NB * FC - 1, slot(1, FC - 1))
            for part in range(4):
                root(NB - 1, part)
            dve.wait_ge(gb_loaded, 16 * NB)
            dve.wait_ge(res_loaded, 16 * NB)
            dve.wait_ge(rms_steps, 12 * NB)
            for t in range(TT):
                dve.wait_ge(y_read, (NB - 1) * TT + t + 1)
                nc.vector.scalar_tensor_tensor(o_last[:, t, :], y_sb[:, t, :], rms[:, t:t + 1], gb_all[:],
                                               ALU.mult, ALU.mult).then_inc(last_gated, 1)
                dve.wait_ge(last_gated, t + 1)
                nc.vector.tensor_tensor(o_last[:, t, :], o_last[:, t, :], x_res[:, t, 0:D],
                                        ALU.add).then_inc(last_ready, 1)

        return dict(unpack=unpack, take_scales=take_scales, split=split,
                               blocks=lambda: pairs(dve, emit, finish))

    def tensor(pe):
        owner = {3: (att["spread_read"], BATCH * JB * KC)}

        def claim(i):
            if i in owner:
                wait(pe, *owner[i])

        def transposes(n, c, i):
            claim(i)
            if c == 0:
                pe.wait_ge(xn_ready, (n + 1) * TT)
            for t in range(TT):
                last = nc.tensor.transpose(part[i][:, t * P:(t + 1) * P],
                                           xn[:, t, c].rearrange("p s a -> p (s a)"), ident)
            last.then_inc(turned, 1)
            owner[i] = (h_full_ready, n * KC + c + 1)

        def gate_up(q, f, par, g):
            for u in range(2):
                i = (2 * g + u) % 4
                claim(i)
                w = gu_w[:, f, g, u, :]
                split_matmul(nc, part[i][:], [(w, h_hi[par][:, g, :]), (w, h_lo[par][:, g, :])],
                             True, True).then_inc(part_done, 1)
                owner[i] = (acc_first, 2 * q + u + 1) if g == 0 else (acc_step, 6 * q + 2 * (g - 1) + u + 1)

        def down(q, f, s, t):
            if t == 0:
                pe.wait_ge(hid_ready, q + 1)
            ts = slice(t * P, (t + 1) * P)
            split_matmul(nc, y[t][:], [(hid_hi[s][:, ts], down_w[:, f, 0, :]),
                                       (hid_hi[s][:, ts], down_w[:, f, 1, :]),
                                       (hid_lo[s][:, ts], down_w[:, f, 0, :])],
                         f == 0, f == FC - 1).then_inc(hid_used, 1)

        def start():
            pe.wait_ge(att["h_full_ready"], BATCH * JB * KC)
            for c in range(KC):
                transposes(0, c, FIRST_TURNS[c])

        def emit(n, par, last):
            first = isinstance(n, int) and n == 0
            if not first:
                for i in range(4):
                    owner[i] = (acc_step, 6 * n * FC)
            pe.wait_ge(h_ready, (n + 1) * KC)
            for f in range(FC):
                q = n * FC + f
                if first:
                    pe.wait_ge(gu_ready, f + 1)
                for i in range(KC):
                    gate_up(q, f, par, i)
                    if f >= LAG:
                        if f == LAG:
                            if first:
                                pe.wait_ge(att["o_read"], BATCH * JB * TT + 2)
                            wait(pe, y_read, (n - 1) * TT + i + 1)
                        if first:
                            pe.wait_ge(down_ready, f - LAG + 1)
                        down(q - LAG, f - LAG, slot(par, f - LAG), i)
                    elif not first:
                        down(q - LAG, f - LAG + FC, slot(1 - par, f - LAG + FC), i)
                    if i == 0 and not last and TURN_AT <= f < TURN_AT + KC:
                        transposes(n + 1, f - TURN_AT, 0)

        def finish():
            for f in range(FC - LAG, FC):
                for t in range(TT):
                    down((NB - 1) * FC + f, f, slot(1, f), t)

        return dict(start=start, blocks=lambda: pairs(pe, emit, finish))

    return dict(sync=sync, gpsimd=gpsimd, scalar=scalar, vector=vector, tensor=tensor)


def kernel(**inputs):
    import numpy as np
    import concourse.bacc as bacc
    from concourse.bass_utils import run_bass_kernel_spmd

    a = {name: np.asarray(value) for name, value in inputs.items()}
    order = np.arange(P).reshape(WPG, NIB).T.reshape(-1)

    consts = np.zeros((P, C_END), np.float32)
    consts[:, C_ID:C_ID + P] = np.eye(P)
    head = np.arange(P) // DK
    consts[:, C_MASK:C_MASK + P] = head[:, None] == head[None, :]
    for k in range(KC):
        one = (k * (P // DK) + head)[:, None] == (np.arange(QUAD) % HEADS)[None, :]
        consts[:, C_HEAD + k * QUAD:C_HEAD + (k + 1) * QUAD] = one
        consts[:, C_SEL + k * P:C_SEL + (k + 1) * P] = np.tile(one.T, (P // QUAD, 1))
    low = np.arange(P) % QUAD >= HEADS
    consts[:, C_PART], consts[:, C_PART + 1] = np.where(low, -1, 1), low
    consts[:, C_QUAD:C_QUAD + TT] = (np.arange(P) // QUAD)[:, None] == np.arange(TT)[None, :]
    consts[:, C_ROW:C_END] = (np.arange(P) % QUAD)[:, None] == np.arange(BATCH)[None, :]
    shifts = (28 - 4 * (np.arange(P) // WPG)).astype(np.int32).reshape(P, 1)

    wmod = a["L0_wmod"].reshape(D, 6, KC, P).copy()
    for section in (3, 4):
        wmod[:, section] = wmod[:, section][:, :, order]
    gu = a["L0_ffn_gate_up_packed"].reshape(2, FC, P, KC, WPG)[:, :, order]
    gu = gu.transpose(1, 4, 3, 0, 2).reshape(FC, WPG, KC * 2 * P)
    down = a["L0_ffn_down_packed"].reshape(D, FC, WPG).transpose(1, 2, 0)
    gu_scales = a["L0_ffn_gate_up_scales"].reshape(KC, 2, FC, P)[:, :, :, order].transpose(3, 1, 2, 0)

    arrays = {
        "x": a["L0_attn_x"].reshape(BATCH * SEQ, D),
        "wq_t": a["L0_attn_wq"].T, "wk_t": a["L0_attn_wk"].T, "wv_t": a["L0_attn_wv"].T, "wo_t": a["L0_attn_wo"].T,
        "bq": a["L0_attn_bq"].reshape(KC, P).T, "bk": a["L0_attn_bk"].reshape(1, D),
        "bv": a["L0_attn_bv"], "bo": a["L0_attn_bo"],
        "gu_down_words": np.concatenate([gu, down], axis=2),
        "gu_scales": gu_scales.reshape(P, 2 * FC * KC),
        "down_scales": a["L0_ffn_down_scales"],
        "c_t": a["L0_c"].T.reshape(KC, P, BATCH).transpose(1, 0, 2),
        "wmod": wmod.reshape(D, 6 * D),
        "consts": consts, "shifts": shifts,
    }
    nc = bacc.Bacc("TRN2", target_bir_lowering=False, num_devices=1)
    feed, aps = {}, {}
    for name, value in arrays.items():
        feed[f"in_{name}"] = np.ascontiguousarray(value)
        aps[name] = nc.dram_tensor(f"in_{name}", value.shape, mybir.dt.from_np(value.dtype), kind="ExternalInput").ap()
    out = nc.dram_tensor("out", (BATCH * SEQ, D), F32, kind="ExternalOutput").ap()
    adaln_block(nc, **aps, out=out)
    result = run_bass_kernel_spmd(nc, [feed], core_ids=[0])
    return result.results[0]["out"].reshape(BATCH, SEQ, D)
```
